# Optimizing a Trainium2 kernel written in Bass

```python
import numpy as np
import jax
import jax.numpy as jnp

def _softmax(x, axis=-1):
    return jax.nn.softmax(x, axis=axis)

def _gelu(x):
    return jax.nn.gelu(x, approximate=True)

def _silu(x):
    return jax.nn.silu(x)

def _sigmoid(x):
    return jax.nn.sigmoid(x)

def _layernorm(x, axis=-1, eps=1e-05):
    m = jnp.mean(x, axis=axis, keepdims=True)
    v = jnp.var(x, axis=axis, keepdims=True)
    return (x - m) / jnp.sqrt(v + eps)

def _scatter_add(tgt, idx, src, axis=0):
    return tgt.at[idx].add(src)

def _segment_sum(src, seg, n):
    return jax.ops.segment_sum(src, seg, n)
kernel_name = 'mk_hybrid_d1_jaxref_r4_be0712'

def setup_inputs(seed: int=0):
    np.random.seed(seed)
    _w = jnp.asarray

    def _L0_attn_a_setup():
        import jax, jax.numpy as jnp
        import numpy as np
        CHUNK = 32
        FLOOR = 0.01
        EPS_MIX = 1e-05
        EPS_NORM = 1e-05

        def l2norm(x):
            return x / jnp.sqrt(jnp.sum(x * x, -1, keepdims=True) + 1e-12)

        def dw_causal_conv(x, w):
            K = w.shape[-1]
            L = x.shape[1]
            xp = jnp.pad(x, ((0, 0), (K - 1, 0), (0, 0)))
            y = jnp.zeros_like(x)
            for t in range(K):
                y = y + xp[:, t:t + L, :] * w[:, t]
            return y

        def delta_rule_chunkwise(q, k, v, beta):
            b, h, L, dk = q.shape
            dv = v.shape[-1]
            c = CHUNK
            n = L // c
            q = l2norm(q)
            k = l2norm(k)
            v = v * beta[..., None]
            kb = k * beta[..., None]
            rs = lambda x: x.reshape(b, h, n, c, -1)
            qc, kc, vc, kbc = (rs(q), rs(k), rs(v), rs(kb))
            T = -jnp.einsum('bhnid,bhnjd->bhnij', kbc, kc)
            tri_strict = jnp.tril(jnp.ones((c, c), bool), -1)
            T = jnp.where(tri_strict, T, 0.0)
            for i in range(1, c):
                T = T.at[..., i, :i].add(jnp.einsum('bhnj,bhnji->bhni', T[..., i, :], T[..., :, :i]))
            T = T + jnp.eye(c, dtype=T.dtype)
            u = jnp.einsum('bhnij,bhnjd->bhnid', T, vc)
            w = jnp.einsum('bhnij,bhnjd->bhnid', T, kbc)
            mask_incl = jnp.tril(jnp.ones((c, c), bool), 0)

            def step(S, inp):
                qi, ki, ui, wi = inp
                attn = jnp.einsum('bhid,bhjd->bhij', qi, ki)
                attn = jnp.where(mask_incl, attn, 0.0)
                u_i = ui - jnp.einsum('bhik,bhkd->bhid', wi, S)
                o_i = jnp.einsum('bhik,bhkd->bhid', qi, S) + jnp.einsum('bhij,bhjd->bhid', attn, u_i)
                S = S + jnp.einsum('bhci,bhcd->bhid', ki, u_i)
                return (S, o_i)
            S0 = jnp.zeros((b, h, dk, dv), q.dtype)
            xs = tuple((jnp.moveaxis(a, 2, 0) for a in (qc, kc, u, w)))
            S, o = jax.lax.scan(step, S0, xs)
            o = jnp.moveaxis(o, 0, 2).reshape(b, h, L, dv)
            return (o, S)
        key = jax.random.key(seed)
        B, L, D, H = (4, 1024, 256, 4)
        dh = D // H
        ks = jax.random.split(key, 20)
        s = 1.0 / np.sqrt(D)
        inp = {'hidden_states': jax.random.normal(ks[0], (B, L, D), jnp.float32), 'Wq': jax.random.normal(ks[1], (D, D), jnp.float32) * s, 'Wk': jax.random.normal(ks[2], (D, D), jnp.float32) * s, 'Wv': jax.random.normal(ks[3], (D, D), jnp.float32) * s, 'Wb': jax.random.normal(ks[4], (D, H), jnp.float32) * s, 'conv_q_w': jax.random.normal(ks[5], (D, 4), jnp.float32) * 0.5, 'conv_k_w': jax.random.normal(ks[6], (D, 4), jnp.float32) * 0.5, 'conv_v_w': jax.random.normal(ks[7], (D, 4), jnp.float32) * 0.5, 'local_w': (jax.random.normal(ks[8], (H * dh, 7), jnp.float32) / np.sqrt(7.0)).at[:, -1].add(1.0), 'mid_w': (jax.random.normal(ks[9], (H * dh, 25), jnp.float32) / np.sqrt(25.0)).at[:, -1].add(1.0), 'r_w1': jax.random.normal(ks[10], (D + 14 * H, 2 * (D + 14 * H)), jnp.float32) / np.sqrt(D + 14 * H), 'r_b1': jnp.zeros((2 * (D + 14 * H),), jnp.float32), 'r_w2': jax.random.normal(ks[11], (2 * (D + 14 * H), H * 4), jnp.float32) / np.sqrt(2.0 * (D + 14 * H)), 'r_b2': jnp.zeros((H, 4), jnp.float32).at[:, 2:].set(0.7).reshape(-1), 'mix_w': jnp.ones((H, dh), jnp.float32), 'onorm_w': jnp.ones((dh,), jnp.float32), 'Wo': jax.random.normal(ks[12], (D, D), jnp.float32) * s}
        return inp
    _L0_attn_a_in = _L0_attn_a_setup()

    def _L0_attn_b_setup():
        import jax, jax.numpy as jnp
        import numpy as np
        import math
        D_MODEL = 256
        NUM_HEADS = 16
        HEAD_DIM = D_MODEL // NUM_HEADS
        key = jax.random.key(seed)
        k_x, k_qkv, k_o = jax.random.split(key, 3)
        B, S = (2, 512)
        x = jax.random.normal(k_x, (B, S, D_MODEL), dtype=jnp.float32)
        sigma_qkv = math.sqrt(2.0 / (D_MODEL + 3 * D_MODEL))
        w_qkv = jax.random.truncated_normal(k_qkv, -3.0, 3.0, (3 * D_MODEL, D_MODEL), dtype=jnp.float32) * sigma_qkv
        sigma_o = math.sqrt(2.0 / (D_MODEL + D_MODEL))
        w_out = jax.random.truncated_normal(k_o, -3.0, 3.0, (D_MODEL, D_MODEL), dtype=jnp.float32) * sigma_o
        return {'x': x, 'w_qkv': w_qkv, 'w_out': w_out}
    _L0_attn_b_in = _L0_attn_b_setup()

    def _L0_ffn_setup():
        import jax, jax.numpy as jnp
        import numpy as np
        D_MODEL = 256
        NUM_SLOTS = 64
        TOP_K = 8
        B, T = (4, 1024)

        def _forward(x, slot_init, slot_scale, w1, b1, w2, b2, gru_wih, gru_whh, gru_bih, gru_bhh, wv, bv, wo, bo, tau):
            Bn, Tn, D = x.shape
            Sn = slot_init.shape[0]
            S = jnp.broadcast_to((slot_init * slot_scale)[None], (Bn, Sn, D)).astype(x.dtype)
            slot_mean = S.mean(axis=1, keepdims=True)
            ctx = jnp.concatenate([x, jnp.broadcast_to(slot_mean, x.shape)], axis=-1)
            h = jax.nn.gelu(ctx @ w1.T + b1, approximate=False)
            route_logits = (h @ w2.T + b2) / (jnp.abs(tau) + 0.1)
            topk_vals, topk_idx = jax.lax.top_k(route_logits, TOP_K)
            topk_w = jax.nn.softmax(topk_vals, axis=-1)
            alpha = jnp.sum(topk_w[..., None] * jax.nn.one_hot(topk_idx, Sn, dtype=x.dtype), axis=-2)
            slot_input = jnp.einsum('bts,btd->bsd', alpha, x)
            slot_wsum = alpha.sum(axis=1) + 1e-08
            gi = (slot_input / slot_wsum[..., None]).reshape(Bn * Sn, D)
            hs = S.reshape(Bn * Sn, D)
            gx = gi @ gru_wih.T + gru_bih
            gh = hs @ gru_whh.T + gru_bhh
            xr, xz, xn = jnp.split(gx, 3, axis=-1)
            hr, hz, hn = jnp.split(gh, 3, axis=-1)
            r = jax.nn.sigmoid(xr + hr)
            z = jax.nn.sigmoid(xz + hz)
            n = jnp.tanh(xn + r * hn)
            h_new = (1.0 - z) * n + z * hs
            S_new = h_new.reshape(Bn, Sn, D)
            slot_values = S_new @ wv.T + bv
            out = jnp.einsum('bts,bsd->btd', alpha, slot_values)
            return out @ wo.T + bo
        key = jax.random.key(seed)
        ks = jax.random.split(key, 16)
        D, S = (D_MODEL, NUM_SLOTS)
        H = D // 2
        sc = lambda fan_in: 1.0 / np.sqrt(fan_in)
        inp = {'x': jax.random.normal(ks[0], (B, T, D), dtype=jnp.float32), 'slot_init': jax.random.normal(ks[1], (S, D), dtype=jnp.float32) * 0.1, 'slot_scale': jnp.ones((S, 1), dtype=jnp.float32), 'w1': jax.random.normal(ks[2], (H, 2 * D), dtype=jnp.float32) * sc(2 * D), 'b1': jnp.zeros((H,), dtype=jnp.float32), 'w2': jax.random.normal(ks[3], (S, H), dtype=jnp.float32) * sc(H), 'b2': jnp.zeros((S,), dtype=jnp.float32), 'gru_wih': jax.random.normal(ks[4], (3 * D, D), dtype=jnp.float32) * sc(D), 'gru_whh': jax.random.normal(ks[5], (3 * D, D), dtype=jnp.float32) * sc(D), 'gru_bih': jnp.zeros((3 * D,), dtype=jnp.float32), 'gru_bhh': jnp.zeros((3 * D,), dtype=jnp.float32), 'wv': jax.random.normal(ks[6], (D, D), dtype=jnp.float32) * sc(D), 'bv': jnp.zeros((D,), dtype=jnp.float32), 'wo': jax.random.normal(ks[7], (D, D), dtype=jnp.float32) * sc(D), 'bo': jnp.zeros((D,), dtype=jnp.float32), 'tau': jnp.ones((1,), dtype=jnp.float32)}
        return inp
    _L0_ffn_in = _L0_ffn_setup()
    _d = {'L0_attn_a_hidden_states': _L0_attn_a_in['hidden_states'], 'L0_attn_a_Wq': _L0_attn_a_in['Wq'], 'L0_attn_a_Wk': _L0_attn_a_in['Wk'], 'L0_attn_a_Wv': _L0_attn_a_in['Wv'], 'L0_attn_a_Wb': _L0_attn_a_in['Wb'], 'L0_attn_a_conv_q_w': _L0_attn_a_in['conv_q_w'], 'L0_attn_a_conv_k_w': _L0_attn_a_in['conv_k_w'], 'L0_attn_a_conv_v_w': _L0_attn_a_in['conv_v_w'], 'L0_attn_a_local_w': _L0_attn_a_in['local_w'], 'L0_attn_a_mid_w': _L0_attn_a_in['mid_w'], 'L0_attn_a_r_w1': _L0_attn_a_in['r_w1'], 'L0_attn_a_r_b1': _L0_attn_a_in['r_b1'], 'L0_attn_a_r_w2': _L0_attn_a_in['r_w2'], 'L0_attn_a_r_b2': _L0_attn_a_in['r_b2'], 'L0_attn_a_mix_w': _L0_attn_a_in['mix_w'], 'L0_attn_a_onorm_w': _L0_attn_a_in['onorm_w'], 'L0_attn_a_Wo': _L0_attn_a_in['Wo'], 'L0_attn_b_w_qkv': _L0_attn_b_in['w_qkv'], 'L0_attn_b_w_out': _L0_attn_b_in['w_out'], 'L0_ffn_slot_init': _L0_ffn_in['slot_init'], 'L0_ffn_slot_scale': _L0_ffn_in['slot_scale'], 'L0_ffn_w1': _L0_ffn_in['w1'], 'L0_ffn_b1': _L0_ffn_in['b1'], 'L0_ffn_w2': _L0_ffn_in['w2'], 'L0_ffn_b2': _L0_ffn_in['b2'], 'L0_ffn_gru_wih': _L0_ffn_in['gru_wih'], 'L0_ffn_gru_whh': _L0_ffn_in['gru_whh'], 'L0_ffn_gru_bih': _L0_ffn_in['gru_bih'], 'L0_ffn_gru_bhh': _L0_ffn_in['gru_bhh'], 'L0_ffn_wv': _L0_ffn_in['wv'], 'L0_ffn_bv': _L0_ffn_in['bv'], 'L0_ffn_wo': _L0_ffn_in['wo'], 'L0_ffn_bo': _L0_ffn_in['bo'], 'L0_ffn_tau': _L0_ffn_in['tau']}
    _x0 = _d['L0_attn_a_hidden_states']
    _d['L0_attn_a_hidden_states'] = jax.random.normal(jax.random.fold_in(jax.random.key(seed), 1), (16, 1024, 256), dtype=_x0.dtype)
    del _x0
    return _d

def reference(L0_attn_a_hidden_states, L0_attn_a_Wq, L0_attn_a_Wk, L0_attn_a_Wv, L0_attn_a_Wb, L0_attn_a_conv_q_w, L0_attn_a_conv_k_w, L0_attn_a_conv_v_w, L0_attn_a_local_w, L0_attn_a_mid_w, L0_attn_a_r_w1, L0_attn_a_r_b1, L0_attn_a_r_w2, L0_attn_a_r_b2, L0_attn_a_mix_w, L0_attn_a_onorm_w, L0_attn_a_Wo, L0_attn_b_w_qkv, L0_attn_b_w_out, L0_ffn_slot_init, L0_ffn_slot_scale, L0_ffn_w1, L0_ffn_b1, L0_ffn_w2, L0_ffn_b2, L0_ffn_gru_wih, L0_ffn_gru_whh, L0_ffn_gru_bih, L0_ffn_gru_bhh, L0_ffn_wv, L0_ffn_bv, L0_ffn_wo, L0_ffn_bo, L0_ffn_tau):

    def _L0_attn_a_ref(hidden_states, Wq, Wk, Wv, Wb, conv_q_w, conv_k_w, conv_v_w, local_w, mid_w, r_w1, r_b1, r_w2, r_b2, mix_w, onorm_w, Wo):
        import jax, jax.numpy as jnp
        import numpy as np
        CHUNK = 32
        FLOOR = 0.01
        EPS_MIX = 1e-05
        EPS_NORM = 1e-05

        def l2norm(x):
            return x / jnp.sqrt(jnp.sum(x * x, -1, keepdims=True) + 1e-12)

        def dw_causal_conv(x, w):
            K = w.shape[-1]
            L = x.shape[1]
            xp = jnp.pad(x, ((0, 0), (K - 1, 0), (0, 0)))
            y = jnp.zeros_like(x)
            for t in range(K):
                y = y + xp[:, t:t + L, :] * w[:, t]
            return y

        def delta_rule_chunkwise(q, k, v, beta):
            b, h, L, dk = q.shape
            dv = v.shape[-1]
            c = CHUNK
            n = L // c
            q = l2norm(q)
            k = l2norm(k)
            v = v * beta[..., None]
            kb = k * beta[..., None]
            rs = lambda x: x.reshape(b, h, n, c, -1)
            qc, kc, vc, kbc = (rs(q), rs(k), rs(v), rs(kb))
            T = -jnp.einsum('bhnid,bhnjd->bhnij', kbc, kc)
            tri_strict = jnp.tril(jnp.ones((c, c), bool), -1)
            T = jnp.where(tri_strict, T, 0.0)
            for i in range(1, c):
                T = T.at[..., i, :i].add(jnp.einsum('bhnj,bhnji->bhni', T[..., i, :], T[..., :, :i]))
            T = T + jnp.eye(c, dtype=T.dtype)
            u = jnp.einsum('bhnij,bhnjd->bhnid', T, vc)
            w = jnp.einsum('bhnij,bhnjd->bhnid', T, kbc)
            mask_incl = jnp.tril(jnp.ones((c, c), bool), 0)

            def step(S, inp):
                qi, ki, ui, wi = inp
                attn = jnp.einsum('bhid,bhjd->bhij', qi, ki)
                attn = jnp.where(mask_incl, attn, 0.0)
                u_i = ui - jnp.einsum('bhik,bhkd->bhid', wi, S)
                o_i = jnp.einsum('bhik,bhkd->bhid', qi, S) + jnp.einsum('bhij,bhjd->bhid', attn, u_i)
                S = S + jnp.einsum('bhci,bhcd->bhid', ki, u_i)
                return (S, o_i)
            S0 = jnp.zeros((b, h, dk, dv), q.dtype)
            xs = tuple((jnp.moveaxis(a, 2, 0) for a in (qc, kc, u, w)))
            S, o = jax.lax.scan(step, S0, xs)
            o = jnp.moveaxis(o, 0, 2).reshape(b, h, L, dv)
            return (o, S)
        B, L, D = hidden_states.shape
        H = mix_w.shape[0]
        dh = mix_w.shape[1]
        q = jax.nn.silu(dw_causal_conv(hidden_states @ Wq, conv_q_w))
        k = jax.nn.silu(dw_causal_conv(hidden_states @ Wk, conv_k_w))
        v = jax.nn.silu(dw_causal_conv(hidden_states @ Wv, conv_v_w))
        q4 = q.reshape(B, L, H, dh)
        k4 = k.reshape(B, L, H, dh)
        v4 = v.reshape(B, L, H, dh)
        beta = jax.nn.sigmoid(hidden_states @ Wb)
        delta_out, _ = delta_rule_chunkwise(jnp.transpose(q4, (0, 2, 1, 3)), jnp.transpose(k4, (0, 2, 1, 3)), jnp.transpose(v4, (0, 2, 1, 3)), jnp.transpose(beta, (0, 2, 1)))
        delta_out = jnp.transpose(delta_out, (0, 2, 1, 3))
        v_direct = v4
        vflat = v4.reshape(B, L, H * dh)
        local_out = dw_causal_conv(vflat, local_w).reshape(B, L, H, dh)
        mid_out = dw_causal_conv(vflat, mid_w).reshape(B, L, H, dh)
        outs = [local_out, mid_out, delta_out, v_direct]
        feats = []
        for o_ in outs:
            feats.append(o_.mean(-1))
            feats.append(jnp.var(o_, -1, ddof=1))
        for i in range(4):
            for j in range(i + 1, 4):
                feats.append((outs[i] * outs[j]).mean(-1))
        router_feat = jnp.concatenate([hidden_states] + feats, axis=-1)
        h1 = jax.nn.silu(router_feat @ r_w1 + r_b1)
        logits = (h1 @ r_w2 + r_b2).reshape(B, L, H, 4)
        p = jax.nn.softmax(logits, -1)
        p = p * (1.0 - 4.0 * FLOOR) + FLOOR
        mixed = sum((p[..., i:i + 1] * outs[i] for i in range(4)))
        rms = jnp.sqrt(jnp.mean(mixed * mixed, -1, keepdims=True) + EPS_MIX)
        mixed = mixed / rms * mix_w
        rms2 = jnp.sqrt(jnp.mean(mixed * mixed, -1, keepdims=True) + EPS_NORM)
        o_n = mixed / rms2 * onorm_w
        return o_n.reshape(B, L, H * dh) @ Wo

    def _L0_attn_b_ref(x, w_qkv, w_out):
        import jax, jax.numpy as jnp
        import numpy as np
        import math
        D_MODEL = 256
        NUM_HEADS = 16
        HEAD_DIM = D_MODEL // NUM_HEADS
        B, S, _ = x.shape
        qkv = jnp.einsum('bsi,oi->bso', x, w_qkv)
        q, k, v = jnp.split(qkv, 3, axis=-1)

        def to_heads(t):
            return t.reshape(B, S, NUM_HEADS, HEAD_DIM).transpose(0, 2, 1, 3)
        q, k, v = (to_heads(q), to_heads(k), to_heads(v))
        scale = 1.0 / math.sqrt(HEAD_DIM)
        logits = jnp.einsum('bhsd,bhtd->bhst', q, k) * scale
        mask = jnp.tril(jnp.ones((S, S), dtype=bool))
        neg_inf = jnp.finfo(jnp.float32).min
        logits = jnp.where(mask, logits, neg_inf)
        probs = jax.nn.softmax(logits, axis=-1)
        probs = probs * mask.astype(probs.dtype)
        out = jnp.einsum('bhst,bhtd->bhsd', probs, v)
        out = out.transpose(0, 2, 1, 3).reshape(B, S, D_MODEL)
        return jnp.einsum('bsi,oi->bso', out, w_out)

    def _L0_ffn_ref(x, slot_init, slot_scale, w1, b1, w2, b2, gru_wih, gru_whh, gru_bih, gru_bhh, wv, bv, wo, bo, tau):
        import jax, jax.numpy as jnp
        import numpy as np
        D_MODEL = 256
        NUM_SLOTS = 64
        TOP_K = 8
        B, T = (4, 1024)

        def _forward(x, slot_init, slot_scale, w1, b1, w2, b2, gru_wih, gru_whh, gru_bih, gru_bhh, wv, bv, wo, bo, tau):
            Bn, Tn, D = x.shape
            Sn = slot_init.shape[0]
            S = jnp.broadcast_to((slot_init * slot_scale)[None], (Bn, Sn, D)).astype(x.dtype)
            slot_mean = S.mean(axis=1, keepdims=True)
            ctx = jnp.concatenate([x, jnp.broadcast_to(slot_mean, x.shape)], axis=-1)
            h = jax.nn.gelu(ctx @ w1.T + b1, approximate=False)
            route_logits = (h @ w2.T + b2) / (jnp.abs(tau) + 0.1)
            topk_vals, topk_idx = jax.lax.top_k(route_logits, TOP_K)
            topk_w = jax.nn.softmax(topk_vals, axis=-1)
            alpha = jnp.sum(topk_w[..., None] * jax.nn.one_hot(topk_idx, Sn, dtype=x.dtype), axis=-2)
            slot_input = jnp.einsum('bts,btd->bsd', alpha, x)
            slot_wsum = alpha.sum(axis=1) + 1e-08
            gi = (slot_input / slot_wsum[..., None]).reshape(Bn * Sn, D)
            hs = S.reshape(Bn * Sn, D)
            gx = gi @ gru_wih.T + gru_bih
            gh = hs @ gru_whh.T + gru_bhh
            xr, xz, xn = jnp.split(gx, 3, axis=-1)
            hr, hz, hn = jnp.split(gh, 3, axis=-1)
            r = jax.nn.sigmoid(xr + hr)
            z = jax.nn.sigmoid(xz + hz)
            n = jnp.tanh(xn + r * hn)
            h_new = (1.0 - z) * n + z * hs
            S_new = h_new.reshape(Bn, Sn, D)
            slot_values = S_new @ wv.T + bv
            out = jnp.einsum('bts,bsd->btd', alpha, slot_values)
            return out @ wo.T + bo
        return _forward(x, slot_init, slot_scale, w1, b1, w2, b2, gru_wih, gru_whh, gru_bih, gru_bhh, wv, bv, wo, bo, tau)
    x = L0_attn_a_hidden_states
    x = x + _L0_attn_a_ref(_layernorm(x, axis=-1), L0_attn_a_Wq, L0_attn_a_Wk, L0_attn_a_Wv, L0_attn_a_Wb, L0_attn_a_conv_q_w, L0_attn_a_conv_k_w, L0_attn_a_conv_v_w, L0_attn_a_local_w, L0_attn_a_mid_w, L0_attn_a_r_w1, L0_attn_a_r_b1, L0_attn_a_r_w2, L0_attn_a_r_b2, L0_attn_a_mix_w, L0_attn_a_onorm_w, L0_attn_a_Wo)
    x = x + _L0_ffn_ref(_layernorm(x, axis=-1), L0_ffn_slot_init, L0_ffn_slot_scale, L0_ffn_w1, L0_ffn_b1, L0_ffn_w2, L0_ffn_b2, L0_ffn_gru_wih, L0_ffn_gru_whh, L0_ffn_gru_bih, L0_ffn_gru_bhh, L0_ffn_wv, L0_ffn_bv, L0_ffn_wo, L0_ffn_bo, L0_ffn_tau)
    x = x + _L0_attn_b_ref(_layernorm(x, axis=-1), L0_attn_b_w_qkv, L0_attn_b_w_out)
    x = x + _L0_ffn_ref(_layernorm(x, axis=-1), L0_ffn_slot_init, L0_ffn_slot_scale, L0_ffn_w1, L0_ffn_b1, L0_ffn_w2, L0_ffn_b2, L0_ffn_gru_wih, L0_ffn_gru_whh, L0_ffn_gru_bih, L0_ffn_gru_bhh, L0_ffn_wv, L0_ffn_bv, L0_ffn_wo, L0_ffn_bo, L0_ffn_tau)
    return x

_drawn_inputs = setup_inputs


def setup_inputs(seed=0):
    import zlib

    import numpy as np

    out = dict(_drawn_inputs(seed))
    spreads = {'L0_attn_a_r_b1': (0.0, 0.432),
     'L0_attn_a_mix_w': (1.0, 0.2),
     'L0_attn_a_onorm_w': (1.0, 0.2),
     'L0_ffn_slot_scale': (1.0, 0.6),
     'L0_ffn_b1': (0.0, 0.566),
     'L0_ffn_b2': (0.0, 0.468),
     'L0_ffn_gru_bih': (0.0, 0.1),
     'L0_ffn_gru_bhh': (0.0, 0.274),
     'L0_ffn_bv': (0.0, 0.1),
     'L0_ffn_bo': (0.0, 0.1)}
    factors = {'L0_ffn_gru_whh': 4.553}
    for name, (base, spread) in spreads.items():
        noise = np.random.default_rng([zlib.crc32(name.encode()), seed]).standard_normal(out[name].shape)
        drawn = base * np.exp(spread * noise) if base else spread * noise
        out[name] = jnp.asarray(drawn.astype(out[name].dtype))
    for name, factor in factors.items():
        out[name] = (out[name] * factor).astype(out[name].dtype)
    return out
```

```python
from collections import namedtuple
from contextlib import ExitStack

import numpy as np

import concourse.bass as bass
from concourse import mybir

ALU = mybir.AluOpType
ACT = mybir.ActivationFunctionType
AX = mybir.AxisListType
F32 = mybir.dt.float32
BF16 = mybir.dt.bfloat16

P = 128
SEQS, L, D = 16, 1024, 256
T = L // P
HALVES = D // P
BANK = 512
NB = L // BANK
H, DH = 4, 64
MID, LOCAL = 25, 7
SHIFTS, CG = 4, 32
GROUPS = D // CG
MID_STEPS, LOCAL_STEPS = -(-MID // SHIFTS), -(-LOCAL // SHIFTS)
PAD = SHIFTS * (MID_STEPS - 1)
PATHS = 4
FEATS = 14 * H
HID = 2 * (D + FEATS)
HC = -(-HID // P)
HLAST = HID - (HC - 1) * P
FLOOR = 0.01
EPS = 1e-5
SLOTS, FH, TOPK = 64, 128, 8
AH, AD = 16, 16
NCOMB = 6
QROWS = NCOMB * AD + 3
NEG = -1.0e30
LEVELS = 7


def chain_of(eng, sem):
    count = [0]

    def settle(ins):
        count[0] += 1
        ins.then_inc(sem, 1)
        eng.wait_ge(sem, count[0])

    return settle


def bc(ap, n):
    return ap.unsqueeze(len(ap.shape)).to_broadcast(list(ap.shape) + [n])


def named(kind, **things):
    return namedtuple(kind, things)(**things)


def sems(nc, ctx, prefix, names):
    return named("Semaphores", **{n: ctx.enter_context(nc.semaphore(f"{prefix}_{n}")) for n in names.split()})


def clear(nc, s):
    nums = [x.num for x in s]
    nc.sync.sem_clear(range(min(nums), max(nums) + 1))
    nc.all_engine_barrier()



def setup(nc, w, k, ps, s):
    with ExitStack() as tmp:
        def sb(name, shape, dt=F32):
            return tmp.enter_context(nc.sbuf_tensor(name, shape, dt))

        taps = sb("su_taps", [P, (MID_STEPS + LOCAL_STEPS) * GROUPS])
        eye32 = sb("su_eye32", [P, CG])
        wo_raw = sb("su_wo", [P, HALVES, D])
        onorm = sb("su_onorm", [P, 1])
        tau = sb("su_tau", [P, 3])
        b_raw = sb("su_b_raw", [P, 6 * P])
        slot_init = sb("su_slot", [SLOTS, D])
        slot_scale = sb("su_scale", [SLOTS, 1])
        w1s = sb("su_w1s", [P, HALVES, FH])
        b1 = sb("su_b1", [FH, 1])
        mean64 = sb("su_mean", [SLOTS, 1])
        slot_mean = sb("su_smean", [P, HALVES])
        hsT = sb("su_hsT", [P, HALVES, SLOTS])
        whhT = sb("su_whhT", [P, HALVES, 3 * D])
        bih = sb("su_bih", [SLOTS, 3 * D])
        bhh = sb("su_bhh", [SLOTS, 3 * D])
        wv = sb("su_wv", [P, HALVES, D])
        woT = sb("su_woT", [P, HALVES, D])
        bvb = sb("su_bvb", [P, HALVES, SLOTS])
        bo = sb("su_bo", [SLOTS, D])

        with nc.Block() as block:
            @block.sync
            def _(sp):
                loads = [
                    (k.wq, w["Wq"].rearrange("(k p) n -> p k n", p=P)),
                    (k.wk, w["Wk"].rearrange("(k p) n -> p k n", p=P)),
                    (k.wv, w["Wv"].rearrange("(k p) n -> p k n", p=P)),
                    (k.wb, w["Wb"].rearrange("(k p) n -> p k n", p=P)),
                    (k.cw, w["cw"].rearrange("s (a p) t -> p s a t", p=P)),
                    (taps, w["taps"]), (eye32, w["eye32"]),
                    (wo_raw, w["Wo"].rearrange("(k p) n -> p k n", p=P)),
                    (onorm, w["onorm"]), (k.mixw, w["mixw"]),
                    (k.rw1[:, 0:2, :], w["rw1"][0:D].rearrange("(k p) n -> p k n", p=P)),
                    (k.rw1[0:FEATS, 2, :], w["rw1"][D:D + FEATS]),
                    (k.rb1[:, 0:HC - 1], w["rb1"][0:(HC - 1) * P].rearrange("(k p) -> p k", p=P)),
                    (k.rb1[0:HLAST, HC - 1:HC], w["rb1"][(HC - 1) * P:HID].rearrange("(p k) -> p k", k=1)),
                    (k.rw2[:, 0:HC - 1, :], w["rw2"][0:(HC - 1) * P].rearrange("(k p) n -> p k n", p=P)),
                    (k.rw2[0:HLAST, HC - 1, :], w["rw2"][(HC - 1) * P:HID]),
                    (k.rb2, w["rb2"]),
                    (k.ident, w["ident"]), (b_raw[:, 0:4 * P], w["identb"]),
                    (k.maskT, w["maskT"]), (k.incl, w["incl"]),
                    (b_raw[:, 4 * P:5 * P], w["causal"]), (b_raw[:, 5 * P:], w["causalT"]),
                    (k.ones2, w["ones2"]),
                    (tau[:, 0:1], w["tau"]), (slot_init, w["slot_init"]), (slot_scale, w["slot_scale"]),
                    (k.w1x, w["w1T"][0:D].rearrange("(k p) n -> p k n", p=P)),
                    (w1s, w["w1T"][D:2 * D].rearrange("(k p) n -> p k n", p=P)),
                    (b1, w["b1"]), (k.w2T, w["w2T"]), (k.b2, w["b2"]),
                    (k.wihT, w["wihT"].rearrange("(k p) n -> p k n", p=P)),
                    (whhT, w["whhT"].rearrange("(k p) n -> p k n", p=P)),
                    (bih, w["bih"]), (bhh, w["bhh"]),
                    (wv, w["wv"].rearrange("(k p) n -> p k n", p=P)),
                    (woT, w["woT"].rearrange("(k p) n -> p k n", p=P)),
                    (bvb, w["bvb"].rearrange("(k p) n -> p k n", p=P)), (bo, w["bo"]),
                    (k.wqkvT, w["wqkvT"].rearrange("(k p) n -> p k n", p=P)),
                    (k.woutT, w["woutT"].rearrange("(k p) n -> p k n", p=P)),
                ]
                for dst, src in loads:
                    dst = dst if isinstance(dst, bass.AP) else dst[:]
                    sp.dma_start(dst, src, allow_slow_non_contiguous=True).then_inc(s.loaded, 16)
                sp.wait_ge(s.loaded, 16 * len(loads))
                sp.sem_inc(s.all_in, 1)

            @block.gpsimd
            def _(pool):
                nc.gpsimd.memset(mean64[:], 1.0 / SLOTS).then_inc(s.const, 1)
                nc.gpsimd.memset(k.mhalf[:], -0.5).then_inc(s.const, 1)
                nc.gpsimd.memset(k.xn[:, :, D:D + 1], 1.0).then_inc(s.const, 1)

            @block.vector
            def _(dve):
                settle = chain_of(dve, s.dve)
                dve.wait_ge(s.all_in, 1)
                nc.vector.tensor_tensor(k.stack[:].rearrange("p n c -> p n c"), bc(taps[:], CG),
                                        eye32[:].unsqueeze(1).to_broadcast([P, (MID_STEPS + LOCAL_STEPS) * GROUPS, CG]),
                                        ALU.mult).then_inc(s.prepared, 1)
                for a in range(HALVES):
                    nc.vector.tensor_scalar(k.wo[:, a, :], wo_raw[:, a, :], onorm[:, 0:1], None,
                                            ALU.mult).then_inc(s.prepared, 1)
                nc.vector.tensor_copy(k.identb[:], b_raw[:, 0:4 * P]).then_inc(s.prepared, 1)
                nc.vector.tensor_copy(k.causal[:], b_raw[:, 4 * P:5 * P]).then_inc(s.prepared, 1)
                nc.vector.tensor_copy(k.causalT[:], b_raw[:, 5 * P:]).then_inc(s.prepared, 1)
                settle(nc.vector.tensor_scalar(tau[:, 1:2], tau[:, 0:1], -1.0, None, ALU.mult))
                settle(nc.vector.tensor_tensor(tau[:, 2:3], tau[:, 0:1], tau[:, 1:2], ALU.max))
                settle(nc.vector.tensor_scalar(tau[:, 1:2], tau[:, 2:3], 0.1, None, ALU.add))
                settle(nc.vector.reciprocal(k.invtau[:], tau[:, 1:2]))
                nc.vector.tensor_scalar(k.hs[:], slot_init[:], slot_scale[:, 0:1], None, ALU.mult).then_inc(s.hs, 1)
                nc.vector.tensor_tensor(k.bihn[:], bih[:, 2 * D:], bih[:, 2 * D:], ALU.max).then_inc(s.prepared, 1)
                dve.wait_ge(s.pe, 1)
                nc.vector.tensor_copy(slot_mean[:], ps[:, 0, 0:HALVES]).then_inc(s.back, 1)
                dve.wait_ge(s.pe, 2)
                nc.vector.tensor_copy(hsT[:].rearrange("p a s -> p (a s)"), ps[:, 1, 0:HALVES * SLOTS]).then_inc(s.back, 1)
                dve.wait_ge(s.pe, 3)
                nc.vector.tensor_tensor(k.hbias[:], ps[0:FH, 2, 0:1], b1[:], ALU.add).then_inc(s.prepared, 1)
                dve.wait_ge(s.pe, 4)
                settle(nc.vector.tensor_tensor(k.grz[:], ps[0:SLOTS, 3, 0:2 * D], bhh[:, 0:2 * D], ALU.add))
                settle(nc.vector.tensor_tensor(k.grz[:], k.grz[:], bih[:, 0:2 * D], ALU.add))
                settle(nc.vector.tensor_tensor(k.hn[:], ps[0:SLOTS, 4, 0:D], bhh[:, 2 * D:], ALU.add))
                dve.wait_ge(s.pe, 5)
                for a in range(HALVES):
                    settle(nc.vector.tensor_copy(k.wvo[:, a, :], ps[:, 5 + a, 0:D]))
                settle(nc.vector.tensor_tensor(k.bvo[:], ps[0:SLOTS, 7, 0:D], bo[:], ALU.add))

            @block.tensor
            def _(pe):
                pe.wait_ge(s.hs, 1)
                pe.wait_ge(s.const, 3)
                for a in range(HALVES):
                    last = nc.tensor.matmul(ps[:, 0, a:a + 1], k.hs[:, a * P:(a + 1) * P], mean64[:],
                                            start=(a == 0), stop=(a == HALVES - 1), skip_group_check=True)
                last.then_inc(s.pe, 1)
                for a in range(HALVES):
                    last = nc.tensor.transpose(ps[:, 1, a * SLOTS:(a + 1) * SLOTS], k.hs[:, a * P:(a + 1) * P],
                                               k.ident[0:SLOTS, 0:SLOTS])
                last.then_inc(s.pe, 1)
                pe.wait_ge(s.back, 1)
                for a in range(HALVES):
                    last = nc.tensor.matmul(ps[0:FH, 2, 0:1], w1s[:, a, :], slot_mean[:, a:a + 1],
                                            start=(a == 0), stop=(a == HALVES - 1))
                last.then_inc(s.pe, 1)
                pe.wait_ge(s.back, 2)
                for a in range(HALVES):
                    nc.tensor.matmul(ps[0:SLOTS, 3, 0:2 * D], hsT[:, a, :], whhT[:, a, 0:2 * D],
                                     start=(a == 0), stop=(a == HALVES - 1))
                for a in range(HALVES):
                    last = nc.tensor.matmul(ps[0:SLOTS, 4, 0:D], hsT[:, a, :], whhT[:, a, 2 * D:],
                                            start=(a == 0), stop=(a == HALVES - 1))
                last.then_inc(s.pe, 1)
                for c in range(HALVES):
                    for a in range(HALVES):
                        nc.tensor.matmul(ps[:, 5 + c, 0:D], wv[:, a, c * P:(c + 1) * P], woT[:, a, :],
                                         start=(a == 0), stop=(a == HALVES - 1))
                for a in range(HALVES):
                    last = nc.tensor.matmul(ps[0:SLOTS, 7, 0:D], bvb[:, a, :], woT[:, a, :],
                                            start=(a == 0), stop=(a == HALVES - 1))
                last.then_inc(s.pe, 1)



def layer_norm(nc, k, ps, s, x, load=None):
    with nc.Block() as block:
        if load is not None:
            @block.sync
            def _(sp):
                sp.dma_start(x[:], load).then_inc(s.x_in, 16)

        @block.vector
        def _(dve):
            settle = chain_of(dve, s.dve)
            if load is not None:
                dve.wait_ge(s.x_in, 16)
            for t in range(T):
                last = nc.vector.bn_stats(k.stats[:, t, :], x[:, t, :])
            settle(last)
            for t in range(T):
                last = nc.vector.bn_aggr(k.mv[:, t, :], k.stats[:, t, :])
            settle(last)
            nc.vector.tensor_scalar(k.vare[:], k.mv[:, :, 1], EPS, None, ALU.add).then_inc(s.var, 1)
            dve.wait_ge(s.rstd, 1)
            for t in range(T):
                nc.vector.tensor_scalar(k.xn[:, t, 0:D], x[:, t, :], k.mv[:, t, 0:1], k.rstd[:, t:t + 1],
                                        ALU.subtract, ALU.mult).then_inc(s.xn, 1)
            for n in range(NB):
                dve.wait_ge(s.turned, HALVES * n + 2)
                nc.vector.tensor_copy(k.xnT[:, 1, n * BANK:(n + 1) * BANK], ps[:, HALVES * n + 1, :])

        @block.gpsimd
        def _(pool):
            pool.wait_ge(s.var, 1)
            nc.gpsimd.tensor_tensor(k.rstd[:], k.vare[:], k.mhalf[:, 0:T], ALU.pow).then_inc(s.rstd, 1)

        @block.tensor
        def _(pe):
            for n in range(NB):
                for a in range(HALVES):
                    for i in range(BANK // P):
                        t = n * (BANK // P) + i
                        pe.wait_ge(s.xn, t + 1)
                        last = nc.tensor.transpose(ps[:, HALVES * n + a, i * P:(i + 1) * P],
                                                   k.xn[:, t, a * P:(a + 1) * P], k.ident[:])
                    last.then_inc(s.turned, 1)

        @block.scalar
        def _(act):
            for n in range(NB):
                act.wait_ge(s.turned, HALVES * n + 1)
                nc.scalar.activation(k.xnT[:, 0, n * BANK:(n + 1) * BANK], ps[:, HALVES * n, :], ACT.Copy)
    clear(nc, s)



def project_and_convolve(nc, k, m, vT, sq, ps, s):
    with ExitStack() as tmp:
        pre = tmp.enter_context(nc.sbuf_tensor("pc_pre", [P, 2, HALVES, 3 + L], F32))
        acc = tmp.enter_context(nc.sbuf_tensor("pc_acc", [P, HALVES, L], F32))
        outs = [vT, m.kT, m.qT]
        with nc.Block() as block:
            @block.gpsimd
            def _(pool):
                nc.gpsimd.memset(pre[:, :, :, 0:3], 0.0).then_inc(s.padded, 1)

            @block.tensor
            def _(pe):
                for i, w in enumerate((k.wv, k.wk, k.wq)):
                    for a in range(HALVES):
                        for n in range(NB):
                            u = (i * HALVES + a) * NB + n
                            if u >= 4:
                                pe.wait_ge(s.pre, u - 3)
                            for c in range(HALVES):
                                last = nc.tensor.matmul(ps[:, u % 4, :], w[:, c, a * P:(a + 1) * P],
                                                        k.xnT[:, c, n * BANK:(n + 1) * BANK],
                                                        start=(c == 0), stop=(c == HALVES - 1))
                            last.then_inc(s.proj, 1)
                for t in range(T):
                    for c in range(HALVES):
                        last = nc.tensor.matmul(ps[:, 4, t * H:(t + 1) * H], k.xnT[:, c, t * P:(t + 1) * P],
                                                k.wb[:, c, :], start=(t == 0 and c == 0), stop=(c == HALVES - 1),
                                                skip_group_check=True)
                last.then_inc(s.beta, 1)
                for i, src in enumerate((vT, m.kT)):
                    pe.wait_ge(s.silu, HALVES * (i + 1))
                    if i == 0:
                        pe.wait_ge(s.pre, 3 * HALVES * NB)
                    for u in range(T // 2):
                        if i == 1:
                            pe.wait_ge(s.tm, u + 1)
                        for j in range(2):
                            for a in range(HALVES):
                                last = nc.tensor.transpose(ps[:, u, j * D + a * P:j * D + (a + 1) * P],
                                                           src[:, a, (2 * u + j) * P:(2 * u + j + 1) * P], k.ident[:])
                        last.then_inc(s.turned, 1)
                for i in range(2):
                    for a in range(HALVES):
                        pe.wait_ge(s.squared, HALVES * i + a + 1)
                        for t in range(T):
                            last = nc.tensor.matmul(ps[:, 5 + i, t * H + 2 * a:t * H + 2 * a + 2],
                                                    sq[:, i, a, t * P:(t + 1) * P], k.ones2[:],
                                                    start=(a == 0 and t == 0), stop=True, skip_group_check=True)
                    last.then_inc(s.sums, 1)

            @block.scalar
            def _(act):
                def evacuate(i):
                    for a in range(HALVES):
                        for n in range(NB):
                            u = (i * HALVES + a) * NB + n
                            act.wait_ge(s.proj, u + 1)
                            if i == 2:
                                act.wait_ge(s.conv, a + 1)
                            nc.scalar.activation(pre[:, i % 2, a, 3 + n * BANK:3 + (n + 1) * BANK], ps[:, u % 4, :],
                                                 ACT.Copy).then_inc(s.pre, 1)

                def silu(i):
                    for a in range(HALVES):
                        act.wait_ge(s.conv, HALVES * i + a + 1)
                        nc.scalar.activation(outs[i][:, a, :], acc[:, a, :], ACT.Silu).then_inc(s.silu, 1)

                def square(i):
                    act.wait_ge(s.silu, HALVES * (i + 2))
                    for a in range(HALVES):
                        nc.scalar.activation(sq[:, i, a, :], outs[i + 1][:, a, :], ACT.Square).then_inc(s.squared, 1)

                evacuate(0)
                evacuate(1)
                silu(0)
                evacuate(2)
                act.wait_ge(s.beta, 1)
                nc.scalar.activation(m.beta[:], ps[:, 4, 0:T * H], ACT.Tanh, scale=0.5).then_inc(s.tanh, 1)
                for u in range(T // 2):
                    act.wait_ge(s.turned, u + 1)
                    nc.scalar.activation(m.v_tm[:, 2 * u:2 * u + 2, :].rearrange("p t d -> p (t d)"), ps[:, u, :],
                                         ACT.Copy).then_inc(s.tm, 1)
                silu(1)
                square(0)
                for u in range(T // 2):
                    act.wait_ge(s.turned, T // 2 + u + 1)
                    nc.scalar.activation(m.k_tm[:, 2 * u:2 * u + 2, :].rearrange("p t d -> p (t d)"), ps[:, u, :],
                                         ACT.Copy)
                silu(2)
                square(1)

            @block.vector
            def _(dve):
                settle = chain_of(dve, s.dve)
                dve.wait_ge(s.padded, 1)
                for i in range(3):
                    tap = (2, 1, 0)[i]
                    for a in range(HALVES):
                        dve.wait_ge(s.pre, (i * HALVES + a + 1) * NB)
                        if i:
                            dve.wait_ge(s.silu, HALVES * (i - 1) + a + 1)
                        src = pre[:, i % 2, a, :]
                        settle(nc.vector.tensor_scalar(acc[:, a, :], src[:, 0:L], k.cw[:, tap, a, 0:1], None, ALU.mult))
                        for j in range(1, 4):
                            ins = nc.vector.scalar_tensor_tensor(acc[:, a, :], src[:, j:j + L], k.cw[:, tap, a, j:j + 1],
                                                                 acc[:, a, :], ALU.mult, ALU.add)
                            if j < 3:
                                settle(ins)
                            else:
                                ins.then_inc(s.conv, 1)
                    if i == 1:
                        dve.wait_ge(s.tanh, 1)
                        settle(nc.vector.tensor_scalar(m.beta[:], m.beta[:], 0.5, 0.5, ALU.mult, ALU.add))
                for i in range(2):
                    dve.wait_ge(s.sums, i + 1)
                    ins = nc.vector.tensor_scalar(m.ss[:, i, :], ps[:, 5 + i, 0:T * H], 1e-12, None, ALU.add)
                    settle(ins)
                nc.vector.tensor_scalar(m.ss2[:], m.ss[:], 1.0, None, ALU.mult).then_inc(s.ss, 1)
                settle(nc.vector.reciprocal(m.negd[:], m.ss[:, 0, :]))
                settle(nc.vector.tensor_tensor(m.negd[:], m.negd[:], m.beta[:], ALU.mult))
                settle(nc.vector.tensor_scalar(m.negd[:], m.negd[:], -1.0, None, ALU.mult))
                dve.wait_ge(s.rnorm, 1)
                settle(nc.vector.tensor_tensor(m.e[:], m.rn[:, 0, :], m.beta[:], ALU.mult))
                nc.vector.tensor_tensor(m.ev[:].rearrange("p t (h d) -> p (t h) d", h=H),
                                        m.v_tm[:].rearrange("p t (h d) -> p (t h) d", h=H), bc(m.e[:], DH), ALU.mult)

            @block.gpsimd
            def _(pool):
                pool.wait_ge(s.ss, 1)
                nc.gpsimd.tensor_tensor(m.rn[:], m.ss2[:], k.mhalf[:].rearrange("p (i n) -> p i n", i=2),
                                        ALU.pow).then_inc(s.rnorm, 1)
    clear(nc, s)


def long_convolutions(nc, k, m, vT, ps, s):
    with ExitStack() as tmp:
        rep = tmp.enter_context(nc.sbuf_tensor("lc_rep", [P, GROUPS, PAD + L], F32))
        out_cm = tmp.enter_context(nc.sbuf_tensor("lc_out", [P, HALVES, L], F32))
        units = [(c, a, n) for c in range(2) for a in range(HALVES) for n in range(NB)]
        with nc.Block() as block:
            @block.gpsimd
            def _(pool):
                nc.gpsimd.memset(rep[:, :, 0:PAD + SHIFTS - 1], 0.0).then_inc(s.padded, 1)

            @block.sync
            def _(sp):
                sp.wait_ge(s.padded, 1)
                for sh in range(SHIFTS):
                    for g in range(P // CG):
                        sp.dma_start(rep[CG * sh:CG * (sh + 1), g::P // CG, PAD + sh:PAD + L],
                                     vT[CG * g:CG * (g + 1), :, 0:L - sh]).then_inc(s.rep, 16)

            @block.tensor
            def _(pe):
                pe.wait_ge(s.rep, 16 * SHIFTS * (P // CG))
                for u, (c, a, n) in enumerate(units):
                    steps, base = ((LOCAL_STEPS, MID_STEPS), (MID_STEPS, 0))[c]
                    if u >= 4:
                        pe.wait_ge(s.evac, u - 3)
                    for j in range(steps):
                        for g in range(P // CG):
                            gg = a * (P // CG) + g
                            last = nc.tensor.matmul(
                                ps[CG * g:CG * (g + 1), u % 4, :], k.stack[:, (base + j) * GROUPS + gg, :],
                                rep[:, gg, PAD + n * BANK - SHIFTS * j:PAD + (n + 1) * BANK - SHIFTS * j],
                                start=(j == 0), stop=(j == steps - 1))
                    last.then_inc(s.conv, 1)
                    if u % 4 == 3:
                        c = u // 4
                        pe.wait_ge(s.evac, u + 1)
                        for v in range(T // 2):
                            if c:
                                pe.wait_ge(s.tm, v + 1)
                            for j in range(2):
                                for aa in range(HALVES):
                                    last = nc.tensor.transpose(
                                        ps[:, 4 + v, j * D + aa * P:j * D + (aa + 1) * P],
                                        out_cm[:, aa, (2 * v + j) * P:(2 * v + j + 1) * P], k.ident[:])
                            last.then_inc(s.turned, 1)

            @block.scalar
            def _(act):
                for u, (c, a, n) in enumerate(units):
                    act.wait_ge(s.conv, u + 1)
                    nc.scalar.activation(out_cm[:, a, n * BANK:(n + 1) * BANK], ps[:, u % 4, :],
                                         ACT.Copy).then_inc(s.evac, 1)

            @block.vector
            def _(dve):
                for c, dst in enumerate((m.local_tm, m.mid_tm)):
                    for v in range(T // 2):
                        dve.wait_ge(s.turned, c * (T // 2) + v + 1)
                        nc.vector.tensor_copy(dst[:, 2 * v:2 * v + 2, :].rearrange("p t d -> p (t d)"),
                                              ps[:, 4 + v, :]).then_inc(s.tm, 1)
    clear(nc, s)


def invert_blocks(nc, k, m, TT, ps, s):
    HP = H * P
    KEPT = 3
    with ExitStack() as tmp:
        def sb(name, shape):
            return tmp.enter_context(nc.sbuf_tensor(name, shape, F32))

        A = sb("ib_a", [P, 2, HP])
        AT = sb("ib_at", [P, 2, HP])
        AjT = sb("ib_ajt", [P, 2, KEPT, HP])
        X = sb("ib_x", [P, 2, HP])
        XT = sb("ib_xt", [P, 2, HP])
        Z = sb("ib_z", [P, 2, HP])

        def head(ap, h):
            return ap[:, h * P:(h + 1) * P]

        x_out, xt_out = (s.x_even, s.x_odd), (s.xt_even, s.xt_odd)
        z_out, masked = (s.z_even, s.z_odd), (s.m_even, s.m_odd)
        with nc.Block() as block:
            @block.tensor
            def _(pe):
                for pair in range(T // 2):
                    for i in range(2):
                        t = 2 * pair + i
                        for h in range(H):
                            rows = slice(DH * (h % 2), DH * (h % 2) + DH)
                            kt = m.kT[rows, h // 2, t * P:(t + 1) * P]
                            last = nc.tensor.matmul(head(ps[:, 3 * i + 2 - 2 * (h % 2), :], h), kt, kt, start=(h < 2),
                                                    stop=True, skip_group_check=True)
                        last.then_inc(s.gram, 1)
                    for i in range(2):
                        pe.wait_ge(s.a, 2 * (2 * pair + i + 1))
                        for h in range(H):
                            last = nc.tensor.transpose(head(ps[:, 3 * i + 2, :], h), head(A[:, i, :], h), k.ident[:])
                        last.then_inc(s.at_ps, 1)
                    for i in range(2):
                        if pair:
                            pe.wait_ge(xt_out[i], LEVELS * pair)
                        pe.wait_ge(masked[i], LEVELS * pair + 1)
                        nc.tensor.matmul(ps[:, 3 * i, :], k.identb[:, 0:P], k.identb[:], start=True, stop=False,
                                         skip_group_check=True)
                        for h in range(H):
                            last = nc.tensor.matmul(head(ps[:, 3 * i, :], h), head(AjT[:, i, (LEVELS * pair) % KEPT, :], h), k.ident[:],
                                                    start=False, stop=False, skip_group_check=True)
                        last.then_inc(s.x_ps, 1)
                        nc.tensor.matmul(ps[:, 3 * i + 1, :], k.identb[:, 0:P], k.identb[:], start=True, stop=False,
                                         skip_group_check=True)
                        nc.tensor.matmul(ps[:, 3 * i + 1, :], k.ident[:], AjT[:, i, (LEVELS * pair) % KEPT, :], start=False, stop=False,
                                         skip_group_check=True).then_inc(s.xt_ps, 1)
                    for j in range(1, LEVELS):
                        for i in range(2):
                            pe.wait_ge(masked[i], LEVELS * pair + j + 1)
                            pe.wait_ge(x_out[i], (LEVELS - 1) * pair + j)
                            for h in range(H):
                                last = nc.tensor.matmul(head(ps[:, 3 * i + 2, :], h), head(AjT[:, i, (LEVELS * pair + j) % KEPT, :], h),
                                                        head(X[:, i, :], h), start=(h == 0), stop=True,
                                                        skip_group_check=True)
                            last.then_inc(s.y, 1)
                        for i in range(2):
                            pe.wait_ge(xt_out[i], LEVELS * pair + j)
                            pe.wait_ge(z_out[i], (LEVELS - 1) * pair + j)
                            if j < LEVELS - 1:
                                for h in range(H):
                                    last = nc.tensor.matmul(head(ps[:, 3 * i, :], h), head(XT[:, i, :], h),
                                                            head(Z[:, i, :], h), start=False, stop=False,
                                                            skip_group_check=True)
                                last.then_inc(s.x_ps, 1)
                            for h in range(H):
                                last = nc.tensor.matmul(head(ps[:, 3 * i + 1, :], h), head(Z[:, i, :], h),
                                                        head(XT[:, i, :], h), start=False, stop=(j == LEVELS - 1),
                                                        skip_group_check=True)
                            last.then_inc(s.xt_ps, 1)

            @block.vector
            def _(dve):
                for pair in range(T // 2):
                    for i in range(2):
                        t = 2 * pair + i
                        dve.wait_ge(s.gram, t + 1)
                        for odd in range(2):
                            nc.vector.tensor_tensor(A[:, i, :].rearrange("p (h n) -> p h n", h=H)[:, odd::2],
                                                    ps[:, 3 * i + 2 - 2 * odd, :].rearrange("p (h n) -> p h n", h=H)[:, odd::2],
                                                    bc(m.negd[:, t * H + odd:(t + 1) * H:2], P), ALU.mult).then_inc(s.a, 1)
                    for j in range(LEVELS - 1):
                        for i in range(2):
                            dve.wait_ge(s.x_ps, pair * 2 * (LEVELS - 1) + 2 * j + i + 1)
                            nc.vector.tensor_copy(X[:, i, :], ps[:, 3 * i, :]).then_inc(x_out[i], 1)

            @block.scalar
            def _(act):
                for pair in range(T // 2):
                    for i in range(2):
                        act.wait_ge(s.at_ps, 2 * pair + i + 1)
                        if pair:
                            act.wait_ge(masked[i], LEVELS * pair)
                        nc.scalar.activation(AT[:, i, :], ps[:, 3 * i + 2, :], ACT.Copy).then_inc(s.at, 1)
                    for j in range(LEVELS):
                        for i in range(2):
                            t = 2 * pair + i
                            act.wait_ge(s.xt_ps, pair * 2 * LEVELS + 2 * j + i + 1)
                            dst = TT[:, t, :] if j == LEVELS - 1 else XT[:, i, :]
                            nc.scalar.activation(dst, ps[:, 3 * i + 1, :], ACT.Copy).then_inc(xt_out[i], 1)
                        if j < LEVELS - 1:
                            for i in range(2):
                                act.wait_ge(s.y, pair * 2 * (LEVELS - 1) + 2 * j + i + 1)
                                nc.scalar.activation(Z[:, i, :], ps[:, 3 * i + 2, :], ACT.Copy)\
                                    .then_inc(z_out[i], 1)

            @block.gpsimd
            def _(pool):
                for pair in range(T // 2):
                    for i in range(2):
                        pool.wait_ge(s.at, 2 * pair + i + 1)
                    for j in range(LEVELS):
                        for i in range(2):
                            if pair or j >= KEPT:
                                old = j - KEPT if j >= KEPT else j - KEPT + LEVELS
                                q = pair if j >= KEPT else pair - 1
                                if old:
                                    pool.wait_ge(s.y, q * 2 * (LEVELS - 1) + 2 * (old - 1) + i + 1)
                                else:
                                    pool.wait_ge(s.xt_ps, q * 2 * LEVELS + i + 1)
                            nc.gpsimd.tensor_tensor(AjT[:, i, (LEVELS * pair + j) % KEPT, :].rearrange("p (h n) -> p h n", h=H),
                                                    AT[:, i, :].rearrange("p (h n) -> p h n", h=H),
                                                    k.maskT[:, j, :].unsqueeze(1).to_broadcast([P, H, P]), ALU.mult)\
                                .then_inc(masked[i], 1)
    clear(nc, s)


def recurrence(nc, k, m, TT, ps, s):
    with ExitStack() as tmp:
        S = tmp.enter_context(nc.sbuf_tensor("re_s", [P, HALVES, P], F32))
        r = tmp.enter_context(nc.sbuf_tensor("re_r", [P, 2, D], F32))
        u = tmp.enter_context(nc.sbuf_tensor("re_u", [P, 2, D], F32))
        attnT = tmp.enter_context(nc.sbuf_tensor("re_attn", [P, 2, H * P], F32))
        KS, U, O, ST, KQ = 0, 2, 4, 6, (7, 3)

        with nc.Block() as block:
            @block.gpsimd
            def _(pool):
                nc.gpsimd.memset(S[:], 0.0).then_inc(s.zeroed, 1)

            @block.tensor
            def _(pe):
                pe.wait_ge(s.zeroed, 1)
                for t in range(T):
                    b = t % 2
                    if t:
                        pe.wait_ge(s.attn, 2 * t)
                    for h in range(H):
                        rows = slice(DH * (h % 2), DH * (h % 2) + DH)
                        last = nc.tensor.matmul(ps[:, KQ[h % 2], h * P:(h + 1) * P], m.kT[rows, h // 2, t * P:(t + 1) * P],
                                                m.qT[rows, h // 2, t * P:(t + 1) * P],
                                                start=(h < 2), stop=True, skip_group_check=True)
                    last.then_inc(s.kq, 1)
                    if t:
                        pe.wait_ge(s.state, 2 * t)
                    for a in range(HALVES):
                        last = nc.tensor.matmul(ps[:, KS + b, a * P:(a + 1) * P], m.kT[:, a, t * P:(t + 1) * P], S[:, a, :],
                                                start=(a == 0), stop=True, skip_group_check=True)
                    last.then_inc(s.ks, 1)
                    if t >= 2:
                        pe.wait_ge(s.o_out, t - 1)
                    for a in range(HALVES):
                        nc.tensor.matmul(ps[:, O + b, a * P:(a + 1) * P], m.qT[:, a, t * P:(t + 1) * P], S[:, a, :],
                                         start=(a == 0), stop=False, skip_group_check=True)
                    pe.wait_ge(s.r, t + 1)
                    for h in range(H):
                        last = nc.tensor.matmul(ps[:, U, h * DH:(h + 1) * DH], TT[:, t, h * P:(h + 1) * P],
                                                r[:, b, h * DH:(h + 1) * DH], start=(h == 0), stop=True,
                                                skip_group_check=True)
                    last.then_inc(s.u_ps, 1)
                    pe.wait_ge(s.u, t + 1)
                    if t < T - 1:
                        for a in range(HALVES):
                            last = nc.tensor.matmul(ps[:, ST, a * P:(a + 1) * P], m.k_tm[:, t, a * P:(a + 1) * P],
                                                    u[:, b, a * P:(a + 1) * P], start=(t == 0 and a == 0), stop=False,
                                                    skip_group_check=True)
                        last.then_inc(s.s_ps, 1)
                    pe.wait_ge(s.attn, 2 * (t + 1))
                    for h in range(H):
                        last = nc.tensor.matmul(ps[:, O + b, h * DH:(h + 1) * DH], attnT[:, b, h * P:(h + 1) * P],
                                                u[:, b, h * DH:(h + 1) * DH], start=False, stop=True,
                                                skip_group_check=True)
                    last.then_inc(s.o, 1)

            @block.vector
            def _(dve):
                settle = chain_of(dve, s.dve)
                for t in range(T):
                    b = t % 2
                    dve.wait_ge(s.ks, t + 1)
                    settle(nc.vector.tensor_tensor(r[:, b, :].rearrange("p (h d) -> p h d", h=H),
                                                   ps[:, KS + b, 0:D].rearrange("p (h d) -> p h d", h=H),
                                                   bc(m.negd[:, t * H:(t + 1) * H], DH), ALU.mult))
                    nc.vector.tensor_tensor(r[:, b, :], r[:, b, :], m.ev[:, t, :], ALU.add).then_inc(s.r, 1)
                    dve.wait_ge(s.kq, t + 1)
                    for odd in range(2):
                        nc.vector.tensor_tensor(attnT[:, b, :].rearrange("p (h n) -> p h n", h=H)[:, odd::2],
                                                ps[:, KQ[odd], :].rearrange("p (h n) -> p h n", h=H)[:, odd::2],
                                                k.incl[:].unsqueeze(1).to_broadcast([P, H // 2, P]), ALU.mult)\
                            .then_inc(s.attn, 1)
                    if t < T - 1:
                        dve.wait_ge(s.s_ps, t + 1)
                        nc.vector.tensor_copy(S[0:DH, :, 0:DH], ps[0:DH, ST, 0:D].rearrange("p (a n) -> p a n", a=2)[:, :, 0:DH])\
                            .then_inc(s.state, 1)
                        nc.vector.tensor_copy(S[DH:P, :, DH:P], ps[DH:P, ST, 0:D].rearrange("p (a n) -> p a n", a=2)[:, :, DH:P])\
                            .then_inc(s.state, 1)
                    dve.wait_ge(s.o, t + 1)
                    nc.vector.tensor_tensor(m.delta_tm[:, t, :].rearrange("p (h d) -> p h d", h=H),
                                            ps[:, O + b, 0:D].rearrange("p (h d) -> p h d", h=H),
                                            bc(m.rn[:, 1, t * H:(t + 1) * H], DH), ALU.mult).then_inc(s.o_out, 1)

            @block.scalar
            def _(act):
                for t in range(T):
                    act.wait_ge(s.u_ps, t + 1)
                    nc.scalar.activation(u[:, t % 2, :], ps[:, U, 0:D], ACT.Copy).then_inc(s.u, 1)
    clear(nc, s)


def route(nc, k, m, ps, s):
    with ExitStack() as tmp:
        def sb(name, shape):
            return tmp.enter_context(nc.sbuf_tensor(name, shape, F32))

        cross = sb("ro_cross", [P, 2, T, D])
        square = sb("ro_square", [P, 1, T, D])
        F = sb("ro_f", [P, T, FEATS])
        var = sb("ro_var", [P, T, PATHS * H])
        FT = sb("ro_ft", [FEATS, L])
        h1T = sb("ro_h1", [P, HC, L])
        lg = sb("ro_lg", [P, T * H, PATHS])
        red = sb("ro_red", [P, T * H])
        paths = [m.local_tm, m.mid_tm, m.delta_tm, m.v_tm]
        pairs = [(i, j) for i in range(PATHS) for j in range(i + 1, PATHS)]

        def by_head(ap):
            return ap.rearrange("p t (h d) -> p t h d", h=H)

        def feature(n):
            return F[:, :, n * H:(n + 1) * H]

        with nc.Block() as block:
            @block.gpsimd
            def _(pool):
                for n, (i, j) in enumerate(pairs):
                    if n >= 2:
                        pool.wait_ge(s.crossed, n - 1)
                    nc.gpsimd.tensor_tensor(cross[:, n % 2], paths[i][:], paths[j][:], ALU.mult).then_inc(s.cross, 1)

            @block.scalar
            def _(act):
                for n in range(PATHS):
                    if n >= 1:
                        act.wait_ge(s.squared, n)
                    nc.scalar.activation(square[:, 0].rearrange("p t d -> p (t d)"),
                                         paths[n][:].rearrange("p t d -> p (t d)"), ACT.Square).then_inc(s.square, 1)
                for n in range(NB):
                    act.wait_ge(s.ft_ps, n + 1)
                    nc.scalar.activation(FT[:, n * BANK:(n + 1) * BANK], ps[0:FEATS, n, :], ACT.Copy).then_inc(s.ft, 1)
                for n in range(NB):
                    for c in range(HC):
                        u = n * HC + c
                        rows = P if c < HC - 1 else HLAST
                        act.wait_ge(s.h1_ps, u + 1)
                        nc.scalar.activation(h1T[0:rows, c, n * BANK:(n + 1) * BANK], ps[0:rows, 2 + u % 4, :], ACT.Silu,
                                             bias=k.rb1[0:rows, c:c + 1]).then_inc(s.h1, 1)
                act.wait_ge(s.shifted, 1)
                nc.scalar.activation(lg[:].rearrange("p n c -> p (n c)"), lg[:].rearrange("p n c -> p (n c)"),
                                     ACT.Exp).then_inc(s.exp, 1)

            @block.vector
            def _(dve):
                settle = chain_of(dve, s.dve)
                for n in range(PATHS):
                    nc.vector.tensor_reduce(feature(2 * n), by_head(paths[n][:]), AX.X, ALU.add)
                    dve.wait_ge(s.square, n + 1)
                    nc.vector.tensor_reduce(feature(2 * n + 1), by_head(square[:, 0]), AX.X, ALU.add)\
                        .then_inc(s.squared, 1)
                for n in range(len(pairs)):
                    dve.wait_ge(s.cross, n + 1)
                    nc.vector.tensor_reduce(feature(2 * PATHS + n), by_head(cross[:, n % 2]), AX.X, ALU.add)\
                        .then_inc(s.crossed, 1)
                dve.wait_ge(s.crossed, len(pairs))
                moments = F[:, :, 0:2 * PATHS * H].rearrange("p t (n c h) -> p t n c h", n=PATHS, c=2)
                for n in range(PATHS):
                    last = nc.vector.tensor_tensor(var[:, :, n * H:(n + 1) * H], feature(2 * n), feature(2 * n), ALU.mult)
                settle(last)
                for n in range(PATHS):
                    last = nc.vector.scalar_tensor_tensor(feature(2 * n + 1), var[:, :, n * H:(n + 1) * H], -1.0 / DH,
                                                          feature(2 * n + 1), ALU.mult, ALU.add)
                settle(last)
                for n in range(PATHS):
                    nc.vector.tensor_scalar(feature(2 * n), feature(2 * n), 1.0 / DH, None, ALU.mult)
                    nc.vector.tensor_scalar(feature(2 * n + 1), feature(2 * n + 1), 1.0 / (DH - 1), None, ALU.mult)
                nc.vector.tensor_scalar(F[:, :, 2 * PATHS * H:], F[:, :, 2 * PATHS * H:], 1.0 / DH, None,
                                        ALU.mult).then_inc(s.feats, 1)
                dve.wait_ge(s.logits, 1)
                settle(nc.vector.tensor_tensor(lg[:].rearrange("p (t h) c -> p t (h c)", h=H),
                                               ps[:, 6, 0:T * H * PATHS].rearrange("p (t n) -> p t n", t=T),
                                               k.rb2[:].unsqueeze(1).to_broadcast([P, T, H * PATHS]), ALU.add))
                settle(nc.vector.tensor_reduce(red[:], lg[:], AX.X, ALU.max))
                nc.vector.tensor_tensor(lg[:], lg[:], bc(red[:], PATHS), ALU.subtract).then_inc(s.shifted, 1)
                dve.wait_ge(s.exp, 1)
                settle(nc.vector.tensor_reduce(red[:], lg[:], AX.X, ALU.add))
                settle(nc.vector.reciprocal(red[:], red[:]))
                settle(nc.vector.tensor_tensor(lg[:], lg[:], bc(red[:], PATHS), ALU.mult))
                nc.vector.tensor_scalar(m.prob[:], lg[:], 1.0 - PATHS * FLOOR, FLOOR, ALU.mult, ALU.add)

            @block.tensor
            def _(pe):
                pe.wait_ge(s.feats, 1)
                for n in range(NB):
                    for i in range(BANK // P):
                        last = nc.tensor.transpose(ps[0:FEATS, n, i * P:(i + 1) * P], F[:, n * (BANK // P) + i, :], k.ident[:])
                    last.then_inc(s.ft_ps, 1)
                for n in range(NB):
                    for c in range(HC):
                        u = n * HC + c
                        rows = P if c < HC - 1 else HLAST
                        if u >= 4:
                            pe.wait_ge(s.h1, u - 3)
                        cols = slice(n * BANK, (n + 1) * BANK)
                        out = ps[0:rows, 2 + u % 4, :]
                        hid = slice(c * P, c * P + rows)
                        nc.tensor.matmul(out, k.rw1[:, 0, hid], k.xnT[:, 0, cols], start=True, stop=False)
                        nc.tensor.matmul(out, k.rw1[:, 1, hid], k.xnT[:, 1, cols], start=False, stop=False)
                        pe.wait_ge(s.ft, n + 1)
                        nc.tensor.matmul(out, k.rw1[0:FEATS, 2, hid], FT[:, cols], start=False, stop=True)\
                            .then_inc(s.h1_ps, 1)
                pe.wait_ge(s.h1, NB * HC)
                for t in range(T):
                    for c in range(HC):
                        rows = P if c < HC - 1 else HLAST
                        last = nc.tensor.matmul(ps[:, 6, t * H * PATHS:(t + 1) * H * PATHS], h1T[0:rows, c, t * P:(t + 1) * P],
                                                k.rw2[0:rows, c, :], start=(t == 0 and c == 0), stop=(c == HC - 1),
                                                skip_group_check=True)
                last.then_inc(s.logits, 1)
    clear(nc, s)


def mix_and_project(nc, k, m, ps, s, x):
    with ExitStack() as tmp:
        def sb(name, shape):
            return tmp.enter_context(nc.sbuf_tensor(name, shape, F32))

        part = [sb(f"mi_part{i}", [P, T, D]) for i in range(PATHS)]
        sq = sb("mi_sq", [P, T, D])
        oT = sb("mi_ot", [P, HALVES, L])
        ms = sb("mi_ms", [P, 4, T * H])
        paths = [m.local_tm, m.mid_tm, m.delta_tm, m.v_tm]

        def by_head(ap):
            return ap[:].rearrange("p t (h d) -> p (t h) d", h=H)

        def flat(ap):
            return ap[:].rearrange("p t d -> p (t d)")

        def weight(i):
            return m.prob[:, :, i:i + 1].to_broadcast([P, T * H, DH])

        mixed, weighted = part[0], part[1]
        with nc.Block() as block:
            @block.gpsimd
            def _(pool):
                nc.gpsimd.tensor_tensor(by_head(part[2]), by_head(paths[2]), weight(2), ALU.mult).then_inc(s.part, 1)
                pool.wait_ge(s.mixed, 1)
                nc.gpsimd.tensor_tensor(weighted[:], mixed[:], k.mixw[:].unsqueeze(1).to_broadcast([P, T, D]),
                                        ALU.mult).then_inc(s.weighted, 1)
                pool.wait_ge(s.scale_in, 1)
                nc.gpsimd.tensor_tensor(ms[:, 3, :], ms[:, 2, :], k.mhalf[:, 0:T * H], ALU.pow).then_inc(s.scale, 1)

            @block.vector
            def _(dve):
                settle = chain_of(dve, s.dve)
                nc.vector.tensor_tensor(by_head(part[0]), by_head(paths[0]), weight(0), ALU.mult)
                settle(nc.vector.tensor_tensor(by_head(part[1]), by_head(paths[1]), weight(1), ALU.mult))
                nc.vector.tensor_tensor(part[0][:], part[0][:], part[1][:], ALU.add)
                settle(nc.vector.tensor_tensor(by_head(part[3]), by_head(paths[3]), weight(3), ALU.mult))
                settle(nc.vector.tensor_tensor(part[0][:], part[0][:], part[3][:], ALU.add))
                dve.wait_ge(s.part, 1)
                nc.vector.tensor_tensor(mixed[:], part[0][:], part[2][:], ALU.add).then_inc(s.mixed, 1)
                dve.wait_ge(s.square, 1)
                settle(nc.vector.tensor_reduce(ms[:, 0, :], by_head(sq), AX.X, ALU.add))
                settle(nc.vector.tensor_scalar(ms[:, 0, :], ms[:, 0, :], 1.0 / DH, EPS, ALU.mult, ALU.add))
                nc.vector.reciprocal(ms[:, 2, :], ms[:, 0, :]).then_inc(s.sq_free, 1)
                dve.wait_ge(s.square, 2)
                settle(nc.vector.tensor_reduce(ms[:, 1, :], by_head(sq), AX.X, ALU.add))
                dve.wait_ge(s.sq_free, 1)
                settle(nc.vector.tensor_tensor(ms[:, 1, :], ms[:, 1, :], ms[:, 2, :], ALU.mult))
                settle(nc.vector.tensor_scalar(ms[:, 1, :], ms[:, 1, :], 1.0 / DH, EPS, ALU.mult, ALU.add))
                nc.vector.tensor_tensor(ms[:, 2, :], ms[:, 1, :], ms[:, 0, :], ALU.mult).then_inc(s.scale_in, 1)
                dve.wait_ge(s.scale, 1)
                for u in range(T // 2):
                    rows = slice(2 * u * H, (2 * u + 2) * H)
                    nc.vector.tensor_tensor(by_head(part[2])[:, rows], by_head(weighted)[:, rows], bc(ms[:, 3, rows], DH),
                                            ALU.mult).then_inc(s.normed, 1)
                for n in range(NB):
                    dve.wait_ge(s.turned, HALVES * n + 2)
                    nc.vector.tensor_copy(oT[:, 1, n * BANK:(n + 1) * BANK], ps[:, HALVES * n + 1, :]).then_inc(s.ot1, 1)
                for u in range(T // 2):
                    dve.wait_ge(s.out, u + 1)
                    nc.vector.tensor_tensor(k.x1[:, 2 * u:2 * u + 2, :].rearrange("p t d -> p (t d)"),
                                            x[:, 2 * u:2 * u + 2, :].rearrange("p t d -> p (t d)"), ps[:, 4 + u, :], ALU.add)

            @block.scalar
            def _(act):
                act.wait_ge(s.mixed, 1)
                nc.scalar.activation(flat(sq), flat(mixed), ACT.Square).then_inc(s.square, 1)
                act.wait_ge(s.weighted, 1)
                act.wait_ge(s.sq_free, 1)
                nc.scalar.activation(flat(sq), flat(weighted), ACT.Square).then_inc(s.square, 1)
                for n in range(NB):
                    act.wait_ge(s.turned, HALVES * n + 1)
                    nc.scalar.activation(oT[:, 0, n * BANK:(n + 1) * BANK], ps[:, HALVES * n, :], ACT.Copy).then_inc(s.ot0, 1)

            @block.tensor
            def _(pe):
                for n in range(NB):
                    for a in range(HALVES):
                        for i in range(BANK // P):
                            t = n * (BANK // P) + i
                            pe.wait_ge(s.normed, t // 2 + 1)
                            last = nc.tensor.transpose(ps[:, HALVES * n + a, i * P:(i + 1) * P],
                                                       part[2][:, t, a * P:(a + 1) * P], k.ident[:])
                        last.then_inc(s.turned, 1)
                for t in range(T):
                    n = t // (BANK // P)
                    pe.wait_ge(s.ot0, n + 1)
                    pe.wait_ge(s.ot1, n + 1)
                    for a in range(HALVES):
                        last = nc.tensor.matmul(ps[:, 4 + t // 2, (t % 2) * D:(t % 2 + 1) * D], oT[:, a, t * P:(t + 1) * P],
                                                k.wo[:, a, :], start=(t % 2 == 0 and a == 0), stop=(a == HALVES - 1),
                                                skip_group_check=True)
                    if t % 2:
                        last.then_inc(s.out, 1)
    clear(nc, s)



def slot_ffn(nc, k, ps, s, tag, store=None):
    with ExitStack() as tmp:
        def sb(name, shape):
            return tmp.enter_context(nc.sbuf_tensor(name, shape, F32))

        hT = sb(f"{tag}_ht", [FH, L])
        lg = sb(f"{tag}_lg", [P, T, SLOTS])
        left = sb(f"{tag}_left", [P, T, SLOTS])
        alpha = sb(f"{tag}_alpha", [P, T, SLOTS])
        top = sb(f"{tag}_top", [P, T, TOPK])
        total = sb(f"{tag}_total", [P, T])
        alphaT = sb(f"{tag}_alphat", [SLOTS, L])
        gi = sb(f"{tag}_gi", [SLOTS, D])
        wsum = sb(f"{tag}_wsum", [SLOTS, 1])
        giT = sb(f"{tag}_git", [P, HALVES, SLOTS])
        rz = sb(f"{tag}_rz", [SLOTS, 2 * D])
        new = sb(f"{tag}_new", [SLOTS, D])
        mem = sb(f"{tag}_mem", [SLOTS, D])
        memT = sb(f"{tag}_memt", [P, HALVES, SLOTS])
        values = sb(f"{tag}_values", [SLOTS, D])

        with nc.Block() as block:
            @block.tensor
            def _(pe):
                for n in range(NB):
                    for c in range(HALVES):
                        last = nc.tensor.matmul(ps[:, n, :], k.w1x[:, c, :], k.xnT[:, c, n * BANK:(n + 1) * BANK],
                                                start=(c == 0), stop=(c == HALVES - 1))
                    last.then_inc(s.h_ps, 1)
                for t in range(T):
                    pe.wait_ge(s.h, t // (BANK // P) + 1)
                    last = nc.tensor.matmul(ps[:, 2, t * SLOTS:(t + 1) * SLOTS], hT[:, t * P:(t + 1) * P], k.w2T[:],
                                            start=(t == 0), stop=True, skip_group_check=True)
                last.then_inc(s.logits, 1)
                pe.wait_ge(s.alpha, 1)
                for t in range(T):
                    last = nc.tensor.matmul(ps[0:SLOTS, 3, 0:D + 1], alpha[:, t, :], k.xn[:, t, :],
                                            start=(t == 0), stop=(t == T - 1))
                last.then_inc(s.gathered, 1)
                for n in range(NB):
                    for i in range(BANK // P):
                        last = nc.tensor.transpose(ps[0:SLOTS, 4 + n, i * P:(i + 1) * P],
                                                   alpha[:, n * (BANK // P) + i, :], k.ident[:])
                    last.then_inc(s.at_ps, 1)
                pe.wait_ge(s.gi, 1)
                for a in range(HALVES):
                    last = nc.tensor.transpose(ps[:, 6, a * SLOTS:(a + 1) * SLOTS], gi[:, a * P:(a + 1) * P],
                                               k.ident[0:SLOTS, 0:SLOTS])
                last.then_inc(s.git_ps, 1)
                pe.wait_ge(s.git, 1)
                for a in range(HALVES):
                    last = nc.tensor.matmul(ps[0:SLOTS, 0, :], giT[:, a, :], k.wihT[:, a, 0:2 * D],
                                            start=(a == 0), stop=(a == HALVES - 1))
                last.then_inc(s.gates, 1)
                for a in range(HALVES):
                    last = nc.tensor.matmul(ps[0:SLOTS, 1, 0:D], giT[:, a, :], k.wihT[:, a, 2 * D:],
                                            start=(a == 0), stop=(a == HALVES - 1))
                last.then_inc(s.gates, 1)
                pe.wait_ge(s.mem, 1)
                for a in range(HALVES):
                    last = nc.tensor.transpose(ps[:, 6, a * SLOTS:(a + 1) * SLOTS], mem[:, a * P:(a + 1) * P],
                                               k.ident[0:SLOTS, 0:SLOTS])
                last.then_inc(s.memt_ps, 1)
                pe.wait_ge(s.memt, 1)
                for a in range(HALVES):
                    last = nc.tensor.matmul(ps[0:SLOTS, 7, 0:D], memT[:, a, :], k.wvo[:, a, :],
                                            start=(a == 0), stop=(a == HALVES - 1))
                last.then_inc(s.values_ps, 1)
                pe.wait_ge(s.values, 1)
                for t in range(T):
                    pe.wait_ge(s.alphat, t // (BANK // P) + 1)
                    last = nc.tensor.matmul(ps[:, t // 2, (t % 2) * D:(t % 2 + 1) * D], alphaT[:, t * P:(t + 1) * P],
                                            values[:], start=(t % 2 == 0), stop=True, skip_group_check=True)
                    if t % 2:
                        last.then_inc(s.out, 1)

            @block.scalar
            def _(act):
                for n in range(NB):
                    act.wait_ge(s.h_ps, n + 1)
                    nc.scalar.activation(hT[:, n * BANK:(n + 1) * BANK], ps[:, n, :], ACT.Gelu,
                                         bias=k.hbias[:, 0:1]).then_inc(s.h, 1)
                act.wait_ge(s.shifted, 1)
                nc.scalar.activation(alpha[:].rearrange("p t n -> p (t n)"), alpha[:].rearrange("p t n -> p (t n)"),
                                     ACT.Exp).then_inc(s.exp, 1)
                for n in range(NB):
                    act.wait_ge(s.at_ps, n + 1)
                    nc.scalar.activation(alphaT[:, n * BANK:(n + 1) * BANK], ps[0:SLOTS, 4 + n, :],
                                         ACT.Copy).then_inc(s.alphat, 1)
                act.wait_ge(s.rz_in, 1)
                nc.scalar.activation(rz[:], rz[:], ACT.Tanh, scale=0.5).then_inc(s.rz, 1)
                act.wait_ge(s.n_in, 1)
                nc.scalar.activation(new[:], new[:], ACT.Tanh).then_inc(s.n, 1)

            @block.vector
            def _(dve):
                settle = chain_of(dve, s.dve)
                dve.wait_ge(s.logits, 1)
                settle(nc.vector.tensor_tensor(lg[:], ps[:, 2, :].rearrange("p (t n) -> p t n", t=T),
                                               k.b2[:].unsqueeze(1).to_broadcast([P, T, SLOTS]), ALU.add))
                settle(nc.vector.tensor_scalar(lg[:], lg[:], k.invtau[:, 0:1], None, ALU.mult))
                for t in range(T):
                    last = nc.vector.max(top[:, t, :], lg[:, t, :])
                settle(last)
                nc.vector.tensor_tensor(alpha[:], lg[:], top[:, :, 0:1].to_broadcast([P, T, SLOTS]),
                                        ALU.subtract).then_inc(s.shifted, 1)
                for t in range(T):
                    last = nc.vector.match_replace(left[:, t, :], top[:, t, :], lg[:, t, :], NEG)
                settle(last)
                settle(nc.vector.tensor_tensor(left[:], left[:], lg[:], ALU.not_equal))
                dve.wait_ge(s.exp, 1)
                settle(nc.vector.tensor_tensor(alpha[:], alpha[:], left[:], ALU.mult))
                settle(nc.vector.tensor_reduce(total[:], alpha[:], AX.X, ALU.add))
                settle(nc.vector.reciprocal(total[:], total[:]))
                nc.vector.tensor_tensor(alpha[:], alpha[:], bc(total[:], SLOTS), ALU.mult).then_inc(s.alpha, 1)
                dve.wait_ge(s.gathered, 1)
                settle(nc.vector.tensor_scalar(wsum[:], ps[0:SLOTS, 3, D:D + 1], 1e-8, None, ALU.add))
                settle(nc.vector.reciprocal(wsum[:], wsum[:]))
                nc.vector.tensor_scalar(gi[:], ps[0:SLOTS, 3, 0:D], wsum[:, 0:1], None, ALU.mult).then_inc(s.gi, 1)
                dve.wait_ge(s.git_ps, 1)
                nc.vector.tensor_copy(giT[:].rearrange("p a n -> p (a n)"), ps[:, 6, 0:HALVES * SLOTS]).then_inc(s.git, 1)
                dve.wait_ge(s.gates, 1)
                nc.vector.tensor_tensor(rz[:], ps[0:SLOTS, 0, :], k.grz[:], ALU.add).then_inc(s.rz_in, 1)
                dve.wait_ge(s.rz, 1)
                settle(nc.vector.tensor_scalar(rz[:], rz[:], 0.5, 0.5, ALU.mult, ALU.add))
                settle(nc.vector.tensor_tensor(mem[:], rz[:, 0:D], k.hn[:], ALU.mult))
                settle(nc.vector.tensor_tensor(mem[:], mem[:], k.bihn[:], ALU.add))
                dve.wait_ge(s.gates, 2)
                nc.vector.tensor_tensor(new[:], ps[0:SLOTS, 1, 0:D], mem[:], ALU.add).then_inc(s.n_in, 1)
                dve.wait_ge(s.n, 1)
                settle(nc.vector.tensor_tensor(mem[:], k.hs[:], new[:], ALU.subtract))
                settle(nc.vector.tensor_tensor(mem[:], mem[:], rz[:, D:2 * D], ALU.mult))
                nc.vector.tensor_tensor(mem[:], mem[:], new[:], ALU.add).then_inc(s.mem, 1)
                dve.wait_ge(s.memt_ps, 1)
                nc.vector.tensor_copy(memT[:].rearrange("p a n -> p (a n)"), ps[:, 6, 0:HALVES * SLOTS]).then_inc(s.memt, 1)
                dve.wait_ge(s.values_ps, 1)
                nc.vector.tensor_tensor(values[:], ps[0:SLOTS, 7, 0:D], k.bvo[:], ALU.add).then_inc(s.values, 1)
                for u in range(T // 2):
                    dve.wait_ge(s.out, u + 1)
                    xs = k.x1[:, 2 * u:2 * u + 2, :].rearrange("p t d -> p (t d)")
                    nc.vector.tensor_tensor(xs, xs, ps[:, u, :], ALU.add).then_inc(s.x_out, 1)

            if store is not None:
                @block.sync
                def _(sp):
                    sp.wait_ge(s.x_out, T // 2)
                    sp.dma_start(store, k.x1[:]).then_inc(s.stored, 16)
                    sp.wait_ge(s.stored, 16)
    clear(nc, s)



GH = 4
AG = AH // GH
NBUF = 3
RING = 3
STEPS = [(n, kt) for n in range(NB) for kt in range((n + 1) * (BANK // P))]
PIECES = [(t, j, c) for t in range(T) for j in range(GH) for c in range(-(-(t + 1) * P // BANK))]
PER_STEP = len(PIECES) // len(STEPS)
Q_PARTS = (0, 0, 1, 0, 2, 1)
K_PARTS = (0, 1, 0, 2, 0, 1)
RATIO = float(AD) ** -0.5


def softmax_attention(nc, k, ps, s, stacked):
    with ExitStack() as tmp:
        def sb(name, shape, dt=F32):
            return tmp.enter_context(nc.sbuf_tensor(name, shape, dt))

        qs = sb("sa_qs", [P, NBUF, GH, L], BF16)
        ks = sb("sa_ks", [P, NBUF, GH, L], BF16)
        va = sb("sa_va", [P, T, AH, AD + 1])
        nm = sb("sa_nm", [P, 2, T, GH, 2])
        otm = sb("sa_otm", [P, T, D])
        rec = sb("sa_rec", [P, BANK // P, GH])
        osb = sb("sa_o", [P, BANK])
        mr = sb("sa_mr", [GH, BANK])
        mp = sb("sa_mp", [GH, 2, 3, L], BF16)

        with ExitStack() as early:
            parts = [early.enter_context(nc.sbuf_tensor(f"sa_parts{i}", [P, 3, HALVES, L], BF16)) for i in range(2)]
            pt = early.enter_context(nc.sbuf_tensor("sa_pt", [P, 2, GH, BANK], F32))
            rest = pt[:, 0, 0:2, :]

            pe_use, dve_use = [0], [0]

            def take(pe):
                if pe_use[0] >= RING:
                    pe.wait_ge(s.ring_free, pe_use[0] - RING + 1)
                pe_use[0] += 1
                return ps[:, (pe_use[0] - 1) % RING, :]

            def give(dve):
                dve_use[0] += 1
                dve.wait_ge(s.ring_ready, dve_use[0])
                return ps[:, (dve_use[0] - 1) % RING, :]

            def max_pe(pe, g, first, n):
                if first == 0:
                    pe.wait_ge(stacked[g], 16 * 2 * NCOMB * 2)
                    if g == 0:
                        pe.wait_ge(s.const, 2)
                        pe.wait_ge(s.rest, 2 * HALVES * NB)
                for t, j, c in PIECES[first:first + n]:
                    bank = take(pe)
                    w = min(BANK, (t + 1) * P - c * BANK)
                    diagonal = c == t * P // BANK
                    last = nc.tensor.matmul(bank[:, 0:w], qs[0:NCOMB * AD, g % NBUF, j, t * P:(t + 1) * P],
                                            ks[0:NCOMB * AD, g % NBUF, j, c * BANK:c * BANK + w],
                                            start=True, stop=not diagonal, skip_group_check=True)
                    if diagonal:
                        last = nc.tensor.matmul(bank[:, w - P:w], k.identb[:, 0:P], k.causal[:], start=False,
                                                stop=True, skip_group_check=True)
                    last.then_inc(s.ring_ready, 1)

            def max_dve(dve, g, first, n):
                for t, j, c in PIECES[first:first + n]:
                    bank = give(dve)
                    w = min(BANK, (t + 1) * P - c * BANK)
                    nc.vector.tensor_reduce(nm[:, g % 2, t, j, c:c + 1], bank[:, 0:w], AX.X, ALU.max,
                                            negate=True).then_inc(s.ring_free, 1)

            def turn_max_pe(pe, g):
                pe.wait_ge(s.nm, g + 1)
                for n in range(NB):
                    bank = take(pe)
                    for i in range(BANK // P):
                        last = nc.tensor.transpose(bank[0:GH, i * P:(i + 1) * P],
                                                   nm[:, g % 2, n * (BANK // P) + i, :, 0], k.ident[:])
                    last.then_inc(s.ring_ready, 1)

            def turn_max_dve(dve, settle, g):
                late = nm[:, g % 2, BANK // P:T]
                dve.wait_ge(s.ring_free, dve_use[0])
                nc.vector.tensor_tensor(late[:, :, :, 0], late[:, :, :, 0], late[:, :, :, 1], ALU.min)\
                    .then_inc(s.nm, 1)
                if g >= 2:
                    dve.wait_ge(s.m_rows, 16 * 3 * (g - 1))
                for n in range(NB):
                    bank = give(dve)
                    cols = slice(n * BANK, (n + 1) * BANK)
                    settle(nc.vector.tensor_copy(mp[:, g % 2, 0, cols], bank[0:GH, :]))
                    nc.vector.tensor_tensor(mr[:], bank[0:GH, :], mp[:, g % 2, 0, cols], ALU.subtract)\
                        .then_inc(s.ring_free, 1)
                    dve.wait_ge(s.ring_free, dve_use[0])
                    settle(nc.vector.tensor_copy(mp[:, g % 2, 1, cols], mr[:]))
                    nc.vector.tensor_tensor(mp[:, g % 2, 2, cols], mr[:], mp[:, g % 2, 1, cols], ALU.subtract)\
                        .then_inc(s.m_parts, 1)

            def scores_pe(pe, g, st):
                n, kt = STEPS[st]
                if st == 0:
                    pe.wait_ge(s.m_rows, 16 * 3 * (g + 1))
                    if g == 0:
                        pe.wait_ge(s.v_out, T // 2)
                off = max(0, kt * P - n * BANK)
                unit = (g * len(STEPS) + st) * GH
                for j in range(GH):
                    if unit:
                        pe.wait_ge(s.exp, unit - GH + j + 1)
                    diagonal = kt * P >= n * BANK
                    last = nc.tensor.matmul(ps[:, RING + j, off:BANK], ks[0:QROWS, g % NBUF, j, kt * P:(kt + 1) * P],
                                            qs[0:QROWS, g % NBUF, j, n * BANK + off:(n + 1) * BANK],
                                            start=True, stop=not diagonal, skip_group_check=True)
                    if diagonal:
                        last = nc.tensor.matmul(ps[:, RING + j, off:off + P], k.identb[:, 0:P], k.causalT[:],
                                                start=False, stop=True, skip_group_check=True)
                    last.then_inc(s.scores, 1)

            def sums_pe(pe, g, st):
                n, kt = STEPS[st]
                off = max(0, kt * P - n * BANK)
                if kt == 0 and g * NB + n:
                    pe.wait_ge(s.o_out, g * NB + n)
                pe.wait_ge(s.exp, (g * len(STEPS) + st + 1) * GH)
                for j in range(GH):
                    head = (j % 2) * (AH // 2) + 2 * g + j // 2
                    last = nc.tensor.matmul(ps[2 * AD * j:2 * AD * j + AD + 1, 7, off:BANK], va[:, kt, head, :],
                                            pt[:, st % 2, j, off:BANK], start=(kt == 0),
                                            stop=(kt == (n + 1) * (BANK // P) - 1), skip_group_check=True)
                last.then_inc(s.sums, 1)

            def turn_sums_pe(pe, g, n):
                pe.wait_ge(s.o_out, g * NB + n + 1)
                bank = take(pe)
                for i in range(BANK // P):
                    last = nc.tensor.transpose(bank[:, i * P:(i + 1) * P], osb[:, i * P:(i + 1) * P], k.ident[:])
                last.then_inc(s.ring_ready, 1)

            def sums_dve(dve, g, n):
                dve.wait_ge(s.sums, g * len(STEPS) + (n + 1) * (BANK // P) + n * (BANK // P))
                nc.vector.tensor_copy(osb[:], ps[:, 7, :]).then_inc(s.o_out, 1)

            def turn_sums_dve(dve, settle, g, n):
                bank = give(dve).rearrange("p (i j c) -> p i j c", i=BANK // P, j=GH)
                settle(nc.vector.reciprocal(rec[:], bank[:, :, :, AD]))
                view = otm[:].rearrange("p t (a h d) -> p t a h d", a=HALVES, h=AH // 2)
                for hl in range(2):
                    last = nc.vector.tensor_tensor(view[:, n * (BANK // P):(n + 1) * (BANK // P), :, 2 * g + hl, :],
                                                   bank[:, :, 2 * hl:2 * hl + 2, 0:AD],
                                                   bc(rec[:, :, 2 * hl:2 * hl + 2], AD), ALU.mult)
                last.then_inc(s.ring_free, 1)

            with nc.Block() as block:
                @block.gpsimd
                def _(pool):
                    nc.gpsimd.memset(va[:, :, :, AD:AD + 1], 1.0).then_inc(s.const, 1)
                    pool.wait_ge(s.const, 1)
                    nc.gpsimd.memset(ks[NCOMB * AD:QROWS], 1.0).then_inc(s.const, 1)
                    pool.wait_ge(s.const, 2)
                    for u in range(2 * HALVES * NB):
                        i, a, n = u // (HALVES * NB), u // NB % HALVES, u % NB
                        cols = slice(n * BANK, (n + 1) * BANK)
                        pool.wait_ge(s.second, u + 1)
                        nc.gpsimd.tensor_tensor(parts[i][:, 2, a, cols], rest[:, u % 2, :], parts[i][:, 1, a, cols],
                                                ALU.subtract).then_inc(s.third, 1)

                @block.tensor
                def _(pe):
                    for u in range(2 * HALVES * NB):
                        i, a, n = u // (HALVES * NB), u // NB % HALVES, u % NB
                        if u >= 4:
                            pe.wait_ge(s.rest, u - 3)
                        for c in range(HALVES):
                            last = nc.tensor.matmul(ps[:, u % 4, :], k.wqkvT[:, c, i * D + a * P:i * D + (a + 1) * P],
                                                    k.xnT[:, c, n * BANK:(n + 1) * BANK],
                                                    start=(c == 0), stop=(c == HALVES - 1))
                        last.then_inc(s.qk_ps, 1)
                    for t in range(T):
                        for c in range(HALVES):
                            last = nc.tensor.matmul(ps[:, 4 + t // 2, (t % 2) * D:(t % 2 + 1) * D],
                                                    k.xnT[:, c, t * P:(t + 1) * P], k.wqkvT[:, c, 2 * D:3 * D],
                                                    start=(t % 2 == 0 and c == 0), stop=(c == HALVES - 1),
                                                    skip_group_check=True)
                        if t % 2:
                            last.then_inc(s.v_ps, 1)
                    max_pe(pe, 0, 0, len(PIECES))
                    turn_max_pe(pe, 0)
                    for g in range(AG):
                        for st in range(len(STEPS)):
                            scores_pe(pe, g, st)
                            if st:
                                sums_pe(pe, g, st - 1)
                            if g + 1 < AG:
                                max_pe(pe, g + 1, st * PER_STEP, PER_STEP)
                            if g and st == 1:
                                turn_sums_pe(pe, g - 1, 1)
                            if st == BANK // P + 1:
                                turn_sums_pe(pe, g, 0)
                        sums_pe(pe, g, len(STEPS) - 1)
                        if g + 1 < AG:
                            turn_max_pe(pe, g + 1)
                    turn_sums_pe(pe, AG - 1, 1)

                @block.scalar
                def _(act):
                    for u in range(2 * HALVES * NB):
                        i, a, n = u // (HALVES * NB), u // NB % HALVES, u % NB
                        cols = slice(n * BANK, (n + 1) * BANK)
                        act.wait_ge(s.qk_ps, u + 1)
                        nc.scalar.activation(parts[i][:, 0, a, cols], ps[:, u % 4, :], ACT.Copy).then_inc(s.first, 1)
                        act.wait_ge(s.rest, u + 1)
                        nc.scalar.activation(parts[i][:, 1, a, cols], rest[:, u % 2, :], ACT.Copy).then_inc(s.second, 1)
                    for u in range(T // 2):
                        act.wait_ge(s.v_ps, u + 1)
                        nc.scalar.activation(va[:, 2 * u:2 * u + 2, :, 0:AD],
                                             ps[:, 4 + u, :].rearrange("p (t h d) -> p t h d", t=2, h=AH),
                                             ACT.Copy).then_inc(s.v_out, 1)
                    act.wait_ge(s.third, 2 * HALVES * NB)
                    for g in range(AG):
                        for st, (n, kt) in enumerate(STEPS):
                            off = max(0, kt * P - n * BANK)
                            gs = g * len(STEPS) + st
                            if gs >= 2:
                                act.wait_ge(s.sums, gs - 1)
                            for j in range(GH):
                                act.wait_ge(s.scores, gs * GH + j + 1)
                                nc.scalar.activation(pt[:, st % 2, j, off:BANK], ps[:, RING + j, off:BANK], ACT.Exp,
                                                     scale=RATIO).then_inc(s.exp, 1)

                @block.vector
                def _(dve):
                    settle = chain_of(dve, s.dve)
                    for u in range(2 * HALVES * NB):
                        i, a, n = u // (HALVES * NB), u // NB % HALVES, u % NB
                        dve.wait_ge(s.first, u + 1)
                        if u >= 2:
                            dve.wait_ge(s.third, u - 1)
                        nc.vector.tensor_tensor(rest[:, u % 2, :], ps[:, u % 4, :],
                                                parts[i][:, 0, a, n * BANK:(n + 1) * BANK], ALU.subtract).then_inc(s.rest, 1)
                    max_dve(dve, 0, 0, len(PIECES))
                    turn_max_dve(dve, settle, 0)
                    for g in range(AG):
                        for st in range(len(STEPS)):
                            if g and st == 0:
                                sums_dve(dve, g - 1, 1)
                            if st == BANK // P:
                                sums_dve(dve, g, 0)
                            if g + 1 < AG:
                                max_dve(dve, g + 1, st * PER_STEP, PER_STEP)
                            if g and st == 1:
                                turn_sums_dve(dve, settle, g - 1, 1)
                            if st == BANK // P + 1:
                                turn_sums_dve(dve, settle, g, 0)
                        if g + 1 < AG:
                            turn_max_dve(dve, settle, g + 1)
                    sums_dve(dve, AG - 1, 1)
                    turn_sums_dve(dve, settle, AG - 1, 1)

                @block.sync
                def _(sp):
                    def stack(g):
                        if g >= NBUF:
                            sp.wait_ge(s.scores, (g - NBUF + 1) * len(STEPS) * GH)
                        for dst, src, order in ((qs, parts[0], Q_PARTS), (ks, parts[1], K_PARTS)):
                            for c in range(NCOMB):
                                for hl in range(2):
                                    sp.dma_start(dst[AD * c:AD * (c + 1), g % NBUF, 2 * hl:2 * hl + 2, :],
                                                 src[AD * (2 * g + hl):AD * (2 * g + hl + 1), order[c], :, :])\
                                        .then_inc(stacked[g], 16)

                    def rows(g):
                        sp.wait_ge(s.m_parts, NB * (g + 1))
                        for c in range(3):
                            sp.dma_start(qs[NCOMB * AD + c:NCOMB * AD + c + 1, g % NBUF, :, :],
                                         mp[:, g % 2, c, :]).then_inc(s.m_rows, 16)

                    sp.wait_ge(s.third, 2 * HALVES * NB)
                    for g in range(NBUF):
                        stack(g)
                    rows(0)
                    rows(1)
                    for g in range(NBUF, AG):
                        stack(g)
                    for g in range(2, AG):
                        rows(g)

        oT = sb("sa_ot", [P, HALVES, L])
        with nc.Block() as block:
            @block.tensor
            def _(pe):
                for n in range(NB):
                    for a in range(HALVES):
                        for i in range(BANK // P):
                            last = nc.tensor.transpose(ps[:, HALVES * n + a, i * P:(i + 1) * P],
                                                       otm[:, n * (BANK // P) + i, a * P:(a + 1) * P], k.ident[:])
                        last.then_inc(s.turned, 1)
                for t in range(T):
                    n = t // (BANK // P)
                    pe.wait_ge(s.ot0, n + 1)
                    pe.wait_ge(s.ot1, n + 1)
                    for a in range(HALVES):
                        last = nc.tensor.matmul(ps[:, 4 + t // 2, (t % 2) * D:(t % 2 + 1) * D], oT[:, a, t * P:(t + 1) * P],
                                                k.woutT[:, a, :], start=(t % 2 == 0 and a == 0), stop=(a == HALVES - 1),
                                                skip_group_check=True)
                    if t % 2:
                        last.then_inc(s.out, 1)

            @block.scalar
            def _(act):
                for n in range(NB):
                    act.wait_ge(s.turned, HALVES * n + 1)
                    nc.scalar.activation(oT[:, 0, n * BANK:(n + 1) * BANK], ps[:, HALVES * n, :], ACT.Copy).then_inc(s.ot0, 1)

            @block.vector
            def _(dve):
                for n in range(NB):
                    dve.wait_ge(s.turned, HALVES * n + 2)
                    nc.vector.tensor_copy(oT[:, 1, n * BANK:(n + 1) * BANK], ps[:, HALVES * n + 1, :]).then_inc(s.ot1, 1)
                for u in range(T // 2):
                    dve.wait_ge(s.out, u + 1)
                    xs = k.x1[:, 2 * u:2 * u + 2, :].rearrange("p t d -> p (t d)")
                    nc.vector.tensor_tensor(xs, xs, ps[:, 4 + u, :], ALU.add)
        nc.sync.sem_clear(range(stacked[0].num, stacked[-1].num + 1))
        clear(nc, s)



LN_SEMS = "x_in dve var rstd xn turned"
SEMS = {
    "ln": LN_SEMS,
    "su": "loaded all_in const dve prepared hs pe back",
    "pc": "padded proj pre conv silu beta tanh turned tm squared sums ss rnorm dve",
    "lc": "padded rep conv evac turned tm",
    "ib": "gram a at_ps at x_ps xt_ps y x_even x_odd xt_even xt_odd z_even z_odd m_even m_odd",
    "re": "zeroed kq attn ks r u_ps u s_ps state o o_out dve",
    "ro": "cross crossed square squared feats ft_ps ft h1_ps h1 logits shifted exp dve",
    "mi": "part mixed weighted scale_in scale square sq_free normed turned ot0 ot1 out dve",
    "ff": "h_ps h logits shifted exp alpha gathered at_ps alphat gi git_ps git gates rz_in rz n_in n mem memt_ps memt "
          "values_ps values out x_out stored dve",
    "sa": "const first second third rest qk_ps v_ps v_out ring_ready ring_free nm m_parts m_rows scores exp sums o_out "
          "turned ot0 ot1 out dve",
}


def build(nc, w, y):
    with ExitStack() as ctx:
        def sb(name, shape, dt=F32):
            return ctx.enter_context(nc.sbuf_tensor(name, shape, dt))

        ps = ctx.enter_context(nc.psum_tensor("ps", [P, 8, BANK], F32))
        k = named(
            "Constants",
            wq=sb("wq", [P, HALVES, D]), wk=sb("wk", [P, HALVES, D]), wv=sb("wv", [P, HALVES, D]),
            wb=sb("wb", [P, HALVES, H]), cw=sb("cw", [P, 3, HALVES, 4]),
            stack=sb("stack", [P, (MID_STEPS + LOCAL_STEPS) * GROUPS, CG]),
            wo=sb("wo", [P, HALVES, D]), mixw=sb("mixw", [P, D]),
            rw1=sb("rw1", [P, 3, HID]), rb1=sb("rb1", [P, HC]), rw2=sb("rw2", [P, HC, H * PATHS]),
            rb2=sb("rb2", [P, H * PATHS]),
            ident=sb("ident", [P, P]), identb=sb("identb", [P, 4 * P], BF16),
            maskT=sb("maskT", [P, LEVELS, P]), incl=sb("incl", [P, P]),
            causal=sb("causal", [P, P], BF16), causalT=sb("causalT", [P, P], BF16), ones2=sb("ones2", [P, 2]),
            invtau=sb("invtau", [P, 1]), w1x=sb("w1x", [P, HALVES, FH]), w2T=sb("w2T", [FH, SLOTS]),
            b2=sb("b2", [P, SLOTS]), wihT=sb("wihT", [P, HALVES, 3 * D]), hs=sb("hs", [SLOTS, D]),
            hbias=sb("hbias", [FH, 1]), grz=sb("grz", [SLOTS, 2 * D]), hn=sb("hn", [SLOTS, D]),
            bihn=sb("bihn", [SLOTS, D]), wvo=sb("wvo", [P, HALVES, D]), bvo=sb("bvo", [SLOTS, D]),
            wqkvT=sb("wqkvT", [P, HALVES, 3 * D]), woutT=sb("woutT", [P, HALVES, D]),
            mhalf=sb("mhalf", [P, 2 * T * H]),
            x1=sb("x1", [P, T, D]), xn=sb("xn", [P, T, D + 1]), xnT=sb("xnT", [P, HALVES, L]),
            stats=sb("stats", [P, T, 6]), mv=sb("mv", [P, T, 2]), vare=sb("vare", [P, T]), rstd=sb("rstd", [P, T]),
        )
        s = {n: sems(nc, ctx, n, names) for n, names in SEMS.items()}
        stacked = [ctx.enter_context(nc.semaphore(f"sa_stacked{g}")) for g in range(AG)]
        x_view = w["x"].rearrange("b (t p) d -> b p t d", p=P)
        y_view = y.rearrange("b (t p) d -> b p t d", p=P)
        setup(nc, w, k, ps, s["su"])
        with nc.Fori(0, SEQS) as b:
            with ExitStack() as first:
                def sf(name, shape):
                    return first.enter_context(nc.sbuf_tensor(name, shape, F32))

                x0 = sf("x0", [P, T, D])
                m = named(
                    "DeltaTensors",
                    kT=sf("kT", [P, HALVES, L]), qT=sf("qT", [P, HALVES, L]),
                    v_tm=sf("v_tm", [P, T, D]), k_tm=sf("k_tm", [P, T, D]), ev=sf("ev", [P, T, D]),
                    beta=sf("beta", [P, T * H]), ss=sf("ss", [P, 2, T * H]), ss2=sf("ss2", [P, 2, T * H]),
                    rn=sf("rn", [P, 2, T * H]), negd=sf("negd", [P, T * H]), e=sf("e", [P, T * H]),
                    prob=sf("prob", [P, T * H, PATHS]),
                    local_tm=sf("local_tm", [P, T, D]), mid_tm=sf("mid_tm", [P, T, D]),
                    delta_tm=sf("delta_tm", [P, T, D]))
                layer_norm(nc, k, ps, s["ln"], x0, load=x_view[b])
                with nc.sbuf_tensor("vT", [P, HALVES, L], F32) as vT:
                    with nc.sbuf_tensor("sq", [P, 2, HALVES, L], F32) as sq:
                        project_and_convolve(nc, k, m, vT, sq, ps, s["pc"])
                    long_convolutions(nc, k, m, vT, ps, s["lc"])
                with nc.sbuf_tensor("TT", [P, T, H * P], F32) as TT:
                    invert_blocks(nc, k, m, TT, ps, s["ib"])
                    recurrence(nc, k, m, TT, ps, s["re"])
                route(nc, k, m, ps, s["ro"])
                mix_and_project(nc, k, m, ps, s["mi"], x0)
            layer_norm(nc, k, ps, s["ln"], k.x1)
            slot_ffn(nc, k, ps, s["ff"], "ffa")
            layer_norm(nc, k, ps, s["ln"], k.x1)
            softmax_attention(nc, k, ps, s["sa"], stacked)
            layer_norm(nc, k, ps, s["ln"], k.x1)
            slot_ffn(nc, k, ps, s["ff"], "ffb", store=y_view[b])


def laid_out(inputs):
    def a(name):
        return np.asarray(inputs[name])

    def lags(w, taps, steps):
        padded = np.zeros((D, SHIFTS * steps), w.dtype)
        padded[:, :taps] = w[:, ::-1]
        return padded.reshape(GROUPS, CG, steps, SHIFTS).transpose(3, 1, 2, 0).reshape(P, steps * GROUPS)

    def rows(v, n):
        return np.broadcast_to(v.reshape(1, -1), (n, v.size))

    i, j = np.arange(P)[:, None], np.arange(P)[None, :]
    mask_t = np.stack([((j >> l) == (i >> l) + 1) & ((j >> (l + 1)) == (i >> (l + 1))) for l in range(LEVELS)], 1)
    own, ffn = "L0_attn_a_", "L0_ffn_"
    out = {
        "x": a(own + "hidden_states"), "Wq": a(own + "Wq"), "Wk": a(own + "Wk"), "Wv": a(own + "Wv"), "Wb": a(own + "Wb"),
        "cw": np.stack([a(own + f"conv_{n}_w") for n in "qkv"]),
        "taps": np.concatenate([lags(a(own + "mid_w"), MID, MID_STEPS), lags(a(own + "local_w"), LOCAL, LOCAL_STEPS)], 1),
        "eye32": np.tile(np.eye(CG, dtype=np.float32), (SHIFTS, 1)),
        "Wo": a(own + "Wo"), "onorm": np.tile(a(own + "onorm_w"), P // DH)[:, None],
        "mixw": rows(a(own + "mix_w"), P),
        "rw1": a(own + "r_w1"), "rb1": a(own + "r_b1"), "rw2": a(own + "r_w2"), "rb2": rows(a(own + "r_b2"), P),
        "ident": np.eye(P, dtype=np.float32),
        "identb": np.tile(np.eye(P, dtype=np.float32), (1, 4)),
        "maskT": mask_t.astype(np.float32), "incl": (j >= i).astype(np.float32),
        "causal": np.where(j > i, NEG, 0.0).astype(np.float32),
        "causalT": np.where(i > j, NEG, 0.0).astype(np.float32),
        "ones2": ((i // DH) == j[:, 0:2]).astype(np.float32),
        "tau": rows(a(ffn + "tau"), P), "slot_init": a(ffn + "slot_init"), "slot_scale": a(ffn + "slot_scale"),
        "w1T": a(ffn + "w1").T, "b1": a(ffn + "b1")[:, None], "w2T": a(ffn + "w2").T, "b2": rows(a(ffn + "b2"), P),
        "wihT": a(ffn + "gru_wih").T, "whhT": a(ffn + "gru_whh").T,
        "bih": rows(a(ffn + "gru_bih"), SLOTS), "bhh": rows(a(ffn + "gru_bhh"), SLOTS),
        "wv": a(ffn + "wv"), "woT": a(ffn + "wo").T,
        "bvb": np.broadcast_to(a(ffn + "bv")[:, None], (D, SLOTS)), "bo": rows(a(ffn + "bo"), SLOTS),
        "wqkvT": a("L0_attn_b_w_qkv").T, "woutT": a("L0_attn_b_w_out").T,
    }
    return {n: np.ascontiguousarray(v) for n, v in out.items()}


def kernel(**inputs):
    import concourse.bacc as bacc
    from concourse.bass_utils import run_bass_kernel_spmd

    nc = bacc.Bacc("TRN2", target_bir_lowering=False, num_devices=1)
    arrays = {f"in_{n}": v for n, v in laid_out(inputs).items()}
    w = {n[3:]: nc.dram_tensor(n, v.shape, mybir.dt.from_np(v.dtype), kind="ExternalInput").ap() for n, v in arrays.items()}
    y = nc.dram_tensor("out_y", (SEQS, L, D), F32, kind="ExternalOutput").ap()
    build(nc, w, y)
    r = run_bass_kernel_spmd(nc, [arrays], core_ids=[0])
    return r.results[0]["out_y"]
```

```python
from collections import namedtuple
from contextlib import ExitStack

import numpy as np

import concourse.bass as bass
from concourse import mybir

ALU = mybir.AluOpType
ACT = mybir.ActivationFunctionType
AX = mybir.AxisListType
F32 = mybir.dt.float32
BF16 = mybir.dt.bfloat16

P = 128
SEQS, L, D = 16, 1024, 256
T = L // P
HALVES = D // P
BANK = 512
NB = L // BANK
H, DH = 4, 64
MID, LOCAL = 25, 7
SHIFTS, CG = 4, 32
GROUPS = D // CG
MID_STEPS, LOCAL_STEPS = -(-MID // SHIFTS), -(-LOCAL // SHIFTS)
PAD = SHIFTS * (MID_STEPS - 1)
PATHS = 4
FEATS = 14 * H
HID = 2 * (D + FEATS)
HC = -(-HID // P)
HLAST = HID - (HC - 1) * P
FLOOR = 0.01
EPS = 1e-5
SLOTS, FH, TOPK = 64, 128, 8
AH, AD = 16, 16
NCOMB = 6
QROWS = NCOMB * AD + 3
NEG = -1.0e30
CHUNK = 32
BLOCKS = P // CHUNK


def chain_of(eng, sem):
    count = [0]

    def settle(ins):
        count[0] += 1
        ins.then_inc(sem, 1)
        eng.wait_ge(sem, count[0])

    return settle


def bc(ap, n):
    return ap.unsqueeze(len(ap.shape)).to_broadcast(list(ap.shape) + [n])


def named(kind, **things):
    return namedtuple(kind, things)(**things)


def by_blocks(ap, n):
    return ap[:].rearrange("p t (h n) -> p (t h) n", n=n)


def sems(nc, ctx, prefix, names):
    return named("Semaphores", **{n: ctx.enter_context(nc.semaphore(f"{prefix}_{n}")) for n in names.split()})


def clear(nc, s):
    nums = [x.num for x in s]
    nc.sync.sem_clear(range(min(nums), max(nums) + 1))
    nc.all_engine_barrier()



def setup(nc, w, k, ps, s):
    with ExitStack() as tmp:
        def sb(name, shape, dt=F32):
            return tmp.enter_context(nc.sbuf_tensor(name, shape, dt))

        taps = sb("su_taps", [P, (MID_STEPS + LOCAL_STEPS) * GROUPS])
        eye32 = sb("su_eye32", [P, CG])
        wo_raw = sb("su_wo", [P, HALVES, D])
        onorm = sb("su_onorm", [P, 1])
        tau = sb("su_tau", [P, 3])
        b_raw = sb("su_b_raw", [P, 6 * P])
        slot_init = sb("su_slot", [SLOTS, D])
        slot_scale = sb("su_scale", [SLOTS, 1])
        w1s = sb("su_w1s", [P, HALVES, FH])
        b1 = sb("su_b1", [FH, 1])
        mean64 = sb("su_mean", [SLOTS, 1])
        slot_mean = sb("su_smean", [P, HALVES])
        hsT = sb("su_hsT", [P, HALVES, SLOTS])
        whhT = sb("su_whhT", [P, HALVES, 3 * D])
        bih = sb("su_bih", [SLOTS, 3 * D])
        bhh = sb("su_bhh", [SLOTS, 3 * D])
        wv = sb("su_wv", [P, HALVES, D])
        woT = sb("su_woT", [P, HALVES, D])
        bvb = sb("su_bvb", [P, HALVES, SLOTS])
        bo = sb("su_bo", [SLOTS, D])

        with nc.Block() as block:
            @block.sync
            def _(sp):
                loads = [
                    (k.wq, w["Wq"].rearrange("(k p) n -> p k n", p=P)),
                    (k.wk, w["Wk"].rearrange("(k p) n -> p k n", p=P)),
                    (k.wv, w["Wv"].rearrange("(k p) n -> p k n", p=P)),
                    (k.wb, w["Wb"].rearrange("(k p) n -> p k n", p=P)),
                    (k.cw, w["cw"].rearrange("s (a p) t -> p s a t", p=P)),
                    (taps, w["taps"]), (eye32, w["eye32"]),
                    (wo_raw, w["Wo"].rearrange("(k p) n -> p k n", p=P)),
                    (onorm, w["onorm"]), (k.mixw, w["mixw"]),
                    (k.rw1[:, 0:2, :], w["rw1"][0:D].rearrange("(k p) n -> p k n", p=P)),
                    (k.rw1[0:FEATS, 2, :], w["rw1"][D:D + FEATS]),
                    (k.rb1[:, 0:HC - 1], w["rb1"][0:(HC - 1) * P].rearrange("(k p) -> p k", p=P)),
                    (k.rb1[0:HLAST, HC - 1:HC], w["rb1"][(HC - 1) * P:HID].rearrange("(p k) -> p k", k=1)),
                    (k.rw2[:, 0:HC - 1, :], w["rw2"][0:(HC - 1) * P].rearrange("(k p) n -> p k n", p=P)),
                    (k.rw2[0:HLAST, HC - 1, :], w["rw2"][(HC - 1) * P:HID]),
                    (k.rb2, w["rb2"]),
                    (k.ident, w["ident"]), (b_raw[:, 0:4 * P], w["identb"]),
                    (k.incl, w["incl"]),
                    (b_raw[:, 4 * P:5 * P], w["causal"]), (b_raw[:, 5 * P:], w["causalT"]),
                    (k.ones2, w["ones2"]),
                    (tau[:, 0:1], w["tau"]), (slot_init, w["slot_init"]), (slot_scale, w["slot_scale"]),
                    (k.w1x, w["w1T"][0:D].rearrange("(k p) n -> p k n", p=P)),
                    (w1s, w["w1T"][D:2 * D].rearrange("(k p) n -> p k n", p=P)),
                    (b1, w["b1"]), (k.w2T, w["w2T"]), (k.b2, w["b2"]),
                    (k.wihT, w["wihT"].rearrange("(k p) n -> p k n", p=P)),
                    (whhT, w["whhT"].rearrange("(k p) n -> p k n", p=P)),
                    (bih, w["bih"]), (bhh, w["bhh"]),
                    (wv, w["wv"].rearrange("(k p) n -> p k n", p=P)),
                    (woT, w["woT"].rearrange("(k p) n -> p k n", p=P)),
                    (bvb, w["bvb"].rearrange("(k p) n -> p k n", p=P)), (bo, w["bo"]),
                    (k.wqkvT, w["wqkvT"].rearrange("(k p) n -> p k n", p=P)),
                    (k.woutT, w["woutT"].rearrange("(k p) n -> p k n", p=P)),
                ]
                for dst, src in loads:
                    dst = dst if isinstance(dst, bass.AP) else dst[:]
                    sp.dma_start(dst, src, allow_slow_non_contiguous=True).then_inc(s.loaded, 16)
                sp.wait_ge(s.loaded, 16 * len(loads))
                sp.sem_inc(s.all_in, 1)

            @block.gpsimd
            def _(pool):
                nc.gpsimd.memset(mean64[:], 1.0 / SLOTS).then_inc(s.const, 1)
                nc.gpsimd.memset(k.mhalf[:], -0.5).then_inc(s.const, 1)
                nc.gpsimd.memset(k.xn[:, :, D:D + 1], 1.0).then_inc(s.const, 1)

            @block.vector
            def _(dve):
                settle = chain_of(dve, s.dve)
                dve.wait_ge(s.all_in, 1)
                nc.vector.tensor_tensor(k.stack[:].rearrange("p n c -> p n c"), bc(taps[:], CG),
                                        eye32[:].unsqueeze(1).to_broadcast([P, (MID_STEPS + LOCAL_STEPS) * GROUPS, CG]),
                                        ALU.mult).then_inc(s.prepared, 1)
                for a in range(HALVES):
                    nc.vector.tensor_scalar(k.wo[:, a, :], wo_raw[:, a, :], onorm[:, 0:1], None,
                                            ALU.mult).then_inc(s.prepared, 1)
                nc.vector.tensor_copy(k.identb[:], b_raw[:, 0:4 * P]).then_inc(s.prepared, 1)
                nc.vector.tensor_copy(k.causal[:], b_raw[:, 4 * P:5 * P]).then_inc(s.prepared, 1)
                nc.vector.tensor_copy(k.causalT[:], b_raw[:, 5 * P:]).then_inc(s.prepared, 1)
                settle(nc.vector.tensor_scalar(tau[:, 1:2], tau[:, 0:1], -1.0, None, ALU.mult))
                settle(nc.vector.tensor_tensor(tau[:, 2:3], tau[:, 0:1], tau[:, 1:2], ALU.max))
                settle(nc.vector.tensor_scalar(tau[:, 1:2], tau[:, 2:3], 0.1, None, ALU.add))
                settle(nc.vector.reciprocal(k.invtau[:], tau[:, 1:2]))
                nc.vector.tensor_scalar(k.hs[:], slot_init[:], slot_scale[:, 0:1], None, ALU.mult).then_inc(s.hs, 1)
                nc.vector.tensor_tensor(k.bihn[:], bih[:, 2 * D:], bih[:, 2 * D:], ALU.max).then_inc(s.prepared, 1)
                dve.wait_ge(s.pe, 1)
                nc.vector.tensor_copy(slot_mean[:], ps[:, 0, 0:HALVES]).then_inc(s.back, 1)
                dve.wait_ge(s.pe, 2)
                nc.vector.tensor_copy(hsT[:].rearrange("p a s -> p (a s)"), ps[:, 1, 0:HALVES * SLOTS]).then_inc(s.back, 1)
                dve.wait_ge(s.pe, 3)
                nc.vector.tensor_tensor(k.hbias[:], ps[0:FH, 2, 0:1], b1[:], ALU.add).then_inc(s.prepared, 1)
                dve.wait_ge(s.pe, 4)
                settle(nc.vector.tensor_tensor(k.grz[:], ps[0:SLOTS, 3, 0:2 * D], bhh[:, 0:2 * D], ALU.add))
                settle(nc.vector.tensor_tensor(k.grz[:], k.grz[:], bih[:, 0:2 * D], ALU.add))
                settle(nc.vector.tensor_tensor(k.hn[:], ps[0:SLOTS, 4, 0:D], bhh[:, 2 * D:], ALU.add))
                dve.wait_ge(s.pe, 5)
                for a in range(HALVES):
                    settle(nc.vector.tensor_copy(k.wvo[:, a, :], ps[:, 5 + a, 0:D]))
                settle(nc.vector.tensor_tensor(k.bvo[:], ps[0:SLOTS, 7, 0:D], bo[:], ALU.add))

            @block.tensor
            def _(pe):
                pe.wait_ge(s.hs, 1)
                pe.wait_ge(s.const, 3)
                for a in range(HALVES):
                    last = nc.tensor.matmul(ps[:, 0, a:a + 1], k.hs[:, a * P:(a + 1) * P], mean64[:],
                                            start=(a == 0), stop=(a == HALVES - 1), skip_group_check=True)
                last.then_inc(s.pe, 1)
                for a in range(HALVES):
                    last = nc.tensor.transpose(ps[:, 1, a * SLOTS:(a + 1) * SLOTS], k.hs[:, a * P:(a + 1) * P],
                                               k.ident[0:SLOTS, 0:SLOTS])
                last.then_inc(s.pe, 1)
                pe.wait_ge(s.back, 1)
                for a in range(HALVES):
                    last = nc.tensor.matmul(ps[0:FH, 2, 0:1], w1s[:, a, :], slot_mean[:, a:a + 1],
                                            start=(a == 0), stop=(a == HALVES - 1))
                last.then_inc(s.pe, 1)
                pe.wait_ge(s.back, 2)
                for a in range(HALVES):
                    nc.tensor.matmul(ps[0:SLOTS, 3, 0:2 * D], hsT[:, a, :], whhT[:, a, 0:2 * D],
                                     start=(a == 0), stop=(a == HALVES - 1))
                for a in range(HALVES):
                    last = nc.tensor.matmul(ps[0:SLOTS, 4, 0:D], hsT[:, a, :], whhT[:, a, 2 * D:],
                                            start=(a == 0), stop=(a == HALVES - 1))
                last.then_inc(s.pe, 1)
                for c in range(HALVES):
                    for a in range(HALVES):
                        nc.tensor.matmul(ps[:, 5 + c, 0:D], wv[:, a, c * P:(c + 1) * P], woT[:, a, :],
                                         start=(a == 0), stop=(a == HALVES - 1))
                for a in range(HALVES):
                    last = nc.tensor.matmul(ps[0:SLOTS, 7, 0:D], bvb[:, a, :], woT[:, a, :],
                                            start=(a == 0), stop=(a == HALVES - 1))
                last.then_inc(s.pe, 1)



def layer_norm(nc, k, ps, s, x, load=None):
    with nc.Block() as block:
        if load is not None:
            @block.sync
            def _(sp):
                sp.dma_start(x[:], load).then_inc(s.x_in, 16)

        @block.vector
        def _(dve):
            settle = chain_of(dve, s.dve)
            if load is not None:
                dve.wait_ge(s.x_in, 16)
            for t in range(T):
                last = nc.vector.bn_stats(k.stats[:, t, :], x[:, t, :])
            settle(last)
            for t in range(T):
                last = nc.vector.bn_aggr(k.mv[:, t, :], k.stats[:, t, :])
            settle(last)
            nc.vector.tensor_scalar(k.vare[:], k.mv[:, :, 1], EPS, None, ALU.add).then_inc(s.var, 1)
            dve.wait_ge(s.rstd, 1)
            for t in range(T):
                nc.vector.tensor_scalar(k.xn[:, t, 0:D], x[:, t, :], k.mv[:, t, 0:1], k.rstd[:, t:t + 1],
                                        ALU.subtract, ALU.mult).then_inc(s.xn, 1)
            for n in range(NB):
                dve.wait_ge(s.turned, HALVES * n + 2)
                nc.vector.tensor_copy(k.xnT[:, 1, n * BANK:(n + 1) * BANK], ps[:, HALVES * n + 1, :])

        @block.gpsimd
        def _(pool):
            pool.wait_ge(s.var, 1)
            nc.gpsimd.tensor_tensor(k.rstd[:], k.vare[:], k.mhalf[:, 0:T], ALU.pow).then_inc(s.rstd, 1)

        @block.tensor
        def _(pe):
            for n in range(NB):
                for a in range(HALVES):
                    for i in range(BANK // P):
                        t = n * (BANK // P) + i
                        pe.wait_ge(s.xn, t + 1)
                        last = nc.tensor.transpose(ps[:, HALVES * n + a, i * P:(i + 1) * P],
                                                   k.xn[:, t, a * P:(a + 1) * P], k.ident[:])
                    last.then_inc(s.turned, 1)

        @block.scalar
        def _(act):
            for n in range(NB):
                act.wait_ge(s.turned, HALVES * n + 1)
                nc.scalar.activation(k.xnT[:, 0, n * BANK:(n + 1) * BANK], ps[:, HALVES * n, :], ACT.Copy)
    clear(nc, s)



def project_and_convolve(nc, k, m, rep, pre, A, bounce, ps, s):
    def channel_major(ap):
        return ap.rearrange("p t d -> p (t d)").rearrange("p (a l) -> p a l", a=HALVES)

    vT, acc = channel_major(m.delta_tm), channel_major(m.ev[:])
    sq = [channel_major(m.local_tm), channel_major(m.mid_tm)]
    outs = [m.kT, vT, m.qT]
    AB = 6
    GRAM = (4, 0, 2, 4)
    BETA, SS = slice(0, T * H), (slice(2 * T * H, 3 * T * H), slice(4 * T * H, 5 * T * H))
    with nc.Block() as block:
        @block.gpsimd
        def _(pool):
            nc.gpsimd.memset(pre[:, :, :, 0:3], 0.0).then_inc(s.padded, 1)
            pool.wait_ge(s.padded, 1)
            nc.gpsimd.memset(rep[:, :, 0:PAD + SHIFTS - 1], 0.0).then_inc(s.padded, 1)

        @block.sync
        def _(sp):
            sp.wait_ge(s.padded, 2)
            sp.wait_ge(s.silu, 2 * HALVES)
            for sh in range(SHIFTS):
                for g in range(P // CG):
                    sp.dma_start(rep[CG * sh:CG * (sh + 1), g::P // CG, PAD + sh:PAD + L],
                                 vT[CG * g:CG * (g + 1), :, 0:L - sh]).then_inc(s.rep, 16)
            sp.wait_ge(s.a, T)
            for b in range(BLOCKS):
                part = slice(CHUNK * b, CHUNK * (b + 1))
                sp.dma_start(bounce[0, b].rearrange("g r c -> r g c"),
                             by_blocks(A, P)[part, :, part]).then_inc(s.blocks_out, 16)
            sp.wait_ge(s.rep, 16 * SHIFTS * (P // CG))
            sp.wait_ge(s.blocks_out, 16 * BLOCKS)

        @block.tensor
        def _(pe):
            def to_token_major(i):
                pe.wait_ge(s.silu, HALVES * (i + 1))
                if i == 0:
                    pe.wait_ge(s.a, 6)
                for u in range(T // 2):
                    if i == 1:
                        pe.wait_ge(s.tm, u + 1)
                    for j in range(2):
                        for a in range(HALVES):
                            last = nc.tensor.transpose(ps[:, u, j * D + a * P:j * D + (a + 1) * P],
                                                       outs[i][:, a, (2 * u + j) * P:(2 * u + j + 1) * P], k.ident[:])
                    last.then_inc(s.turned, 1)

            def sums_of_squares(i):
                for a in range(HALVES):
                    pe.wait_ge(s.squared, HALVES * i + a + 1)
                    for t in range(T):
                        first = SS[i].start + t * H + 2 * a
                        last = nc.tensor.matmul(ps[:, AB, first:first + 2], sq[i][:, a, t * P:(t + 1) * P], k.ones2[:],
                                                start=False, stop=True, skip_group_check=True)
                last.then_inc(s.sums, 1)

            for i, w in enumerate((k.wk, k.wv, k.wq)):
                for a in range(HALVES):
                    for n in range(NB):
                        u = (i * HALVES + a) * NB + n
                        if u >= 4:
                            pe.wait_ge(s.pre, u - 3)
                        for c in range(HALVES):
                            last = nc.tensor.matmul(ps[:, u % 4, :], w[:, c, a * P:(a + 1) * P],
                                                    k.xnT[:, c, n * BANK:(n + 1) * BANK],
                                                    start=(c == 0), stop=(c == HALVES - 1))
                        last.then_inc(s.proj, 1)
            for t in range(T):
                for c in range(HALVES):
                    last = nc.tensor.matmul(ps[:, AB, t * H:(t + 1) * H], k.xnT[:, c, t * P:(t + 1) * P],
                                            k.wb[:, c, :], start=(t == 0 and c == 0), stop=(c == HALVES - 1),
                                            skip_group_check=True)
            last.then_inc(s.beta, 1)
            pe.wait_ge(s.tanh, 1)
            sums_of_squares(0)
            pe.wait_ge(s.pre, 3 * HALVES * NB)
            for u in range(T // 2):
                if u == 3:
                    pe.wait_ge(s.a, 2)
                for j in range(2):
                    t = 2 * u + j
                    for h in range(H):
                        part = slice(DH * (h % 2), DH * (h % 2) + DH)
                        kt = m.kT[part, h // 2, t * P:(t + 1) * P]
                        col = (2 * j + h // 2) * P
                        last = nc.tensor.matmul(ps[:, GRAM[u] + h % 2, col:col + P], kt, kt,
                                                start=(j == 0 and h < 2), stop=True, skip_group_check=True)
                last.then_inc(s.gram, 1)
            to_token_major(0)
            pe.wait_ge(s.ss, 1)
            sums_of_squares(1)
            to_token_major(1)

        @block.scalar
        def _(act):
            def evacuate(i):
                for a in range(HALVES):
                    for n in range(NB):
                        u = (i * HALVES + a) * NB + n
                        act.wait_ge(s.proj, u + 1)
                        if i == 2:
                            act.wait_ge(s.conv, a + 1)
                        nc.scalar.activation(pre[:, i % 2, a, 3 + n * BANK:3 + (n + 1) * BANK], ps[:, u % 4, :],
                                             ACT.Copy).then_inc(s.pre, 1)

            def silu(i):
                for a in range(HALVES):
                    act.wait_ge(s.conv, HALVES * i + a + 1)
                    nc.scalar.activation(outs[i][:, a, :], acc[:, a, :], ACT.Silu).then_inc(s.silu, 1)

            def square(i):
                act.wait_ge(s.silu, HALVES * (2 * i + 1))
                for a in range(HALVES):
                    nc.scalar.activation(sq[i][:, a, :], outs[2 * i][:, a, :], ACT.Square).then_inc(s.squared, 1)

            def to_token_major(i, dst):
                for u in range(T // 2):
                    act.wait_ge(s.turned, i * (T // 2) + u + 1)
                    nc.scalar.activation(dst[:, 2 * u:2 * u + 2, :].rearrange("p t d -> p (t d)"), ps[:, u, :],
                                         ACT.Copy).then_inc(s.tm, 1)

            evacuate(0)
            evacuate(1)
            silu(0)
            square(0)
            evacuate(2)
            act.wait_ge(s.beta, 1)
            nc.scalar.activation(m.beta[:], ps[:, AB, BETA], ACT.Tanh, scale=0.5).then_inc(s.tanh, 1)
            silu(1)
            silu(2)
            to_token_major(0, m.k_tm[:])
            square(1)
            to_token_major(1, m.v_tm)

        @block.vector
        def _(dve):
            settle = chain_of(dve, s.dve)

            def convolve(i, halves=range(HALVES)):
                tap = (1, 2, 0)[i]
                for a in halves:
                    dve.wait_ge(s.pre, (i * HALVES + a + 1) * NB)
                    if i:
                        dve.wait_ge(s.silu, HALVES * (i - 1) + a + 1)
                    src = pre[:, i % 2, a, :]
                    settle(nc.vector.tensor_scalar(acc[:, a, :], src[:, 0:L], k.cw[:, tap, a, 0:1], None, ALU.mult))
                    for j in range(1, 4):
                        ins = nc.vector.scalar_tensor_tensor(acc[:, a, :], src[:, j:j + L], k.cw[:, tap, a, j:j + 1],
                                                             acc[:, a, :], ALU.mult, ALU.add)
                        if j < 3:
                            settle(ins)
                        else:
                            ins.then_inc(s.conv, 1)

            dve.wait_ge(s.padded, 1)
            convolve(0)
            convolve(1)
            dve.wait_ge(s.tanh, 1)
            settle(nc.vector.tensor_scalar(m.beta[:], m.beta[:], 0.5, 0.5, ALU.mult, ALU.add))
            dve.wait_ge(s.sums, 1)
            nc.vector.tensor_scalar(m.ss[:, 0, :], ps[:, AB, SS[0]], 1e-12, None, ALU.add).then_inc(s.ss, 1)
            dve.wait_ge(s.ss, 1)
            settle(nc.vector.reciprocal(m.negd[:], m.ss[:, 0, :]))
            settle(nc.vector.tensor_tensor(m.negd[:], m.negd[:], m.beta[:], ALU.mult))
            settle(nc.vector.tensor_scalar(m.negd[:], m.negd[:], -1.0, None, ALU.mult))
            for half in range(HALVES):
                convolve(2, (half,))
                for u in (2 * half, 2 * half + 1):
                    dve.wait_ge(s.gram, u + 1)
                    for odd in range(2):
                        nc.vector.tensor_tensor(
                            by_blocks(A, P)[:, 2 * u * H + odd:(2 * u + 2) * H:2],
                            ps[:, GRAM[u] + odd, :].rearrange("p (g n) -> p g n", n=P),
                            bc(m.negd[:, 2 * u * H + odd:(2 * u + 2) * H:2], P), ALU.mult).then_inc(s.a, 1)
            dve.wait_ge(s.sums, 2)
            nc.vector.tensor_scalar(m.ss[:, 1, :], ps[:, AB, SS[1]], 1e-12, None, ALU.add)
    clear(nc, s)


def long_convolutions(nc, k, m, rep, TT, bounce, ps, s):
    Xd = m.delta_tm
    def two_squares(ap):
        flat = ap[:].rearrange("p t d -> p (t d)").rearrange("p (s i j) -> p s i j", i=CHUNK, j=CHUNK)
        return flat[:, 0], flat[:, 1]

    block_a, product = two_squares(m.ev)
    X, XT = two_squares(m.local_tm)

    def out_cm(a, col, n):
        r, c = 4 * a + col // D, col % D
        return k.xn[:, r:r + n // D, 0:D] if n >= D else k.xn[:, r, c:c + n]

    units = [(c, a, n) for c in range(2) for a in range(HALVES) for n in range(NB)]

    def rows(b):
        return slice(CHUNK * b, CHUNK * (b + 1))

    with nc.Block() as block:
        @block.gpsimd
        def _(pool):
            nc.gpsimd.memset(X, 0.0).then_inc(s.zeroed, 1)
            pool.wait_ge(s.zeroed, 1)
            nc.gpsimd.memset(X.rearrange("p i j -> p (i j)")[:, 0:CHUNK * CHUNK:CHUNK + 1], 1.0).then_inc(s.zeroed, 1)
            pool.wait_ge(s.zeroed, 2)
            nc.gpsimd.memset(TT, 0.0).then_inc(s.zeroed, 1)
            pool.wait_ge(s.zeroed, 3)
            nc.gpsimd.memset(Xd[:], 0.0).then_inc(s.zeroed, 1)
            nc.gpsimd.tensor_tensor(m.rn[:], m.ss[:], k.mhalf[:].rearrange("p (i n) -> p i n", i=2),
                                    ALU.pow).then_inc(s.rnorm, 1)

        @block.sync
        def _(sp):
            sp.dma_start(block_a, bounce[0].rearrange("b g r c -> (b g) r c")).then_inc(s.blocks, 16)
            sp.wait_ge(s.inverse, 1)
            sp.dma_start(bounce[1].rearrange("b g r c -> (b g) r c"), X).then_inc(s.inverse_out, 16)
            sp.wait_ge(s.inverse, 2)
            sp.dma_start(bounce[2].rearrange("b g r c -> (b g) r c"), XT).then_inc(s.inverse_out, 16)
            sp.wait_ge(s.inverse_out, 32)
            sp.wait_ge(s.zeroed, 4)
            for b in range(BLOCKS):
                if b < 3:
                    left = CHUNK * (b % 2)
                    sp.dma_start(by_blocks(Xd, 2 * CHUNK)[rows(b), :, left:left + CHUNK],
                                 bounce[1, b].rearrange("g r c -> r g c")).then_inc(s.inverse_in, 16)
                sp.dma_start(by_blocks(TT, P)[rows(b), :, rows(b)],
                             bounce[2, b].rearrange("g r c -> r g c")).then_inc(s.inverse_in, 16)
            sp.wait_ge(s.inverse_in, 16 * (2 * BLOCKS - 1))

        @block.tensor
        def _(pe):
            for u, (c, a, n) in enumerate(units):
                steps, base = ((MID_STEPS, 0), (LOCAL_STEPS, MID_STEPS))[c]
                if u >= 4:
                    pe.wait_ge(s.evac, u - 3)
                for j in range(steps):
                    for g in range(P // CG):
                        gg = a * (P // CG) + g
                        last = nc.tensor.matmul(
                            ps[CG * g:CG * (g + 1), u % 4, :], k.stack[:, (base + j) * GROUPS + gg, :],
                            rep[:, gg, PAD + n * BANK - SHIFTS * j:PAD + (n + 1) * BANK - SHIFTS * j],
                            start=(j == 0), stop=(j == steps - 1))
                last.then_inc(s.conv, 1)
                if u % 4 == 3:
                    c = u // 4
                    pe.wait_ge(s.evac, u + 1)
                    for v in range(T // 2):
                        if c:
                            pe.wait_ge(s.tm, v + 1)
                        for j in range(2):
                            for aa in range(HALVES):
                                last = nc.tensor.transpose(
                                    ps[:, 4 + v, j * D + aa * P:j * D + (aa + 1) * P],
                                    out_cm(aa, (2 * v + j) * P, P), k.ident[:])
                        last.then_inc(s.turned, 1)

        @block.scalar
        def _(act):
            for c, dst in enumerate((m.mid_tm, m.local_tm)):
                for u in range(4 * c, 4 * c + 4):
                    a, n = units[u][1:]
                    act.wait_ge(s.conv, u + 1)
                    nc.scalar.activation(out_cm(a, n * BANK, BANK), ps[:, u % 4, :].rearrange("p (r d) -> p r d", d=D),
                                         ACT.Copy).then_inc(s.evac, 1)
                if c:
                    act.wait_ge(s.inverse_out, 32)
                for v in range(T // 2):
                    act.wait_ge(s.turned, c * (T // 2) + v + 1)
                    nc.scalar.activation(dst[:, 2 * v:2 * v + 2, :].rearrange("p t d -> p (t d)"),
                                         ps[:, 4 + v, :], ACT.Copy).then_inc(s.tm, 1)

        @block.vector
        def _(dve):
            settle = chain_of(dve, s.dve)
            dve.wait_ge(s.zeroed, 2)
            dve.wait_ge(s.blocks, 16)
            for i in range(1, CHUNK):
                settle(nc.vector.tensor_tensor(product[:, 0:i, 0:i], block_a[:, i:i + 1, 0:i].to_broadcast([P, i, i]),
                                               X[:, 0:i, 0:i].rearrange("p j c -> p c j"), ALU.mult))
                last = nc.vector.tensor_reduce(X[:, i, 0:i], product[:, 0:i, 0:i], AX.X, ALU.add)
                if i < CHUNK - 1:
                    settle(last)
                else:
                    last.then_inc(s.inverse, 1)
            dve.wait_ge(s.inverse, 1)
            nc.vector.tensor_copy(XT, X.rearrange("p i j -> p j i")).then_inc(s.inverse, 1)
            dve.wait_ge(s.rnorm, 1)
            settle(nc.vector.tensor_tensor(m.e[:], m.rn[:, 0, :], m.beta[:], ALU.mult))
            nc.vector.tensor_tensor(m.ev[:].rearrange("p t (h d) -> p (t h) d", h=H),
                                    m.v_tm[:].rearrange("p t (h d) -> p (t h) d", h=H), bc(m.e[:], DH), ALU.mult)
    clear(nc, s)


def delta_rule(nc, k, m, A, TT, ps, s):
    Xd = m.delta_tm[:].rearrange("p t (h n) -> p (t h) n", n=2 * CHUNK)
    C, HALF = CHUNK, 2 * CHUNK
    B0, B1, B2, B3 = (slice(C * b, C * (b + 1)) for b in range(BLOCKS))
    TOP, LOW = slice(0, HALF), slice(HALF, P)
    KSU, O, ST, KQ, AT_T, L5, L6 = 0, 1, 2, (3, 4), 5, 6, 7
    with ExitStack() as tmp:
        def sb(name, shape):
            return tmp.enter_context(nc.sbuf_tensor(name, shape, F32))

        AT5 = sb("dr_at5", [P, 2, H, P])
        W = sb("dr_w", [P, 4, H, HALF])
        AT6, Y6 = W[TOP], W
        Z = sb("dr_z", [P, 2, H, P])
        S = sb("dr_s", [P, HALVES, P])
        r = sb("dr_r", [P, 2, D])
        u = sb("dr_u", [P, 2, D])
        attnT = sb("dr_attn", [P, 2, H * P])

        def tile(ap, t):
            return ap[:, t, :].rearrange("p (h n) -> p h n", h=H)

        def bank(b, n, first=0):
            return ps[:, b, first:first + H * n].rearrange("p (h n) -> p h n", h=H)

        y5, x10, t01 = bank(L5, C), bank(L5, C, H * C), bank(L5, HALF, 2 * H * C)
        squares = sb("dr_squares", [P, 2, 6, D])
        with_delta = A[:, 0:4, :].rearrange("p (b t) (n d) -> p b (t n) d", b=2, d=D)
        paths = [m.local_tm, m.mid_tm, m.v_tm]

        def feature_sums(first, src, t, n):
            return nc.vector.tensor_reduce(m.feats[:, t, first * H:(first + n) * H].rearrange("p (n h) -> p n h", h=H),
                                           src.rearrange("p n (h d) -> p n h d", h=H), AX.X, ALU.add)

        at, y6, t6 = bank(AT_T, P), bank(L6, HALF), bank(AT_T, HALF)
        steps = [(step, step - 1, step - 2, step - 3, step - 4, step - 5) for step in range(T + 5)]
        with nc.Block() as block:
            @block.gpsimd
            def _(pool):
                nc.gpsimd.memset(AT5[:], 0.0).then_inc(s.zeroed, 1)
                nc.gpsimd.memset(Z[:], 0.0).then_inc(s.zeroed, 1)
                nc.gpsimd.memset(S[:], 0.0).then_inc(s.zeroed, 1)
                for t0, _, _, _, _, t in steps:
                    if t0 < T:
                        if t0 >= 2:
                            pool.wait_ge(s.summed, t0 - 1)
                        for n, (i, j) in enumerate(((0, 1), (0, 2), (1, 2))):
                            nc.gpsimd.tensor_tensor(squares[:, t0 % 2, 3 + n, :], paths[i][:, t0, :], paths[j][:, t0, :],
                                                    ALU.mult).then_inc(s.products, 1)
                    if t >= 0:
                        pool.wait_ge(s.o_out, t + 1)
                        if t >= 2:
                            pool.wait_ge(s.d_summed, t - 1)
                        for n in range(3):
                            nc.gpsimd.tensor_tensor(with_delta[:, t % 2, 1 + n, :], m.delta_tm[:, t, :], paths[n][:, t, :],
                                                    ALU.mult).then_inc(s.d_products, 1)

            @block.tensor
            def _(pe):
                for t0, t1, t2, t3, t4, t in steps:
                    if t >= 0:
                        b = t % 2
                        if t:
                            pe.wait_ge(s.attn, 2 * t)
                        for h in range(H):
                            rows = slice(DH * (h % 2), DH * (h % 2) + DH)
                            last = nc.tensor.matmul(ps[:, KQ[h % 2], h * P:(h + 1) * P], m.kT[rows, h // 2, t * P:(t + 1) * P],
                                                    m.qT[rows, h // 2, t * P:(t + 1) * P],
                                                    start=(h < 2), stop=True, skip_group_check=True)
                        last.then_inc(s.kq, 1)
                        if t:
                            pe.wait_ge(s.state, 2 * t)
                        for a in range(HALVES):
                            last = nc.tensor.matmul(ps[:, KSU, a * P:(a + 1) * P], m.kT[:, a, t * P:(t + 1) * P], S[:, a, :],
                                                    start=(a == 0), stop=True, skip_group_check=True)
                        last.then_inc(s.ks, 1)
                    if t0 < T:
                        if t4 > 0:
                            pe.wait_ge(s.t6, t4)
                        elif t0 > 0:
                            pe.wait_ge(s.at6, t0)
                        for h in range(H):
                            last = nc.tensor.transpose(at[:, h], tile(A, t0)[:, h], k.ident[:])
                        last.then_inc(s.at_ps, 1)
                    if t >= 0:
                        if t:
                            pe.wait_ge(s.o_out, t)
                        for a in range(HALVES):
                            nc.tensor.matmul(ps[:, O, a * P:(a + 1) * P], m.qT[:, a, t * P:(t + 1) * P], S[:, a, :],
                                             start=(a == 0), stop=False, skip_group_check=True)
                    if 0 <= t1 < T:
                        pe.wait_ge(s.at5, 2 * (t1 + 1))
                        if t1:
                            pe.wait_ge(s.z, 2 * t1)
                        if t2 > 0:
                            pe.wait_ge(s.x10, t2)
                            pe.wait_ge(s.t01, t2)
                            pe.wait_ge(s.t23, t2)
                        for h in range(H):
                            last = nc.tensor.matmul(y5[:, h], AT5[:, t1 % 2, h, :], Xd[:, t1 * H + h, 0:C],
                                                    start=(h == 0), stop=True, skip_group_check=True)
                        last.then_inc(s.y5_ps, 1)
                    if t >= 0:
                        pe.wait_ge(s.r, t + 1)
                        pe.wait_ge(s.t6, t + 1)
                        for h in range(H):
                            last = nc.tensor.matmul(ps[:, KSU, D + h * DH:D + (h + 1) * DH], TT[:, t, h * P:(h + 1) * P],
                                                    r[:, b, h * DH:(h + 1) * DH], start=False, stop=True,
                                                    skip_group_check=True)
                        last.then_inc(s.u_ps, 1)
                    if 0 <= t2 < T:
                        pe.wait_ge(s.z, 2 * min(t1 + 1, T))
                        for h in range(H):
                            nc.tensor.matmul(x10[:, h], tile(TT, t2)[:, h], Z[:, t2 % 2, h, 0:C],
                                             start=(h == 0), stop=True, skip_group_check=True)
                        for h in range(H):
                            last = nc.tensor.matmul(t01[:, h], Z[:, t2 % 2, h, :],
                                                    tile(TT, t2)[:, h].rearrange("p (b n) -> p b n", n=C)[:, 1::2],
                                                    start=False, stop=True, skip_group_check=True)
                        last.then_inc(s.x_ps, 1)
                    if t >= 0:
                        pe.wait_ge(s.u, t + 1)
                        if t < T - 1:
                            for a in range(HALVES):
                                last = nc.tensor.matmul(ps[:, ST, a * P:(a + 1) * P], m.k_tm[:, t, a * P:(a + 1) * P],
                                                        u[:, b, a * P:(a + 1) * P], start=(t == 0 and a == 0), stop=False,
                                                        skip_group_check=True)
                            last.then_inc(s.s_ps, 1)
                        pe.wait_ge(s.attn, 2 * (t + 1))
                        for h in range(H):
                            last = nc.tensor.matmul(ps[:, O, h * DH:(h + 1) * DH], attnT[:, b, h * P:(h + 1) * P],
                                                    u[:, b, h * DH:(h + 1) * DH], start=False, stop=True,
                                                    skip_group_check=True)
                        last.then_inc(s.o, 1)
                    if 0 <= t3 < T:
                        pe.wait_ge(s.x10, t3 + 1)
                        pe.wait_ge(s.at6, t3 + 1)
                        if t3:
                            pe.wait_ge(s.y6, t3)
                        for h in range(H):
                            last = nc.tensor.matmul(y6[LOW, h], AT6[:, t3 % 4, h, :], Xd[TOP, t3 * H + h, :],
                                                    start=(h == 0), stop=True, skip_group_check=True)
                        last.then_inc(s.y6_ps, 1)
                    if 0 <= t4 < T:
                        pe.wait_ge(s.y6, t4 + 1)
                        pe.wait_ge(s.t23, t4 + 1)
                        pe.wait_ge(s.at6, min(t0 + 1, T))
                        if t4:
                            pe.wait_ge(s.t6, t4)
                        for h in range(H):
                            last = nc.tensor.matmul(t6[TOP, h], Y6[LOW, t4 % 2, h, :], tile(TT, t4)[LOW, h, HALF:P],
                                                    start=(h == 0), stop=True, skip_group_check=True)
                        last.then_inc(s.t_ps, 1)

            @block.vector
            def _(dve):
                settle = chain_of(dve, s.dve)
                dve.wait_ge(s.zeroed, 3)
                def sum_with_delta(t):
                    dve.wait_ge(s.d_products, 3 * (t + 1))
                    dve.wait_ge(s.d_square, t + 1)
                    feature_sums(9, m.delta_tm[:, t:t + 1, :], t, 1)
                    feature_sums(10, with_delta[:, t % 2], t, 4).then_inc(s.d_summed, 1)

                for t0, t1, t2, t3, t4, t in steps:
                    b = t % 2
                    if t >= 0:
                        dve.wait_ge(s.ks, t + 1)
                        settle(nc.vector.tensor_tensor(r[:, b, :].rearrange("p (h d) -> p h d", h=H),
                                                       ps[:, KSU, 0:D].rearrange("p (h d) -> p h d", h=H),
                                                       bc(m.negd[:, t * H:(t + 1) * H], DH), ALU.mult))
                        nc.vector.tensor_tensor(r[:, b, :], r[:, b, :], m.ev[:, t, :], ALU.add).then_inc(s.r, 1)
                        for odd in range(2):
                            nc.vector.tensor_tensor(attnT[:, b, :].rearrange("p (h n) -> p h n", h=H)[:, odd::2],
                                                    ps[:, KQ[odd], :].rearrange("p (h n) -> p h n", h=H)[:, odd::2],
                                                    k.incl[:].unsqueeze(1).to_broadcast([P, H // 2, P]), ALU.mult)\
                                .then_inc(s.attn, 1)
                    if t0 < T:
                        dve.wait_ge(s.at_ps, t0 + 1)
                        if t0 >= 2:
                            dve.wait_ge(s.y5_ps, t0 - 1)
                        nc.vector.tensor_copy(AT5[B0, t0 % 2, :, B1], at[B0, :, B1]).then_inc(s.at5, 1)
                        nc.vector.tensor_copy(AT5[B2, t0 % 2, :, B3], at[B2, :, B3]).then_inc(s.at5, 1)
                        if t0 >= 4:
                            dve.wait_ge(s.y6_ps, t0 - 3)
                        nc.vector.tensor_copy(AT6[:, t0 % 4], at[TOP, :, HALF:P]).then_inc(s.at6, 1)
                        feature_sums(0, m.paths[:, 0:3, t0, :], t0, 3)
                    if 0 <= t2 < T:
                        dve.wait_ge(s.x_ps, t2 + 1)
                        nc.vector.tensor_copy(Xd[B1, t2 * H:(t2 + 1) * H, 0:C], x10[B1]).then_inc(s.x10, 1)
                        nc.vector.tensor_copy(tile(TT, t2)[B0, :, B1], t01[B0, :, 0:C]).then_inc(s.t01, 1)
                    if t >= 0:
                        if t < T - 1:
                            dve.wait_ge(s.s_ps, t + 1)
                            for part in (TOP, LOW):
                                nc.vector.tensor_copy(S[part, :, part],
                                                      ps[part, ST, 0:D].rearrange("p (a n) -> p a n", a=2)[:, :, part])\
                                    .then_inc(s.state, 1)
                        dve.wait_ge(s.o, t + 1)
                        nc.vector.tensor_tensor(m.delta_tm[:, t, :].rearrange("p (h d) -> p h d", h=H),
                                                ps[:, O, 0:D].rearrange("p (h d) -> p h d", h=H),
                                                bc(m.rn[:, 1, t * H:(t + 1) * H], DH), ALU.mult).then_inc(s.o_out, 1)
                        if t >= 2:
                            sum_with_delta(t - 2)
                    if t0 < T:
                        dve.wait_ge(s.products, 3 * (t0 + 1))
                        dve.wait_ge(s.square, t0 + 1)
                        feature_sums(3, squares[:, t0 % 2], t0, 6).then_inc(s.summed, 1)
                sum_with_delta(T - 2)
                sum_with_delta(T - 1)

            @block.scalar
            def _(act):
                act.wait_ge(s.zeroed, 2)
                def square_others(t):
                    if t >= 2:
                        act.wait_ge(s.summed, t - 1)
                    nc.scalar.activation(squares[:, t % 2, 0:3, :], m.paths[:, 0:3, t, :], ACT.Square).then_inc(s.square, 1)

                def square_delta(t):
                    act.wait_ge(s.o_out, t + 1)
                    if t >= 2:
                        act.wait_ge(s.d_summed, t - 1)
                    nc.scalar.activation(with_delta[:, t % 2, 0, :], m.delta_tm[:, t, :], ACT.Square).then_inc(s.d_square, 1)

                square_others(0)
                for t0, t1, t2, t3, t4, t in steps:
                    if 0 <= t1 < T:
                        act.wait_ge(s.y5_ps, t1 + 1)
                        if t1 >= 2:
                            act.wait_ge(s.x_ps, t1 - 1)
                        nc.scalar.activation(Z[B1, t1 % 2, :, B0], y5[B1], ACT.Copy).then_inc(s.z, 1)
                        nc.scalar.activation(Z[B3, t1 % 2, :, B2], y5[B3], ACT.Copy).then_inc(s.z, 1)
                    if t >= 0:
                        act.wait_ge(s.u_ps, t + 1)
                        nc.scalar.activation(u[:, t % 2, :], ps[:, KSU, D:2 * D], ACT.Copy).then_inc(s.u, 1)
                    if 0 <= t2 < T:
                        act.wait_ge(s.x_ps, t2 + 1)
                        nc.scalar.activation(tile(TT, t2)[B2, :, B3], t01[B2, :, C:HALF], ACT.Copy).then_inc(s.t23, 1)
                    if 0 <= t3 < T:
                        act.wait_ge(s.y6_ps, t3 + 1)
                        if t3 >= 2:
                            act.wait_ge(s.t_ps, t3 - 1)
                        nc.scalar.activation(Y6[LOW, t3 % 2], y6[LOW], ACT.Copy).then_inc(s.y6, 1)
                    if 0 <= t4 < T:
                        act.wait_ge(s.t_ps, t4 + 1)
                        nc.scalar.activation(tile(TT, t4)[TOP, :, HALF:P], t6[TOP], ACT.Copy).then_inc(s.t6, 1)
                    if t0 + 1 < T:
                        square_others(t0 + 1)
                    if t > 0:
                        square_delta(t - 1)
                square_delta(T - 1)
    clear(nc, s)


def route(nc, k, m, ps, s):
    with ExitStack() as tmp:
        def sb(name, shape):
            return tmp.enter_context(nc.sbuf_tensor(name, shape, F32))

        F = m.feats
        var = sb("ro_var", [P, T, 4 * H])
        FT = sb("ro_ft", [FEATS, L])
        h1T = sb("ro_h1", [P, HC, L])
        lg = sb("ro_lg", [P, T * H, PATHS])
        red = sb("ro_red", [P, T * H])

        def feature(first, n):
            return F[:, :, first * H:(first + n) * H]

        with nc.Block() as block:
            @block.scalar
            def _(act):
                for n in range(NB):
                    act.wait_ge(s.ft_ps, n + 1)
                    nc.scalar.activation(FT[:, n * BANK:(n + 1) * BANK], ps[0:FEATS, n, :], ACT.Copy).then_inc(s.ft, 1)
                for n in range(NB):
                    for c in range(HC):
                        u = n * HC + c
                        rows = P if c < HC - 1 else HLAST
                        act.wait_ge(s.h1_ps, u + 1)
                        nc.scalar.activation(h1T[0:rows, c, n * BANK:(n + 1) * BANK], ps[0:rows, 2 + u % 4, :], ACT.Silu,
                                             bias=k.rb1[0:rows, c:c + 1]).then_inc(s.h1, 1)
                act.wait_ge(s.shifted, 1)
                nc.scalar.activation(lg[:].rearrange("p n c -> p (n c)"), lg[:].rearrange("p n c -> p (n c)"),
                                     ACT.Exp).then_inc(s.exp, 1)

            @block.vector
            def _(dve):
                settle = chain_of(dve, s.dve)
                for first, sums, squares, n in ((0, 0, 3, 3), (3, 9, 10, 1)):
                    last = nc.vector.tensor_tensor(var[:, :, first * H:(first + n) * H], feature(sums, n), feature(sums, n),
                                                   ALU.mult)
                settle(last)
                for first, sums, squares, n in ((0, 0, 3, 3), (3, 9, 10, 1)):
                    last = nc.vector.scalar_tensor_tensor(feature(squares, n), var[:, :, first * H:(first + n) * H], -1.0 / DH,
                                                          feature(squares, n), ALU.mult, ALU.add)
                settle(last)
                for squares, n in ((3, 3), (10, 1)):
                    nc.vector.tensor_scalar(feature(squares, n), feature(squares, n), 1.0 / (DH - 1), None, ALU.mult)
                for first, n in ((0, 3), (6, 4), (11, 3)):
                    last = nc.vector.tensor_scalar(feature(first, n), feature(first, n), 1.0 / DH, None, ALU.mult)
                last.then_inc(s.feats, 1)
                dve.wait_ge(s.logits, 1)
                settle(nc.vector.tensor_tensor(lg[:].rearrange("p (t h) c -> p t (h c)", h=H),
                                               ps[:, 6, 0:T * H * PATHS].rearrange("p (t n) -> p t n", t=T),
                                               k.rb2[:].unsqueeze(1).to_broadcast([P, T, H * PATHS]), ALU.add))
                settle(nc.vector.tensor_reduce(red[:], lg[:], AX.X, ALU.max))
                nc.vector.tensor_tensor(lg[:], lg[:], bc(red[:], PATHS), ALU.subtract).then_inc(s.shifted, 1)
                dve.wait_ge(s.exp, 1)
                settle(nc.vector.tensor_reduce(red[:], lg[:], AX.X, ALU.add))
                settle(nc.vector.reciprocal(red[:], red[:]))
                settle(nc.vector.tensor_tensor(lg[:], lg[:], bc(red[:], PATHS), ALU.mult))
                nc.vector.tensor_scalar(m.prob[:], lg[:], 1.0 - PATHS * FLOOR, FLOOR, ALU.mult, ALU.add)

            @block.tensor
            def _(pe):
                def unit(u):
                    n, c = u // HC, u % HC
                    rows = P if c < HC - 1 else HLAST
                    return n, slice(n * BANK, (n + 1) * BANK), ps[0:rows, 2 + u % 4, :], slice(c * P, c * P + rows)

                def from_hidden(u):
                    n, cols, out, hid = unit(u)
                    if u >= 4:
                        pe.wait_ge(s.h1, u - 3)
                    nc.tensor.matmul(out, k.rw1[:, 0, hid], k.xnT[:, 0, cols], start=True, stop=False)
                    nc.tensor.matmul(out, k.rw1[:, 1, hid], k.xnT[:, 1, cols], start=False, stop=False)

                for u in range(4):
                    from_hidden(u)
                pe.wait_ge(s.feats, 1)
                for n in range(NB):
                    for i in range(BANK // P):
                        last = nc.tensor.transpose(ps[0:FEATS, n, i * P:(i + 1) * P], F[:, n * (BANK // P) + i, :], k.ident[:])
                    last.then_inc(s.ft_ps, 1)
                for u in range(NB * HC):
                    n, cols, out, hid = unit(u)
                    pe.wait_ge(s.ft, n + 1)
                    nc.tensor.matmul(out, k.rw1[0:FEATS, 2, hid], FT[:, cols], start=False, stop=True).then_inc(s.h1_ps, 1)
                    if u + 4 < NB * HC:
                        from_hidden(u + 4)
                pe.wait_ge(s.h1, NB * HC)
                for t in range(T):
                    for c in range(HC):
                        rows = P if c < HC - 1 else HLAST
                        last = nc.tensor.matmul(ps[:, 6, t * H * PATHS:(t + 1) * H * PATHS], h1T[0:rows, c, t * P:(t + 1) * P],
                                                k.rw2[0:rows, c, :], start=(t == 0 and c == 0), stop=(c == HC - 1),
                                                skip_group_check=True)
                last.then_inc(s.logits, 1)
    clear(nc, s)


def mix_and_project(nc, k, m, ps, s):
    with ExitStack() as tmp:
        def sb(name, shape):
            return tmp.enter_context(nc.sbuf_tensor(name, shape, F32))

        part = [sb(f"mi_part{i}", [P, T, D]) for i in range(PATHS)]
        sq = sb("mi_sq", [P, T, D])
        oT = sb("mi_ot", [P, HALVES, L])
        ms = sb("mi_ms", [P, 4, T * H])
        paths = [m.local_tm, m.mid_tm, m.delta_tm, m.v_tm]

        def by_head(ap):
            return ap[:].rearrange("p t (h d) -> p (t h) d", h=H)

        def flat(ap):
            return ap[:].rearrange("p t d -> p (t d)")

        def weight(i):
            return m.prob[:, :, i:i + 1].to_broadcast([P, T * H, DH])

        mixed, weighted = part[0], part[1]
        with nc.Block() as block:
            @block.gpsimd
            def _(pool):
                nc.gpsimd.tensor_tensor(by_head(part[2]), by_head(paths[2]), weight(2), ALU.mult).then_inc(s.part, 1)
                pool.wait_ge(s.mixed, 1)
                nc.gpsimd.tensor_tensor(weighted[:], mixed[:], k.mixw[:].unsqueeze(1).to_broadcast([P, T, D]),
                                        ALU.mult).then_inc(s.weighted, 1)
                pool.wait_ge(s.scale_in, 1)
                nc.gpsimd.tensor_tensor(ms[:, 3, :], ms[:, 2, :], k.mhalf[:, 0:T * H], ALU.pow).then_inc(s.scale, 1)

            @block.vector
            def _(dve):
                settle = chain_of(dve, s.dve)
                nc.vector.tensor_tensor(by_head(part[0]), by_head(paths[0]), weight(0), ALU.mult)
                settle(nc.vector.tensor_tensor(by_head(part[1]), by_head(paths[1]), weight(1), ALU.mult))
                nc.vector.tensor_tensor(part[0][:], part[0][:], part[1][:], ALU.add)
                settle(nc.vector.tensor_tensor(by_head(part[3]), by_head(paths[3]), weight(3), ALU.mult))
                settle(nc.vector.tensor_tensor(part[0][:], part[0][:], part[3][:], ALU.add))
                dve.wait_ge(s.part, 1)
                nc.vector.tensor_tensor(mixed[:], part[0][:], part[2][:], ALU.add).then_inc(s.mixed, 1)
                dve.wait_ge(s.square, 1)
                settle(nc.vector.tensor_reduce(ms[:, 0, :], by_head(sq), AX.X, ALU.add))
                settle(nc.vector.tensor_scalar(ms[:, 0, :], ms[:, 0, :], 1.0 / DH, EPS, ALU.mult, ALU.add))
                nc.vector.reciprocal(ms[:, 2, :], ms[:, 0, :]).then_inc(s.sq_free, 1)
                dve.wait_ge(s.square, 2)
                settle(nc.vector.tensor_reduce(ms[:, 1, :], by_head(sq), AX.X, ALU.add))
                dve.wait_ge(s.sq_free, 1)
                settle(nc.vector.tensor_tensor(ms[:, 1, :], ms[:, 1, :], ms[:, 2, :], ALU.mult))
                settle(nc.vector.tensor_scalar(ms[:, 1, :], ms[:, 1, :], 1.0 / DH, EPS, ALU.mult, ALU.add))
                nc.vector.tensor_tensor(ms[:, 2, :], ms[:, 1, :], ms[:, 0, :], ALU.mult).then_inc(s.scale_in, 1)
                dve.wait_ge(s.scale, 1)
                for u in range(T // 2):
                    rows = slice(2 * u * H, (2 * u + 2) * H)
                    nc.vector.tensor_tensor(by_head(part[2])[:, rows], by_head(weighted)[:, rows], bc(ms[:, 3, rows], DH),
                                            ALU.mult).then_inc(s.normed, 1)
                for n in range(NB):
                    dve.wait_ge(s.turned, HALVES * n + 2)
                    nc.vector.tensor_copy(oT[:, 1, n * BANK:(n + 1) * BANK], ps[:, HALVES * n + 1, :]).then_inc(s.ot1, 1)
                for u in range(T // 2):
                    dve.wait_ge(s.out, u + 1)
                    nc.vector.tensor_tensor(k.x1[:, 2 * u:2 * u + 2, :].rearrange("p t d -> p (t d)"),
                                            k.x1[:, 2 * u:2 * u + 2, :].rearrange("p t d -> p (t d)"), ps[:, 4 + u, :], ALU.add)

            @block.scalar
            def _(act):
                act.wait_ge(s.mixed, 1)
                nc.scalar.activation(flat(sq), flat(mixed), ACT.Square).then_inc(s.square, 1)
                act.wait_ge(s.weighted, 1)
                act.wait_ge(s.sq_free, 1)
                nc.scalar.activation(flat(sq), flat(weighted), ACT.Square).then_inc(s.square, 1)
                for n in range(NB):
                    act.wait_ge(s.turned, HALVES * n + 1)
                    nc.scalar.activation(oT[:, 0, n * BANK:(n + 1) * BANK], ps[:, HALVES * n, :], ACT.Copy).then_inc(s.ot0, 1)

            @block.tensor
            def _(pe):
                for n in range(NB):
                    for a in range(HALVES):
                        for i in range(BANK // P):
                            t = n * (BANK // P) + i
                            pe.wait_ge(s.normed, t // 2 + 1)
                            last = nc.tensor.transpose(ps[:, HALVES * n + a, i * P:(i + 1) * P],
                                                       part[2][:, t, a * P:(a + 1) * P], k.ident[:])
                        last.then_inc(s.turned, 1)
                for t in range(T):
                    n = t // (BANK // P)
                    pe.wait_ge(s.ot0, n + 1)
                    pe.wait_ge(s.ot1, n + 1)
                    for a in range(HALVES):
                        last = nc.tensor.matmul(ps[:, 4 + t // 2, (t % 2) * D:(t % 2 + 1) * D], oT[:, a, t * P:(t + 1) * P],
                                                k.wo[:, a, :], start=(t % 2 == 0 and a == 0), stop=(a == HALVES - 1),
                                                skip_group_check=True)
                    if t % 2:
                        last.then_inc(s.out, 1)
    clear(nc, s)



def slot_ffn(nc, k, ps, s, tag, store=None):
    with ExitStack() as tmp:
        def sb(name, shape):
            return tmp.enter_context(nc.sbuf_tensor(name, shape, F32))

        hT = sb(f"{tag}_ht", [FH, L])
        lg = sb(f"{tag}_lg", [P, T, SLOTS])
        left = sb(f"{tag}_left", [P, T, SLOTS])
        alpha = sb(f"{tag}_alpha", [P, T, SLOTS])
        top = sb(f"{tag}_top", [P, T, TOPK])
        total = sb(f"{tag}_total", [P, T])
        alphaT = sb(f"{tag}_alphat", [SLOTS, L])
        gi = sb(f"{tag}_gi", [SLOTS, D])
        wsum = sb(f"{tag}_wsum", [SLOTS, 1])
        giT = sb(f"{tag}_git", [P, HALVES, SLOTS])
        rz = sb(f"{tag}_rz", [SLOTS, 2 * D])
        new = sb(f"{tag}_new", [SLOTS, D])
        mem = sb(f"{tag}_mem", [SLOTS, D])
        memT = sb(f"{tag}_memt", [P, HALVES, SLOTS])
        values = sb(f"{tag}_values", [SLOTS, D])

        with nc.Block() as block:
            @block.tensor
            def _(pe):
                for n in range(NB):
                    for c in range(HALVES):
                        last = nc.tensor.matmul(ps[:, n, :], k.w1x[:, c, :], k.xnT[:, c, n * BANK:(n + 1) * BANK],
                                                start=(c == 0), stop=(c == HALVES - 1))
                    last.then_inc(s.h_ps, 1)
                for t in range(T):
                    pe.wait_ge(s.h, t // (BANK // P) + 1)
                    last = nc.tensor.matmul(ps[:, 2, t * SLOTS:(t + 1) * SLOTS], hT[:, t * P:(t + 1) * P], k.w2T[:],
                                            start=(t == 0), stop=True, skip_group_check=True)
                last.then_inc(s.logits, 1)
                pe.wait_ge(s.alpha, 1)
                for t in range(T):
                    last = nc.tensor.matmul(ps[0:SLOTS, 3, 0:D + 1], alpha[:, t, :], k.xn[:, t, :],
                                            start=(t == 0), stop=(t == T - 1))
                last.then_inc(s.gathered, 1)
                for n in range(NB):
                    for i in range(BANK // P):
                        last = nc.tensor.transpose(ps[0:SLOTS, 4 + n, i * P:(i + 1) * P],
                                                   alpha[:, n * (BANK // P) + i, :], k.ident[:])
                    last.then_inc(s.at_ps, 1)
                pe.wait_ge(s.gi, 1)
                for a in range(HALVES):
                    last = nc.tensor.transpose(ps[:, 6, a * SLOTS:(a + 1) * SLOTS], gi[:, a * P:(a + 1) * P],
                                               k.ident[0:SLOTS, 0:SLOTS])
                last.then_inc(s.git_ps, 1)
                pe.wait_ge(s.git, 1)
                for a in range(HALVES):
                    last = nc.tensor.matmul(ps[0:SLOTS, 0, :], giT[:, a, :], k.wihT[:, a, 0:2 * D],
                                            start=(a == 0), stop=(a == HALVES - 1))
                last.then_inc(s.gates, 1)
                for a in range(HALVES):
                    last = nc.tensor.matmul(ps[0:SLOTS, 1, 0:D], giT[:, a, :], k.wihT[:, a, 2 * D:],
                                            start=(a == 0), stop=(a == HALVES - 1))
                last.then_inc(s.gates, 1)
                pe.wait_ge(s.mem, 1)
                for a in range(HALVES):
                    last = nc.tensor.transpose(ps[:, 6, a * SLOTS:(a + 1) * SLOTS], mem[:, a * P:(a + 1) * P],
                                               k.ident[0:SLOTS, 0:SLOTS])
                last.then_inc(s.memt_ps, 1)
                pe.wait_ge(s.memt, 1)
                for a in range(HALVES):
                    last = nc.tensor.matmul(ps[0:SLOTS, 7, 0:D], memT[:, a, :], k.wvo[:, a, :],
                                            start=(a == 0), stop=(a == HALVES - 1))
                last.then_inc(s.values_ps, 1)
                pe.wait_ge(s.values, 1)
                for t in range(T):
                    pe.wait_ge(s.alphat, t // (BANK // P) + 1)
                    last = nc.tensor.matmul(ps[:, t // 2, (t % 2) * D:(t % 2 + 1) * D], alphaT[:, t * P:(t + 1) * P],
                                            values[:], start=(t % 2 == 0), stop=True, skip_group_check=True)
                    if t % 2:
                        last.then_inc(s.out, 1)

            @block.scalar
            def _(act):
                for n in range(NB):
                    act.wait_ge(s.h_ps, n + 1)
                    nc.scalar.activation(hT[:, n * BANK:(n + 1) * BANK], ps[:, n, :], ACT.Gelu,
                                         bias=k.hbias[:, 0:1]).then_inc(s.h, 1)
                act.wait_ge(s.shifted, 1)
                nc.scalar.activation(alpha[:].rearrange("p t n -> p (t n)"), alpha[:].rearrange("p t n -> p (t n)"),
                                     ACT.Exp).then_inc(s.exp, 1)
                for n in range(NB):
                    act.wait_ge(s.at_ps, n + 1)
                    nc.scalar.activation(alphaT[:, n * BANK:(n + 1) * BANK], ps[0:SLOTS, 4 + n, :],
                                         ACT.Copy).then_inc(s.alphat, 1)
                act.wait_ge(s.rz_in, 1)
                nc.scalar.activation(rz[:], rz[:], ACT.Tanh, scale=0.5).then_inc(s.rz, 1)
                act.wait_ge(s.n_in, 1)
                nc.scalar.activation(new[:], new[:], ACT.Tanh).then_inc(s.n, 1)

            @block.vector
            def _(dve):
                settle = chain_of(dve, s.dve)
                dve.wait_ge(s.logits, 1)
                settle(nc.vector.tensor_tensor(lg[:], ps[:, 2, :].rearrange("p (t n) -> p t n", t=T),
                                               k.b2[:].unsqueeze(1).to_broadcast([P, T, SLOTS]), ALU.add))
                settle(nc.vector.tensor_scalar(lg[:], lg[:], k.invtau[:, 0:1], None, ALU.mult))
                for t in range(T):
                    last = nc.vector.max(top[:, t, :], lg[:, t, :])
                settle(last)
                nc.vector.tensor_tensor(alpha[:], lg[:], top[:, :, 0:1].to_broadcast([P, T, SLOTS]),
                                        ALU.subtract).then_inc(s.shifted, 1)
                for t in range(T):
                    last = nc.vector.match_replace(left[:, t, :], top[:, t, :], lg[:, t, :], NEG)
                settle(last)
                settle(nc.vector.tensor_tensor(left[:], left[:], lg[:], ALU.not_equal))
                dve.wait_ge(s.exp, 1)
                settle(nc.vector.tensor_tensor(alpha[:], alpha[:], left[:], ALU.mult))
                settle(nc.vector.tensor_reduce(total[:], alpha[:], AX.X, ALU.add))
                settle(nc.vector.reciprocal(total[:], total[:]))
                nc.vector.tensor_tensor(alpha[:], alpha[:], bc(total[:], SLOTS), ALU.mult).then_inc(s.alpha, 1)
                dve.wait_ge(s.gathered, 1)
                settle(nc.vector.tensor_scalar(wsum[:], ps[0:SLOTS, 3, D:D + 1], 1e-8, None, ALU.add))
                settle(nc.vector.reciprocal(wsum[:], wsum[:]))
                nc.vector.tensor_scalar(gi[:], ps[0:SLOTS, 3, 0:D], wsum[:, 0:1], None, ALU.mult).then_inc(s.gi, 1)
                dve.wait_ge(s.git_ps, 1)
                nc.vector.tensor_copy(giT[:].rearrange("p a n -> p (a n)"), ps[:, 6, 0:HALVES * SLOTS]).then_inc(s.git, 1)
                dve.wait_ge(s.gates, 1)
                nc.vector.tensor_tensor(rz[:], ps[0:SLOTS, 0, :], k.grz[:], ALU.add).then_inc(s.rz_in, 1)
                dve.wait_ge(s.rz, 1)
                settle(nc.vector.tensor_scalar(rz[:], rz[:], 0.5, 0.5, ALU.mult, ALU.add))
                settle(nc.vector.tensor_tensor(mem[:], rz[:, 0:D], k.hn[:], ALU.mult))
                settle(nc.vector.tensor_tensor(mem[:], mem[:], k.bihn[:], ALU.add))
                dve.wait_ge(s.gates, 2)
                nc.vector.tensor_tensor(new[:], ps[0:SLOTS, 1, 0:D], mem[:], ALU.add).then_inc(s.n_in, 1)
                dve.wait_ge(s.n, 1)
                settle(nc.vector.tensor_tensor(mem[:], k.hs[:], new[:], ALU.subtract))
                settle(nc.vector.tensor_tensor(mem[:], mem[:], rz[:, D:2 * D], ALU.mult))
                nc.vector.tensor_tensor(mem[:], mem[:], new[:], ALU.add).then_inc(s.mem, 1)
                dve.wait_ge(s.memt_ps, 1)
                nc.vector.tensor_copy(memT[:].rearrange("p a n -> p (a n)"), ps[:, 6, 0:HALVES * SLOTS]).then_inc(s.memt, 1)
                dve.wait_ge(s.values_ps, 1)
                nc.vector.tensor_tensor(values[:], ps[0:SLOTS, 7, 0:D], k.bvo[:], ALU.add).then_inc(s.values, 1)
                for u in range(T // 2):
                    dve.wait_ge(s.out, u + 1)
                    xs = k.x1[:, 2 * u:2 * u + 2, :].rearrange("p t d -> p (t d)")
                    nc.vector.tensor_tensor(xs, xs, ps[:, u, :], ALU.add).then_inc(s.x_out, 1)

            if store is not None:
                @block.sync
                def _(sp):
                    sp.wait_ge(s.x_out, T // 2)
                    sp.dma_start(store, k.x1[:]).then_inc(s.stored, 16)
                    sp.wait_ge(s.stored, 16)
    clear(nc, s)



GH = 4
AG = AH // GH
NBUF = 3
RING = 3
STEPS = [(n, kt) for n in range(NB) for kt in range((n + 1) * (BANK // P))]
PIECES = [(t, j, c) for t in range(T) for j in range(GH) for c in range(-(-(t + 1) * P // BANK))]
PER_STEP = len(PIECES) // len(STEPS)
Q_PARTS = (0, 0, 1, 0, 2, 1)
K_PARTS = (0, 1, 0, 2, 0, 1)
RATIO = float(AD) ** -0.5


def softmax_attention(nc, k, ps, s, stacked):
    with ExitStack() as tmp:
        def sb(name, shape, dt=F32):
            return tmp.enter_context(nc.sbuf_tensor(name, shape, dt))

        qs = sb("sa_qs", [P, NBUF, GH, L], BF16)
        ks = sb("sa_ks", [P, NBUF, GH, L], BF16)
        va = sb("sa_va", [P, T, AH, AD + 1])
        nm = sb("sa_nm", [P, 2, T, GH, 2])
        otm = sb("sa_otm", [P, T, D])
        rec = sb("sa_rec", [P, BANK // P, GH])
        osb = sb("sa_o", [P, BANK])
        mr = sb("sa_mr", [GH, BANK])
        mp = sb("sa_mp", [GH, 2, 3, L], BF16)

        with ExitStack() as early:
            parts = [early.enter_context(nc.sbuf_tensor(f"sa_parts{i}", [P, 3, HALVES, L], BF16)) for i in range(2)]
            pt = early.enter_context(nc.sbuf_tensor("sa_pt", [P, 2, GH, BANK], F32))
            rest = pt[:, 0, 0:2, :]

            pe_use, dve_use = [0], [0]

            def take(pe):
                if pe_use[0] >= RING:
                    pe.wait_ge(s.ring_free, pe_use[0] - RING + 1)
                pe_use[0] += 1
                return ps[:, (pe_use[0] - 1) % RING, :]

            def give(dve):
                dve_use[0] += 1
                dve.wait_ge(s.ring_ready, dve_use[0])
                return ps[:, (dve_use[0] - 1) % RING, :]

            def max_pe(pe, g, first, n):
                if first == 0:
                    pe.wait_ge(stacked[g], 16 * 2 * NCOMB * 2)
                    if g == 0:
                        pe.wait_ge(s.const, 2)
                        pe.wait_ge(s.rest, 2 * HALVES * NB)
                for t, j, c in PIECES[first:first + n]:
                    bank = take(pe)
                    w = min(BANK, (t + 1) * P - c * BANK)
                    diagonal = c == t * P // BANK
                    last = nc.tensor.matmul(bank[:, 0:w], qs[0:NCOMB * AD, g % NBUF, j, t * P:(t + 1) * P],
                                            ks[0:NCOMB * AD, g % NBUF, j, c * BANK:c * BANK + w],
                                            start=True, stop=not diagonal, skip_group_check=True)
                    if diagonal:
                        last = nc.tensor.matmul(bank[:, w - P:w], k.identb[:, 0:P], k.causal[:], start=False,
                                                stop=True, skip_group_check=True)
                    last.then_inc(s.ring_ready, 1)

            def max_dve(dve, g, first, n):
                for t, j, c in PIECES[first:first + n]:
                    bank = give(dve)
                    w = min(BANK, (t + 1) * P - c * BANK)
                    nc.vector.tensor_reduce(nm[:, g % 2, t, j, c:c + 1], bank[:, 0:w], AX.X, ALU.max,
                                            negate=True).then_inc(s.ring_free, 1)

            def turn_max_pe(pe, g):
                pe.wait_ge(s.nm, g + 1)
                for n in range(NB):
                    bank = take(pe)
                    for i in range(BANK // P):
                        last = nc.tensor.transpose(bank[0:GH, i * P:(i + 1) * P],
                                                   nm[:, g % 2, n * (BANK // P) + i, :, 0], k.ident[:])
                    last.then_inc(s.ring_ready, 1)

            def turn_max_dve(dve, settle, g):
                late = nm[:, g % 2, BANK // P:T]
                dve.wait_ge(s.ring_free, dve_use[0])
                nc.vector.tensor_tensor(late[:, :, :, 0], late[:, :, :, 0], late[:, :, :, 1], ALU.min)\
                    .then_inc(s.nm, 1)
                if g >= 2:
                    dve.wait_ge(s.m_rows, 16 * 3 * (g - 1))
                for n in range(NB):
                    bank = give(dve)
                    cols = slice(n * BANK, (n + 1) * BANK)
                    settle(nc.vector.tensor_copy(mp[:, g % 2, 0, cols], bank[0:GH, :]))
                    nc.vector.tensor_tensor(mr[:], bank[0:GH, :], mp[:, g % 2, 0, cols], ALU.subtract)\
                        .then_inc(s.ring_free, 1)
                    dve.wait_ge(s.ring_free, dve_use[0])
                    settle(nc.vector.tensor_copy(mp[:, g % 2, 1, cols], mr[:]))
                    nc.vector.tensor_tensor(mp[:, g % 2, 2, cols], mr[:], mp[:, g % 2, 1, cols], ALU.subtract)\
                        .then_inc(s.m_parts, 1)

            def scores_pe(pe, g, st):
                n, kt = STEPS[st]
                if st == 0:
                    pe.wait_ge(s.m_rows, 16 * 3 * (g + 1))
                    if g == 0:
                        pe.wait_ge(s.v_out, T // 2)
                off = max(0, kt * P - n * BANK)
                unit = (g * len(STEPS) + st) * GH
                for j in range(GH):
                    if unit:
                        pe.wait_ge(s.exp, unit - GH + j + 1)
                    diagonal = kt * P >= n * BANK
                    last = nc.tensor.matmul(ps[:, RING + j, off:BANK], ks[0:QROWS, g % NBUF, j, kt * P:(kt + 1) * P],
                                            qs[0:QROWS, g % NBUF, j, n * BANK + off:(n + 1) * BANK],
                                            start=True, stop=not diagonal, skip_group_check=True)
                    if diagonal:
                        last = nc.tensor.matmul(ps[:, RING + j, off:off + P], k.identb[:, 0:P], k.causalT[:],
                                                start=False, stop=True, skip_group_check=True)
                    last.then_inc(s.scores, 1)

            def sums_pe(pe, g, st):
                n, kt = STEPS[st]
                off = max(0, kt * P - n * BANK)
                if kt == 0 and g * NB + n:
                    pe.wait_ge(s.o_out, g * NB + n)
                pe.wait_ge(s.exp, (g * len(STEPS) + st + 1) * GH)
                for j in range(GH):
                    head = (j % 2) * (AH // 2) + 2 * g + j // 2
                    last = nc.tensor.matmul(ps[2 * AD * j:2 * AD * j + AD + 1, 7, off:BANK], va[:, kt, head, :],
                                            pt[:, st % 2, j, off:BANK], start=(kt == 0),
                                            stop=(kt == (n + 1) * (BANK // P) - 1), skip_group_check=True)
                last.then_inc(s.sums, 1)

            def turn_sums_pe(pe, g, n):
                pe.wait_ge(s.o_out, g * NB + n + 1)
                bank = take(pe)
                for i in range(BANK // P):
                    last = nc.tensor.transpose(bank[:, i * P:(i + 1) * P], osb[:, i * P:(i + 1) * P], k.ident[:])
                last.then_inc(s.ring_ready, 1)

            def sums_dve(dve, g, n):
                dve.wait_ge(s.sums, g * len(STEPS) + (n + 1) * (BANK // P) + n * (BANK // P))
                nc.vector.tensor_copy(osb[:], ps[:, 7, :]).then_inc(s.o_out, 1)

            def turn_sums_dve(dve, settle, g, n):
                bank = give(dve).rearrange("p (i j c) -> p i j c", i=BANK // P, j=GH)
                settle(nc.vector.reciprocal(rec[:], bank[:, :, :, AD]))
                view = otm[:].rearrange("p t (a h d) -> p t a h d", a=HALVES, h=AH // 2)
                for hl in range(2):
                    last = nc.vector.tensor_tensor(view[:, n * (BANK // P):(n + 1) * (BANK // P), :, 2 * g + hl, :],
                                                   bank[:, :, 2 * hl:2 * hl + 2, 0:AD],
                                                   bc(rec[:, :, 2 * hl:2 * hl + 2], AD), ALU.mult)
                last.then_inc(s.ring_free, 1)

            with nc.Block() as block:
                @block.gpsimd
                def _(pool):
                    nc.gpsimd.memset(va[:, :, :, AD:AD + 1], 1.0).then_inc(s.const, 1)
                    pool.wait_ge(s.const, 1)
                    nc.gpsimd.memset(ks[NCOMB * AD:QROWS], 1.0).then_inc(s.const, 1)
                    pool.wait_ge(s.const, 2)
                    for u in range(2 * HALVES * NB):
                        i, a, n = u // (HALVES * NB), u // NB % HALVES, u % NB
                        cols = slice(n * BANK, (n + 1) * BANK)
                        pool.wait_ge(s.second, u + 1)
                        nc.gpsimd.tensor_tensor(parts[i][:, 2, a, cols], rest[:, u % 2, :], parts[i][:, 1, a, cols],
                                                ALU.subtract).then_inc(s.third, 1)

                @block.tensor
                def _(pe):
                    for u in range(2 * HALVES * NB):
                        i, a, n = u // (HALVES * NB), u // NB % HALVES, u % NB
                        if u >= 4:
                            pe.wait_ge(s.rest, u - 3)
                        for c in range(HALVES):
                            last = nc.tensor.matmul(ps[:, u % 4, :], k.wqkvT[:, c, i * D + a * P:i * D + (a + 1) * P],
                                                    k.xnT[:, c, n * BANK:(n + 1) * BANK],
                                                    start=(c == 0), stop=(c == HALVES - 1))
                        last.then_inc(s.qk_ps, 1)
                    for t in range(T):
                        for c in range(HALVES):
                            last = nc.tensor.matmul(ps[:, 4 + t // 2, (t % 2) * D:(t % 2 + 1) * D],
                                                    k.xnT[:, c, t * P:(t + 1) * P], k.wqkvT[:, c, 2 * D:3 * D],
                                                    start=(t % 2 == 0 and c == 0), stop=(c == HALVES - 1),
                                                    skip_group_check=True)
                        if t % 2:
                            last.then_inc(s.v_ps, 1)
                    max_pe(pe, 0, 0, len(PIECES))
                    turn_max_pe(pe, 0)
                    for g in range(AG):
                        for st in range(len(STEPS)):
                            scores_pe(pe, g, st)
                            if st:
                                sums_pe(pe, g, st - 1)
                            if g + 1 < AG:
                                max_pe(pe, g + 1, st * PER_STEP, PER_STEP)
                            if g and st == 1:
                                turn_sums_pe(pe, g - 1, 1)
                            if st == BANK // P + 1:
                                turn_sums_pe(pe, g, 0)
                        sums_pe(pe, g, len(STEPS) - 1)
                        if g + 1 < AG:
                            turn_max_pe(pe, g + 1)
                    turn_sums_pe(pe, AG - 1, 1)

                @block.scalar
                def _(act):
                    for u in range(2 * HALVES * NB):
                        i, a, n = u // (HALVES * NB), u // NB % HALVES, u % NB
                        cols = slice(n * BANK, (n + 1) * BANK)
                        act.wait_ge(s.qk_ps, u + 1)
                        nc.scalar.activation(parts[i][:, 0, a, cols], ps[:, u % 4, :], ACT.Copy).then_inc(s.first, 1)
                        act.wait_ge(s.rest, u + 1)
                        nc.scalar.activation(parts[i][:, 1, a, cols], rest[:, u % 2, :], ACT.Copy).then_inc(s.second, 1)
                    for u in range(T // 2):
                        act.wait_ge(s.v_ps, u + 1)
                        nc.scalar.activation(va[:, 2 * u:2 * u + 2, :, 0:AD],
                                             ps[:, 4 + u, :].rearrange("p (t h d) -> p t h d", t=2, h=AH),
                                             ACT.Copy).then_inc(s.v_out, 1)
                    act.wait_ge(s.third, 2 * HALVES * NB)
                    for g in range(AG):
                        for st, (n, kt) in enumerate(STEPS):
                            off = max(0, kt * P - n * BANK)
                            gs = g * len(STEPS) + st
                            if gs >= 2:
                                act.wait_ge(s.sums, gs - 1)
                            for j in range(GH):
                                act.wait_ge(s.scores, gs * GH + j + 1)
                                nc.scalar.activation(pt[:, st % 2, j, off:BANK], ps[:, RING + j, off:BANK], ACT.Exp,
                                                     scale=RATIO).then_inc(s.exp, 1)

                @block.vector
                def _(dve):
                    settle = chain_of(dve, s.dve)
                    for u in range(2 * HALVES * NB):
                        i, a, n = u // (HALVES * NB), u // NB % HALVES, u % NB
                        dve.wait_ge(s.first, u + 1)
                        if u >= 2:
                            dve.wait_ge(s.third, u - 1)
                        nc.vector.tensor_tensor(rest[:, u % 2, :], ps[:, u % 4, :],
                                                parts[i][:, 0, a, n * BANK:(n + 1) * BANK], ALU.subtract).then_inc(s.rest, 1)
                    max_dve(dve, 0, 0, len(PIECES))
                    turn_max_dve(dve, settle, 0)
                    for g in range(AG):
                        for st in range(len(STEPS)):
                            if g and st == 0:
                                sums_dve(dve, g - 1, 1)
                            if st == BANK // P:
                                sums_dve(dve, g, 0)
                            if g + 1 < AG:
                                max_dve(dve, g + 1, st * PER_STEP, PER_STEP)
                            if g and st == 1:
                                turn_sums_dve(dve, settle, g - 1, 1)
                            if st == BANK // P + 1:
                                turn_sums_dve(dve, settle, g, 0)
                        if g + 1 < AG:
                            turn_max_dve(dve, settle, g + 1)
                    sums_dve(dve, AG - 1, 1)
                    turn_sums_dve(dve, settle, AG - 1, 1)

                @block.sync
                def _(sp):
                    def stack(g):
                        if g >= NBUF:
                            sp.wait_ge(s.scores, (g - NBUF + 1) * len(STEPS) * GH)
                        for dst, src, order in ((qs, parts[0], Q_PARTS), (ks, parts[1], K_PARTS)):
                            for c in range(NCOMB):
                                for hl in range(2):
                                    sp.dma_start(dst[AD * c:AD * (c + 1), g % NBUF, 2 * hl:2 * hl + 2, :],
                                                 src[AD * (2 * g + hl):AD * (2 * g + hl + 1), order[c], :, :])\
                                        .then_inc(stacked[g], 16)

                    def rows(g):
                        sp.wait_ge(s.m_parts, NB * (g + 1))
                        for c in range(3):
                            sp.dma_start(qs[NCOMB * AD + c:NCOMB * AD + c + 1, g % NBUF, :, :],
                                         mp[:, g % 2, c, :]).then_inc(s.m_rows, 16)

                    sp.wait_ge(s.third, 2 * HALVES * NB)
                    for g in range(NBUF):
                        stack(g)
                    rows(0)
                    rows(1)
                    for g in range(NBUF, AG):
                        stack(g)
                    for g in range(2, AG):
                        rows(g)

        oT = sb("sa_ot", [P, HALVES, L])
        with nc.Block() as block:
            @block.tensor
            def _(pe):
                for n in range(NB):
                    for a in range(HALVES):
                        for i in range(BANK // P):
                            last = nc.tensor.transpose(ps[:, HALVES * n + a, i * P:(i + 1) * P],
                                                       otm[:, n * (BANK // P) + i, a * P:(a + 1) * P], k.ident[:])
                        last.then_inc(s.turned, 1)
                for t in range(T):
                    n = t // (BANK // P)
                    pe.wait_ge(s.ot0, n + 1)
                    pe.wait_ge(s.ot1, n + 1)
                    for a in range(HALVES):
                        last = nc.tensor.matmul(ps[:, 4 + t // 2, (t % 2) * D:(t % 2 + 1) * D], oT[:, a, t * P:(t + 1) * P],
                                                k.woutT[:, a, :], start=(t % 2 == 0 and a == 0), stop=(a == HALVES - 1),
                                                skip_group_check=True)
                    if t % 2:
                        last.then_inc(s.out, 1)

            @block.scalar
            def _(act):
                for n in range(NB):
                    act.wait_ge(s.turned, HALVES * n + 1)
                    nc.scalar.activation(oT[:, 0, n * BANK:(n + 1) * BANK], ps[:, HALVES * n, :], ACT.Copy).then_inc(s.ot0, 1)

            @block.vector
            def _(dve):
                for n in range(NB):
                    dve.wait_ge(s.turned, HALVES * n + 2)
                    nc.vector.tensor_copy(oT[:, 1, n * BANK:(n + 1) * BANK], ps[:, HALVES * n + 1, :]).then_inc(s.ot1, 1)
                for u in range(T // 2):
                    dve.wait_ge(s.out, u + 1)
                    xs = k.x1[:, 2 * u:2 * u + 2, :].rearrange("p t d -> p (t d)")
                    nc.vector.tensor_tensor(xs, xs, ps[:, 4 + u, :], ALU.add)
        nc.sync.sem_clear(range(stacked[0].num, stacked[-1].num + 1))
        clear(nc, s)



LN_SEMS = "x_in dve var rstd xn turned"
SEMS = {
    "ln": LN_SEMS,
    "su": "loaded all_in const dve prepared hs pe back",
    "pc": "padded proj pre conv silu beta tanh turned tm squared sums ss gram a blocks_out rep dve",
    "lc": "conv evac turned tm zeroed rnorm blocks inverse inverse_out inverse_in dve",
    "dr": "zeroed products square summed d_products d_square d_summed at_ps at5 at6 y5_ps z x_ps x10 t01 t23 y6_ps y6 t_ps t6 kq attn ks r u_ps u s_ps state o o_out dve",
    "ro": "feats ft_ps ft h1_ps h1 logits shifted exp dve",
    "mi": "part mixed weighted scale_in scale square sq_free normed turned ot0 ot1 out dve",
    "ff": "h_ps h logits shifted exp alpha gathered at_ps alphat gi git_ps git gates rz_in rz n_in n mem memt_ps memt "
          "values_ps values out x_out stored dve",
    "sa": "const first second third rest qk_ps v_ps v_out ring_ready ring_free nm m_parts m_rows scores exp sums o_out "
          "turned ot0 ot1 out dve",
}


def build(nc, w, y):
    with ExitStack() as ctx:
        def sb(name, shape, dt=F32):
            return ctx.enter_context(nc.sbuf_tensor(name, shape, dt))

        ps = ctx.enter_context(nc.psum_tensor("ps", [P, 8, BANK], F32))
        k = named(
            "Constants",
            wq=sb("wq", [P, HALVES, D]), wk=sb("wk", [P, HALVES, D]), wv=sb("wv", [P, HALVES, D]),
            wb=sb("wb", [P, HALVES, H]), cw=sb("cw", [P, 3, HALVES, 4]),
            stack=sb("stack", [P, (MID_STEPS + LOCAL_STEPS) * GROUPS, CG]),
            wo=sb("wo", [P, HALVES, D]), mixw=sb("mixw", [P, D]),
            rw1=sb("rw1", [P, 3, HID]), rb1=sb("rb1", [P, HC]), rw2=sb("rw2", [P, HC, H * PATHS]),
            rb2=sb("rb2", [P, H * PATHS]),
            ident=sb("ident", [P, P]), identb=sb("identb", [P, 4 * P], BF16),
            incl=sb("incl", [P, P]),
            causal=sb("causal", [P, P], BF16), causalT=sb("causalT", [P, P], BF16), ones2=sb("ones2", [P, 2]),
            invtau=sb("invtau", [P, 1]), w1x=sb("w1x", [P, HALVES, FH]), w2T=sb("w2T", [FH, SLOTS]),
            b2=sb("b2", [P, SLOTS]), wihT=sb("wihT", [P, HALVES, 3 * D]), hs=sb("hs", [SLOTS, D]),
            hbias=sb("hbias", [FH, 1]), grz=sb("grz", [SLOTS, 2 * D]), hn=sb("hn", [SLOTS, D]),
            bihn=sb("bihn", [SLOTS, D]), wvo=sb("wvo", [P, HALVES, D]), bvo=sb("bvo", [SLOTS, D]),
            wqkvT=sb("wqkvT", [P, HALVES, 3 * D]), woutT=sb("woutT", [P, HALVES, D]),
            mhalf=sb("mhalf", [P, 2 * T * H]),
            x1=sb("x1", [P, T, D]), xn=sb("xn", [P, T, D + 1]), xnT=sb("xnT", [P, HALVES, L]),
            stats=sb("stats", [P, T, 6]), mv=sb("mv", [P, T, 2]), vare=sb("vare", [P, T]), rstd=sb("rstd", [P, T]),
        )
        s = {n: sems(nc, ctx, n, names) for n, names in SEMS.items()}
        stacked = [ctx.enter_context(nc.semaphore(f"sa_stacked{g}")) for g in range(AG)]
        x_view = w["x"].rearrange("b (t p) d -> b p t d", p=P)
        y_view = y.rearrange("b (t p) d -> b p t d", p=P)
        bounce = nc.dram_tensor("bounce", [3, BLOCKS, T * H, CHUNK, CHUNK], F32, kind="Internal").ap()
        setup(nc, w, k, ps, s["su"])
        with nc.Fori(0, SEQS) as b:
            with ExitStack() as first:
                def sf(name, shape):
                    return first.enter_context(nc.sbuf_tensor(name, shape, F32))

                paths = sf("paths", [P, PATHS, T, D])
                m = named(
                    "DeltaTensors",
                    kT=sf("kT", [P, HALVES, L]), qT=sf("qT", [P, HALVES, L]),
                    paths=paths, local_tm=paths[:, 0], mid_tm=paths[:, 1], v_tm=paths[:, 2], delta_tm=paths[:, 3],
                    feats=k.xn[:, :, 0:FEATS],
                    k_tm=sf("k_tm", [P, T, D]), ev=sf("ev", [P, T, D]),
                    beta=sf("beta", [P, T * H]), ss=sf("ss", [P, 2, T * H]),
                    rn=sf("rn", [P, 2, T * H]), negd=sf("negd", [P, T * H]), e=sf("e", [P, T * H]),
                    prob=sf("prob", [P, T * H, PATHS]))
                layer_norm(nc, k, ps, s["ln"], k.x1, load=x_view[b])
                with ExitStack() as inner:
                    pre = inner.enter_context(nc.sbuf_tensor("pre", [P, 2, HALVES, 3 + L], F32))
                    TT = pre[:].rearrange("p i a l -> p (i a l)")[:, 0:T * H * P].rearrange("p (t n) -> p t n", t=T)
                    A = inner.enter_context(nc.sbuf_tensor("A", [P, T, H * P], F32))
                    with nc.sbuf_tensor("rep", [P, GROUPS, PAD + L], F32) as rep:
                        project_and_convolve(nc, k, m, rep, pre, A, bounce, ps, s["pc"])
                        long_convolutions(nc, k, m, rep, TT, bounce, ps, s["lc"])
                    delta_rule(nc, k, m, A, TT, ps, s["dr"])
                route(nc, k, m, ps, s["ro"])
                mix_and_project(nc, k, m, ps, s["mi"])
            layer_norm(nc, k, ps, s["ln"], k.x1)
            slot_ffn(nc, k, ps, s["ff"], "ffa")
            layer_norm(nc, k, ps, s["ln"], k.x1)
            softmax_attention(nc, k, ps, s["sa"], stacked)
            layer_norm(nc, k, ps, s["ln"], k.x1)
            slot_ffn(nc, k, ps, s["ff"], "ffb", store=y_view[b])


def laid_out(inputs):
    def a(name):
        return np.asarray(inputs[name])

    def lags(w, taps, steps):
        padded = np.zeros((D, SHIFTS * steps), w.dtype)
        padded[:, :taps] = w[:, ::-1]
        return padded.reshape(GROUPS, CG, steps, SHIFTS).transpose(3, 1, 2, 0).reshape(P, steps * GROUPS)

    def rows(v, n):
        return np.broadcast_to(v.reshape(1, -1), (n, v.size))

    i, j = np.arange(P)[:, None], np.arange(P)[None, :]
    order = (0, 2, 6, 1, 3, 7, 8, 10, 12, 4, 5, 9, 11, 13)
    feature_rows = np.concatenate([np.arange(D)] + [D + n * H + np.arange(H) for n in order])
    own, ffn = "L0_attn_a_", "L0_ffn_"
    out = {
        "x": a(own + "hidden_states"), "Wq": a(own + "Wq"), "Wk": a(own + "Wk"), "Wv": a(own + "Wv"), "Wb": a(own + "Wb"),
        "cw": np.stack([a(own + f"conv_{n}_w") for n in "qkv"]),
        "taps": np.concatenate([lags(a(own + "mid_w"), MID, MID_STEPS), lags(a(own + "local_w"), LOCAL, LOCAL_STEPS)], 1),
        "eye32": np.tile(np.eye(CG, dtype=np.float32), (SHIFTS, 1)),
        "Wo": a(own + "Wo"), "onorm": np.tile(a(own + "onorm_w"), P // DH)[:, None],
        "mixw": rows(a(own + "mix_w"), P),
        "rw1": a(own + "r_w1")[feature_rows], "rb1": a(own + "r_b1"), "rw2": a(own + "r_w2"), "rb2": rows(a(own + "r_b2"), P),
        "ident": np.eye(P, dtype=np.float32),
        "identb": np.tile(np.eye(P, dtype=np.float32), (1, 4)),
        "incl": (j >= i).astype(np.float32),
        "causal": np.where(j > i, NEG, 0.0).astype(np.float32),
        "causalT": np.where(i > j, NEG, 0.0).astype(np.float32),
        "ones2": ((i // DH) == j[:, 0:2]).astype(np.float32),
        "tau": rows(a(ffn + "tau"), P), "slot_init": a(ffn + "slot_init"), "slot_scale": a(ffn + "slot_scale"),
        "w1T": a(ffn + "w1").T, "b1": a(ffn + "b1")[:, None], "w2T": a(ffn + "w2").T, "b2": rows(a(ffn + "b2"), P),
        "wihT": a(ffn + "gru_wih").T, "whhT": a(ffn + "gru_whh").T,
        "bih": rows(a(ffn + "gru_bih"), SLOTS), "bhh": rows(a(ffn + "gru_bhh"), SLOTS),
        "wv": a(ffn + "wv"), "woT": a(ffn + "wo").T,
        "bvb": np.broadcast_to(a(ffn + "bv")[:, None], (D, SLOTS)), "bo": rows(a(ffn + "bo"), SLOTS),
        "wqkvT": a("L0_attn_b_w_qkv").T, "woutT": a("L0_attn_b_w_out").T,
    }
    return {n: np.ascontiguousarray(v) for n, v in out.items()}


def kernel(**inputs):
    import concourse.bacc as bacc
    from concourse.bass_utils import run_bass_kernel_spmd

    nc = bacc.Bacc("TRN2", target_bir_lowering=False, num_devices=1)
    arrays = {f"in_{n}": v for n, v in laid_out(inputs).items()}
    w = {n[3:]: nc.dram_tensor(n, v.shape, mybir.dt.from_np(v.dtype), kind="ExternalInput").ap() for n, v in arrays.items()}
    y = nc.dram_tensor("out_y", (SEQS, L, D), F32, kind="ExternalOutput").ap()
    build(nc, w, y)
    r = run_bass_kernel_spmd(nc, [arrays], core_ids=[0])
    return r.results[0]["out_y"]
```

```python
from collections import namedtuple
from contextlib import ExitStack

import numpy as np

import concourse.bass as bass
from concourse import mybir

ALU = mybir.AluOpType
ACT = mybir.ActivationFunctionType
AX = mybir.AxisListType
F32 = mybir.dt.float32
BF16 = mybir.dt.bfloat16

P = 128
SEQS, L, D = 16, 1024, 256
T = L // P
HALVES = D // P
BANK = 512
NB = L // BANK
H, DH = 4, 64
MID, LOCAL = 25, 7
SHIFTS, CG = 4, 32
GROUPS = D // CG
MID_STEPS, LOCAL_STEPS = -(-MID // SHIFTS), -(-LOCAL // SHIFTS)
PAD = SHIFTS * (MID_STEPS - 1)
PATHS = 4
FEATS = 14 * H
HID = 2 * (D + FEATS)
HC = -(-HID // P)
HLAST = HID - (HC - 1) * P
FLOOR = 0.01
EPS = 1e-5
SLOTS, FH, TOPK = 64, 128, 8
AH, AD = 16, 16
NCOMB = 6
QROWS = NCOMB * AD + 3
NEG = -1.0e30
CHUNK = 32
BLOCKS = P // CHUNK


def chain_of(eng, sem):
    count = [0]

    def settle(ins):
        count[0] += 1
        ins.then_inc(sem, 1)
        eng.wait_ge(sem, count[0])

    return settle


def bc(ap, n):
    return ap.unsqueeze(len(ap.shape)).to_broadcast(list(ap.shape) + [n])


def named(kind, **things):
    return namedtuple(kind, things)(**things)


def by_blocks(ap, n):
    return ap[:].rearrange("p t (h n) -> p (t h) n", n=n)


def sems(nc, ctx, prefix, names, common=()):
    own = {n: ctx.enter_context(nc.semaphore(f"{prefix}_{n}")) for n in names.split()}
    return named("Semaphores", **own, **{n: x for n, x in zip(COMMON.split(), common)})


def clear(nc, s):
    nums = sorted(x.num for x in s)
    first = nums[0]
    for here, after in zip(nums, nums[1:] + [None]):
        if after != here + 1:
            nc.sync.sem_clear(range(first, here + 1))
            first = after



def setup(nc, w, k, ps, s):
    with ExitStack() as tmp:
        def sb(name, shape, dt=F32):
            return tmp.enter_context(nc.sbuf_tensor(name, shape, dt))

        taps = sb("su_taps", [P, (MID_STEPS + LOCAL_STEPS) * GROUPS])
        eye32 = sb("su_eye32", [P, CG])
        wo_raw = sb("su_wo", [P, HALVES, D])
        onorm = sb("su_onorm", [P, 1])
        tau = sb("su_tau", [P, 3])
        b_raw = sb("su_b_raw", [P, 6 * P])
        slot_init = sb("su_slot", [SLOTS, D])
        slot_scale = sb("su_scale", [SLOTS, 1])
        w1s = sb("su_w1s", [P, HALVES, FH])
        b1 = sb("su_b1", [FH, 1])
        mean64 = sb("su_mean", [SLOTS, 1])
        slot_mean = sb("su_smean", [P, HALVES])
        hsT = sb("su_hsT", [P, HALVES, SLOTS])
        whhT = sb("su_whhT", [P, HALVES, 3 * D])
        bih = sb("su_bih", [SLOTS, 3 * D])
        bhh = sb("su_bhh", [SLOTS, 3 * D])
        wv = sb("su_wv", [P, HALVES, D])
        woT = sb("su_woT", [P, HALVES, D])
        bvb = sb("su_bvb", [P, HALVES, SLOTS])
        bo = sb("su_bo", [SLOTS, D])

        with nc.Block() as block:
            @block.sync
            def _(sp):
                loads = [
                    (k.wq, w["Wq"].rearrange("(k p) n -> p k n", p=P)),
                    (k.wk, w["Wk"].rearrange("(k p) n -> p k n", p=P)),
                    (k.wv, w["Wv"].rearrange("(k p) n -> p k n", p=P)),
                    (k.wb, w["Wb"].rearrange("(k p) n -> p k n", p=P)),
                    (k.cw, w["cw"].rearrange("s (a p) t -> p s a t", p=P)),
                    (taps, w["taps"]), (eye32, w["eye32"]),
                    (wo_raw, w["Wo"].rearrange("(k p) n -> p k n", p=P)),
                    (onorm, w["onorm"]), (k.mixw, w["mixw"]),
                    (k.rw1[:, 0:2, :], w["rw1"][0:D].rearrange("(k p) n -> p k n", p=P)),
                    (k.rw1[0:FEATS, 2, :], w["rw1"][D:D + FEATS]),
                    (k.rb1[:, 0:HC - 1], w["rb1"][0:(HC - 1) * P].rearrange("(k p) -> p k", p=P)),
                    (k.rb1[0:HLAST, HC - 1:HC], w["rb1"][(HC - 1) * P:HID].rearrange("(p k) -> p k", k=1)),
                    (k.rw2[:, 0:HC - 1, :], w["rw2"][0:(HC - 1) * P].rearrange("(k p) n -> p k n", p=P)),
                    (k.rw2[0:HLAST, HC - 1, :], w["rw2"][(HC - 1) * P:HID]),
                    (k.rb2, w["rb2"]),
                    (k.ident, w["ident"]), (b_raw[:, 0:4 * P], w["identb"]),
                    (k.incl, w["incl"]),
                    (b_raw[:, 4 * P:5 * P], w["causal"]), (b_raw[:, 5 * P:], w["causalT"]),
                    (k.ones2, w["ones2"]),
                    (tau[:, 0:1], w["tau"]), (slot_init, w["slot_init"]), (slot_scale, w["slot_scale"]),
                    (k.w1x, w["w1T"][0:D].rearrange("(k p) n -> p k n", p=P)),
                    (w1s, w["w1T"][D:2 * D].rearrange("(k p) n -> p k n", p=P)),
                    (b1, w["b1"]), (k.w2T, w["w2T"]), (k.b2, w["b2"]),
                    (k.wihT, w["wihT"].rearrange("(k p) n -> p k n", p=P)),
                    (whhT, w["whhT"].rearrange("(k p) n -> p k n", p=P)),
                    (bih, w["bih"]), (bhh, w["bhh"]),
                    (wv, w["wv"].rearrange("(k p) n -> p k n", p=P)),
                    (woT, w["woT"].rearrange("(k p) n -> p k n", p=P)),
                    (bvb, w["bvb"].rearrange("(k p) n -> p k n", p=P)), (bo, w["bo"]),
                    (k.wqkvT, w["wqkvT"].rearrange("(k p) n -> p k n", p=P)),
                    (k.woutT, w["woutT"].rearrange("(k p) n -> p k n", p=P)),
                ]
                for dst, src in loads:
                    dst = dst if isinstance(dst, bass.AP) else dst[:]
                    sp.dma_start(dst, src, allow_slow_non_contiguous=True).then_inc(s.loaded, 16)
                sp.wait_ge(s.loaded, 16 * len(loads))
                sp.sem_inc(s.all_in, 1)

            @block.gpsimd
            def _(pool):
                nc.gpsimd.memset(mean64[:], 1.0 / SLOTS).then_inc(s.const, 1)
                nc.gpsimd.memset(k.mhalf[:], -0.5).then_inc(s.const, 1)
                nc.gpsimd.memset(k.xn[:, :, D:D + 1], 1.0).then_inc(s.const, 1)

            @block.vector
            def _(dve):
                settle = chain_of(dve, s.dve)
                dve.wait_ge(s.all_in, 1)
                nc.vector.tensor_tensor(k.stack[:].rearrange("p n c -> p n c"), bc(taps[:], CG),
                                        eye32[:].unsqueeze(1).to_broadcast([P, (MID_STEPS + LOCAL_STEPS) * GROUPS, CG]),
                                        ALU.mult).then_inc(s.prepared, 1)
                for a in range(HALVES):
                    nc.vector.tensor_scalar(k.wo[:, a, :], wo_raw[:, a, :], onorm[:, 0:1], None,
                                            ALU.mult).then_inc(s.prepared, 1)
                nc.vector.tensor_copy(k.identb[:], b_raw[:, 0:4 * P]).then_inc(s.prepared, 1)
                nc.vector.tensor_copy(k.causal[:], b_raw[:, 4 * P:5 * P]).then_inc(s.prepared, 1)
                nc.vector.tensor_copy(k.causalT[:], b_raw[:, 5 * P:]).then_inc(s.prepared, 1)
                settle(nc.vector.tensor_scalar(tau[:, 1:2], tau[:, 0:1], -1.0, None, ALU.mult))
                settle(nc.vector.tensor_tensor(tau[:, 2:3], tau[:, 0:1], tau[:, 1:2], ALU.max))
                settle(nc.vector.tensor_scalar(tau[:, 1:2], tau[:, 2:3], 0.1, None, ALU.add))
                settle(nc.vector.reciprocal(k.invtau[:], tau[:, 1:2]))
                nc.vector.tensor_scalar(k.hs[:], slot_init[:], slot_scale[:, 0:1], None, ALU.mult).then_inc(s.hs, 1)
                nc.vector.tensor_tensor(k.bihn[:], bih[:, 2 * D:], bih[:, 2 * D:], ALU.max).then_inc(s.prepared, 1)
                dve.wait_ge(s.pe, 1)
                nc.vector.tensor_copy(slot_mean[:], ps[:, 0, 0:HALVES]).then_inc(s.back, 1)
                dve.wait_ge(s.pe, 2)
                nc.vector.tensor_copy(hsT[:].rearrange("p a s -> p (a s)"), ps[:, 1, 0:HALVES * SLOTS]).then_inc(s.back, 1)
                dve.wait_ge(s.pe, 3)
                nc.vector.tensor_tensor(k.hbias[:], ps[0:FH, 2, 0:1], b1[:], ALU.add).then_inc(s.prepared, 1)
                dve.wait_ge(s.pe, 4)
                settle(nc.vector.tensor_tensor(k.grz[:], ps[0:SLOTS, 3, 0:2 * D], bhh[:, 0:2 * D], ALU.add))
                settle(nc.vector.tensor_tensor(k.grz[:], k.grz[:], bih[:, 0:2 * D], ALU.add))
                settle(nc.vector.tensor_tensor(k.hn[:], ps[0:SLOTS, 4, 0:D], bhh[:, 2 * D:], ALU.add))
                dve.wait_ge(s.pe, 5)
                for a in range(HALVES):
                    settle(nc.vector.tensor_copy(k.wvo[:, a, :], ps[:, 5 + a, 0:D]))
                settle(nc.vector.tensor_tensor(k.bvo[:], ps[0:SLOTS, 7, 0:D], bo[:], ALU.add))

            @block.tensor
            def _(pe):
                pe.wait_ge(s.hs, 1)
                pe.wait_ge(s.const, 3)
                for a in range(HALVES):
                    last = nc.tensor.matmul(ps[:, 0, a:a + 1], k.hs[:, a * P:(a + 1) * P], mean64[:],
                                            start=(a == 0), stop=(a == HALVES - 1), skip_group_check=True)
                last.then_inc(s.pe, 1)
                for a in range(HALVES):
                    last = nc.tensor.transpose(ps[:, 1, a * SLOTS:(a + 1) * SLOTS], k.hs[:, a * P:(a + 1) * P],
                                               k.ident[0:SLOTS, 0:SLOTS])
                last.then_inc(s.pe, 1)
                pe.wait_ge(s.back, 1)
                for a in range(HALVES):
                    last = nc.tensor.matmul(ps[0:FH, 2, 0:1], w1s[:, a, :], slot_mean[:, a:a + 1],
                                            start=(a == 0), stop=(a == HALVES - 1))
                last.then_inc(s.pe, 1)
                pe.wait_ge(s.back, 2)
                for a in range(HALVES):
                    nc.tensor.matmul(ps[0:SLOTS, 3, 0:2 * D], hsT[:, a, :], whhT[:, a, 0:2 * D],
                                     start=(a == 0), stop=(a == HALVES - 1))
                for a in range(HALVES):
                    last = nc.tensor.matmul(ps[0:SLOTS, 4, 0:D], hsT[:, a, :], whhT[:, a, 2 * D:],
                                            start=(a == 0), stop=(a == HALVES - 1))
                last.then_inc(s.pe, 1)
                for c in range(HALVES):
                    for a in range(HALVES):
                        nc.tensor.matmul(ps[:, 5 + c, 0:D], wv[:, a, c * P:(c + 1) * P], woT[:, a, :],
                                         start=(a == 0), stop=(a == HALVES - 1))
                for a in range(HALVES):
                    last = nc.tensor.matmul(ps[0:SLOTS, 7, 0:D], bvb[:, a, :], woT[:, a, :],
                                            start=(a == 0), stop=(a == HALVES - 1))
                last.then_inc(s.pe, 1)
    clear(nc, s)



def norm_statistics(nc, k, s, settle, x, u):
    pair = slice(2 * u, 2 * u + 2)
    for t in (2 * u, 2 * u + 1):
        last = nc.vector.bn_stats(k.stats[:, t, :], x[:, t, :])
    settle(last)
    for t in (2 * u, 2 * u + 1):
        last = nc.vector.bn_aggr(k.mv[:, t, :], k.stats[:, t, :])
    settle(last)
    nc.vector.tensor_scalar(k.negm[:, pair], k.mv[:, pair, 0], -1.0, None, ALU.mult).then_inc(s.var, 1)
    nc.vector.tensor_scalar(k.vare[:, pair], k.mv[:, pair, 1], EPS, None, ALU.add).then_inc(s.var, 1)


def inverse_deviations(nc, k, s, pool):
    for u in range(T // 2):
        pair = slice(2 * u, 2 * u + 2)
        pool.wait_ge(s.var, 2 * (u + 1))
        nc.gpsimd.tensor_tensor(k.rstd[:, pair], k.vare[:, pair], k.mhalf[:, 0:2], ALU.pow).then_inc(s.rstd, 1)
        pool.wait_ge(s.rstd, 2 * u + 1)
        nc.gpsimd.tensor_tensor(k.shift[:, pair], k.rstd[:, pair], k.negm[:, pair], ALU.mult).then_inc(s.rstd, 1)


def normalise(nc, k, s, act, x):
    for t in range(T):
        act.wait_ge(s.rstd, 2 * (t // 2 + 1))
        nc.scalar.activation(k.xn[:, t, 0:D], x[:, t, :], ACT.Identity, bias=k.shift[:, t:t + 1],
                             scale=k.rstd[:, t:t + 1])


def add_with_statistics(nc, k, s, dve, settle, out):
    for u in range(T // 2):
        dve.wait_ge(s.out, u + 1)
        xs = k.x1[:, 2 * u:2 * u + 2, :].rearrange("p t d -> p (t d)")
        settle(nc.vector.tensor_tensor(xs, xs, out(u), ALU.add))
        norm_statistics(nc, k, s, settle, k.x1, u)



def turn_normed_pe(nc, k, ps, s):
    for n in range(NB):
        for a in range(HALVES):
            for i in range(BANK // P):
                last = nc.tensor.transpose(ps[:, 4 + HALVES * n + a, i * P:(i + 1) * P],
                                           k.xn[:, n * (BANK // P) + i, a * P:(a + 1) * P], k.ident[:])
            last.then_inc(s.xn_turned, 1)


def turn_normed_act(nc, k, ps, s, act):
    for n in range(NB):
        act.wait_ge(s.xn_turned, HALVES * n + 1)
        nc.scalar.activation(k.xnT[:, 0, n * BANK:(n + 1) * BANK], ps[:, 4 + HALVES * n, :], ACT.Copy).then_inc(s.xn0, 1)


def turn_normed_dve(nc, k, ps, s, dve):
    for n in range(NB):
        dve.wait_ge(s.xn_turned, HALVES * n + 2)
        nc.vector.tensor_copy(k.xnT[:, 1, n * BANK:(n + 1) * BANK], ps[:, 4 + HALVES * n + 1, :]).then_inc(s.xn1, 1)


def first_norm(nc, k, s, io):
    with nc.Block() as block:
        @block.scalar
        def _(act):
            act.wait_ge(io.loaded, 16)
            act.wait_ge(io.stored, 16)
            nc.scalar.activation(k.x1[:].rearrange("p t d -> p (t d)"), k.x0[:].rearrange("p t d -> p (t d)"), ACT.Copy)
            normalise(nc, k, s, act, k.x0)

        @block.vector
        def _(dve):
            settle = chain_of(dve, s.dve)
            dve.wait_ge(io.loaded, 16)
            for u in range(T // 2):
                norm_statistics(nc, k, s, settle, k.x0, u)

        @block.gpsimd
        def _(pool):
            inverse_deviations(nc, k, s, pool)
    nc.sync.sem_clear(range(io.loaded.num, io.stored.num + 1))
    clear(nc, s)



def early_features(m):
    return m.prob[:].rearrange("p n c -> p (n c)").rearrange("p (t f h) -> p t f h", t=T, h=H)


def substitution_tensors(m):
    def two_squares(ap):
        flat = ap.rearrange("p t d -> p (t d)").rearrange("p (s i j) -> p s i j", i=CHUNK, j=CHUNK)
        return flat[:, 0], flat[:, 1]

    return two_squares(m.delta_tm) + two_squares(m.local_tm)


EARLY_ROWS = 10


def substitute(nc, dve, settle, m, rows):
    block_a, product, X, _ = substitution_tensors(m)
    for i in rows:
        settle(nc.vector.tensor_tensor(product[:, 0:i, 0:i], block_a[:, i:i + 1, 0:i].to_broadcast([P, i, i]),
                                       X[:, 0:i, 0:i].rearrange("p j c -> p c j"), ALU.mult))
        last = nc.vector.tensor_reduce(X[:, i, 0:i], product[:, 0:i, 0:i], AX.X, ALU.add)
        if i < rows[-1]:
            settle(last)
    return last


def project_and_convolve(nc, k, m, rep, pre, A, bounce, ps, s):
    def channel_major(ap):
        return ap.rearrange("p t d -> p (t d)").rearrange("p (a l) -> p a l", a=HALVES)

    vT, acc = channel_major(m.delta_tm), channel_major(m.ev[:])
    sq = [channel_major(m.local_tm), channel_major(m.mid_tm)]
    outs = [m.kT, vT, m.qT]
    AB = 6
    TAPS = (1, 2, 0)
    GRAM = (4, 0, 2, 4)
    BETA, SS = slice(0, T * H), (slice(2 * T * H, 3 * T * H), slice(4 * T * H, 5 * T * H))
    with nc.Block() as block:
        @block.gpsimd
        def _(pool):
            nc.gpsimd.memset(pre[:, :, :, 0:3], 0.0).then_inc(s.padded, 1)
            pool.wait_ge(s.padded, 1)
            nc.gpsimd.memset(rep[:, :, 0:PAD + SHIFTS - 1], 0.0).then_inc(s.padded, 1)
            X = substitution_tensors(m)[2]
            pool.wait_ge(s.sums, 1)
            nc.gpsimd.memset(X, 0.0).then_inc(s.unit, 1)
            pool.wait_ge(s.unit, 1)
            nc.gpsimd.memset(X.rearrange("p i j -> p (i j)")[:, 0:CHUNK * CHUNK:CHUNK + 1], 1.0).then_inc(s.unit, 1)

        @block.sync
        def _(sp):
            sp.wait_ge(s.padded, 2)
            sp.wait_ge(s.silu, 2 * HALVES)
            for sh in range(SHIFTS):
                for g in range(P // CG):
                    sp.dma_start(rep[CG * sh:CG * (sh + 1), g::P // CG, PAD + sh:PAD + L],
                                 vT[CG * g:CG * (g + 1), :, 0:L - sh]).then_inc(s.rep, 16)
            sp.wait_ge(s.a, T)
            for b in range(BLOCKS):
                part = slice(CHUNK * b, CHUNK * (b + 1))
                sp.dma_start(bounce[0, b].rearrange("g r c -> r g c"),
                             by_blocks(A, P)[part, :, part]).then_inc(s.blocks_out, 16)
            sp.wait_ge(s.rep, 16 * SHIFTS * (P // CG))
            sp.wait_ge(s.blocks_out, 16 * BLOCKS)
            block_a = substitution_tensors(m)[0]
            sp.wait_ge(s.turned, T)
            sp.dma_start(block_a, bounce[0].rearrange("b g r c -> (b g) r c")).then_inc(s.blocks, 16)

        @block.tensor
        def _(pe):
            def to_token_major(i):
                pe.wait_ge(s.silu, HALVES * (i + 1))
                if i == 0:
                    pe.wait_ge(s.a, 6)
                for u in range(T // 2):
                    if i == 1:
                        pe.wait_ge(s.tm, u + 1)
                    for j in range(2):
                        for a in range(HALVES):
                            last = nc.tensor.transpose(ps[:, u, j * D + a * P:j * D + (a + 1) * P],
                                                       outs[i][:, a, (2 * u + j) * P:(2 * u + j + 1) * P], k.ident[:])
                    last.then_inc(s.turned, 1)

            def sums_of_squares(i):
                for a in range(HALVES):
                    pe.wait_ge(s.squared, HALVES * i + a + 1)
                    for t in range(T):
                        first = SS[i].start + t * H + 2 * a
                        last = nc.tensor.matmul(ps[:, AB, first:first + 2], sq[i][:, a, t * P:(t + 1) * P], k.ones2[:],
                                                start=False, stop=True, skip_group_check=True)
                last.then_inc(s.sums, 1)

            turn_normed_pe(nc, k, ps, s)
            for i, w in enumerate((k.wk, k.wv, k.wq)):
                for a in range(HALVES):
                    for n in range(NB):
                        u = (i * HALVES + a) * NB + n
                        if u < NB:
                            pe.wait_ge(s.xn0, n + 1)
                            pe.wait_ge(s.xn1, n + 1)
                        if u >= 4:
                            pe.wait_ge(s.pre, u - 3)
                        for c in range(HALVES):
                            last = nc.tensor.matmul(ps[:, u % 4, :], w[:, c, a * P:(a + 1) * P],
                                                    k.xnT[:, c, n * BANK:(n + 1) * BANK],
                                                    start=(c == 0), stop=(c == HALVES - 1))
                        last.then_inc(s.proj, 1)
            for t in range(T):
                for c in range(HALVES):
                    last = nc.tensor.matmul(ps[:, AB, t * H:(t + 1) * H], k.xnT[:, c, t * P:(t + 1) * P],
                                            k.wb[:, c, :], start=(t == 0 and c == 0), stop=(c == HALVES - 1),
                                            skip_group_check=True)
            last.then_inc(s.beta, 1)
            pe.wait_ge(s.tanh, 1)
            sums_of_squares(0)
            pe.wait_ge(s.pre, 3 * HALVES * NB)
            for u in range(T // 2):
                if u == 3:
                    pe.wait_ge(s.a, 2)
                for j in range(2):
                    t = 2 * u + j
                    for h in range(H):
                        part = slice(DH * (h % 2), DH * (h % 2) + DH)
                        kt = m.kT[part, h // 2, t * P:(t + 1) * P]
                        col = (2 * j + h // 2) * P
                        last = nc.tensor.matmul(ps[:, GRAM[u] + h % 2, col:col + P], kt, kt,
                                                start=(j == 0 and h < 2), stop=True, skip_group_check=True)
                last.then_inc(s.gram, 1)
            to_token_major(0)
            pe.wait_ge(s.ss, 1)
            sums_of_squares(1)
            to_token_major(1)

        @block.scalar
        def _(act):
            def evacuate(i, halves=range(HALVES)):
                for a in halves:
                    for n in range(NB):
                        u = (i * HALVES + a) * NB + n
                        act.wait_ge(s.proj, u + 1)
                        if i == 2:
                            act.wait_ge(s.conv, a + 1)
                        nc.scalar.activation(pre[:, i % 2, a, 3 + n * BANK:3 + (n + 1) * BANK], ps[:, u % 4, :],
                                             ACT.Copy).then_inc(s.pre, 1)

            def silu(i, halves=range(HALVES)):
                for a in halves:
                    act.wait_ge(s.conv, HALVES * i + a + 1)
                    nc.scalar.activation(outs[i][:, a, :], acc[:, a, :], ACT.Silu).then_inc(s.silu, 1)

            def square(i):
                act.wait_ge(s.silu, HALVES * (2 * i + 1))
                for a in range(HALVES):
                    nc.scalar.activation(sq[i][:, a, :], outs[2 * i][:, a, :], ACT.Square).then_inc(s.squared, 1)

            def first_tap(i, a):
                act.wait_ge(s.padded, 1)
                act.wait_ge(s.pre, (i * HALVES + a + 1) * NB)
                if i:
                    act.wait_ge(s.silu, HALVES * (i - 1) + a + 1)
                nc.scalar.activation(acc[:, a, :], pre[:, i % 2, a, 0:L], ACT.Copy,
                                     scale=k.cw[:, TAPS[i], a, 0:1]).then_inc(s.tap, 1)

            def to_token_major(i, dst):
                for u in range(T // 2):
                    act.wait_ge(s.turned, i * (T // 2) + u + 1)
                    nc.scalar.activation(dst[:, 2 * u:2 * u + 2, :].rearrange("p t d -> p (t d)"), ps[:, u, :],
                                         ACT.Copy).then_inc(s.tm, 1)

            turn_normed_act(nc, k, ps, s, act)
            for a in range(HALVES):
                evacuate(0, (a,))
                first_tap(0, a)
            evacuate(1)
            for a in range(HALVES):
                silu(0, (a,))
                first_tap(1, a)
            square(0)
            evacuate(2)
            act.wait_ge(s.beta, 1)
            nc.scalar.activation(m.beta[:], ps[:, AB, BETA], ACT.Tanh, scale=0.5).then_inc(s.tanh, 1)
            for a in range(HALVES):
                silu(1, (a,))
                first_tap(2, a)
            silu(2)
            to_token_major(0, m.k_tm[:])
            square(1)
            to_token_major(1, m.v_tm)

        @block.vector
        def _(dve):
            settle = chain_of(dve, s.dve)

            def convolve(i, halves=range(HALVES)):
                tap = TAPS[i]
                for a in halves:
                    dve.wait_ge(s.tap, HALVES * i + a + 1)
                    src = pre[:, i % 2, a, :]
                    for j in range(1, 4):
                        ins = nc.vector.scalar_tensor_tensor(acc[:, a, :], src[:, j:j + L], k.cw[:, tap, a, j:j + 1],
                                                             acc[:, a, :], ALU.mult, ALU.add)
                        if j < 3:
                            settle(ins)
                        else:
                            ins.then_inc(s.conv, 1)

            turn_normed_dve(nc, k, ps, s, dve)
            dve.wait_ge(s.padded, 1)
            convolve(0)
            convolve(1)
            dve.wait_ge(s.tanh, 1)
            settle(nc.vector.tensor_scalar(m.beta[:], m.beta[:], 0.5, 0.5, ALU.mult, ALU.add))
            dve.wait_ge(s.sums, 1)
            nc.vector.tensor_scalar(m.ss[:, 0, :], ps[:, AB, SS[0]], 1e-12, None, ALU.add).then_inc(s.ss, 1)
            dve.wait_ge(s.ss, 1)
            settle(nc.vector.reciprocal(m.negd[:], m.ss[:, 0, :]))
            settle(nc.vector.tensor_tensor(m.negd[:], m.negd[:], m.beta[:], ALU.mult))
            settle(nc.vector.tensor_scalar(m.negd[:], m.negd[:], -1.0, None, ALU.mult))
            for half in range(HALVES):
                convolve(2, (half,))
                for u in (2 * half, 2 * half + 1):
                    dve.wait_ge(s.gram, u + 1)
                    for odd in range(2):
                        nc.vector.tensor_tensor(
                            by_blocks(A, P)[:, 2 * u * H + odd:(2 * u + 2) * H:2],
                            ps[:, GRAM[u] + odd, :].rearrange("p (g n) -> p g n", n=P),
                            bc(m.negd[:, 2 * u * H + odd:(2 * u + 2) * H:2], P), ALU.mult).then_inc(s.a, 1)
            dve.wait_ge(s.sums, 2)
            nc.vector.tensor_scalar(m.ss[:, 1, :], ps[:, AB, SS[1]], 1e-12, None, ALU.add)
            dve.wait_ge(s.blocks, 16)
            dve.wait_ge(s.unit, 2)
            substitute(nc, dve, settle, m, range(1, EARLY_ROWS))
    clear(nc, s)


def long_convolutions(nc, k, m, rep, TT, bounce, ps, s):
    Xd = m.delta_tm
    block_a, product, X, XT = substitution_tensors(m)

    def out_cm(a, col, n):
        r, c = 4 * a + col // D, col % D
        return k.xn[:, r:r + n // D, 0:D] if n >= D else k.xn[:, r, c:c + n]

    units = [(c, a, n) for c in range(2) for a in range(HALVES) for n in range(NB)]

    def rows(b):
        return slice(CHUNK * b, CHUNK * (b + 1))

    with nc.Block() as block:
        @block.gpsimd
        def _(pool):
            nc.gpsimd.memset(TT, 0.0).then_inc(s.zeroed, 1)
            nc.gpsimd.tensor_tensor(m.rn[:], m.ss[:], k.mhalf[:].rearrange("p (i n) -> p i n", i=2),
                                    ALU.pow).then_inc(s.rnorm, 1)
            pool.wait_ge(s.inverse, 1)
            nc.gpsimd.memset(Xd[:], 0.0).then_inc(s.zeroed, 1)

        @block.sync
        def _(sp):
            sp.wait_ge(s.inverse, 1)
            sp.dma_start(bounce[1].rearrange("b g r c -> (b g) r c"), X).then_inc(s.inverse_out, 16)
            sp.wait_ge(s.inverse, 2)
            sp.dma_start(bounce[2].rearrange("b g r c -> (b g) r c"), XT).then_inc(s.inverse_out, 16)
            sp.wait_ge(s.inverse_out, 32)
            sp.wait_ge(s.zeroed, 2)
            for b in range(BLOCKS):
                if b < 3:
                    left = CHUNK * (b % 2)
                    sp.dma_start(by_blocks(Xd, 2 * CHUNK)[rows(b), :, left:left + CHUNK],
                                 bounce[1, b].rearrange("g r c -> r g c")).then_inc(s.inverse_in, 16)
                sp.dma_start(by_blocks(TT, P)[rows(b), :, rows(b)],
                             bounce[2, b].rearrange("g r c -> r g c")).then_inc(s.inverse_in, 16)
            sp.wait_ge(s.inverse_in, 16 * (2 * BLOCKS - 1))

        @block.tensor
        def _(pe):
            for u, (c, a, n) in enumerate(units):
                steps, base = ((MID_STEPS, 0), (LOCAL_STEPS, MID_STEPS))[c]
                if u >= 4:
                    pe.wait_ge(s.evac, u - 3)
                for j in range(steps):
                    for g in range(P // CG):
                        gg = a * (P // CG) + g
                        last = nc.tensor.matmul(
                            ps[CG * g:CG * (g + 1), u % 4, :], k.stack[:, (base + j) * GROUPS + gg, :],
                            rep[:, gg, PAD + n * BANK - SHIFTS * j:PAD + (n + 1) * BANK - SHIFTS * j],
                            start=(j == 0), stop=(j == steps - 1))
                last.then_inc(s.conv, 1)
                if u % 4 == 3:
                    c = u // 4
                    pe.wait_ge(s.evac, u + 1)
                    for v in range(T // 2):
                        if c:
                            pe.wait_ge(s.tm, v + 1)
                        for j in range(2):
                            for aa in range(HALVES):
                                last = nc.tensor.transpose(
                                    ps[:, 4 + v, j * D + aa * P:j * D + (aa + 1) * P],
                                    out_cm(aa, (2 * v + j) * P, P), k.ident[:])
                        last.then_inc(s.turned, 1)

        @block.scalar
        def _(act):
            nc.scalar.activation(m.ev[:], m.v_tm, ACT.Square).then_inc(s.square, 1)
            for c, dst in enumerate((m.mid_tm, m.local_tm)):
                for u in range(4 * c, 4 * c + 4):
                    a, n = units[u][1:]
                    act.wait_ge(s.conv, u + 1)
                    nc.scalar.activation(out_cm(a, n * BANK, BANK), ps[:, u % 4, :].rearrange("p (r d) -> p r d", d=D),
                                         ACT.Copy).then_inc(s.evac, 1)
                    if u == 4:
                        act.wait_ge(s.summed, 1)
                        act.wait_ge(s.tm, T // 2)
                        nc.scalar.activation(m.ev[:], m.mid_tm, ACT.Square).then_inc(s.square, 1)
                if c:
                    act.wait_ge(s.inverse_out, 32)
                for v in range(T // 2):
                    act.wait_ge(s.turned, c * (T // 2) + v + 1)
                    nc.scalar.activation(dst[:, 2 * v:2 * v + 2, :].rearrange("p t d -> p (t d)"),
                                         ps[:, 4 + v, :], ACT.Copy).then_inc(s.tm, 1)

        @block.vector
        def _(dve):
            settle = chain_of(dve, s.dve)
            substitute(nc, dve, settle, m, range(EARLY_ROWS, CHUNK)).then_inc(s.inverse, 1)
            dve.wait_ge(s.inverse, 1)
            nc.vector.tensor_copy(XT, X.rearrange("p i j -> p j i")).then_inc(s.inverse, 1)
            early = early_features(m)
            for i, path in enumerate((m.v_tm, m.mid_tm)):
                dve.wait_ge(s.square, i + 1)
                nc.vector.tensor_reduce(early[:, :, 3 - i, :], m.ev[:].rearrange("p t (h d) -> p t h d", h=H), AX.X, ALU.add)\
                    .then_inc(s.summed, 1)
                nc.vector.tensor_reduce(early[:, :, 1 - i, :], path.rearrange("p t (h d) -> p t h d", h=H), AX.X, ALU.add)
            dve.wait_ge(s.summed, 2)
            dve.wait_ge(s.rnorm, 1)
            settle(nc.vector.tensor_tensor(m.e[:], m.rn[:, 0, :], m.beta[:], ALU.mult))
            nc.vector.tensor_tensor(m.ev[:].rearrange("p t (h d) -> p (t h) d", h=H),
                                    m.v_tm[:].rearrange("p t (h d) -> p (t h) d", h=H), bc(m.e[:], DH), ALU.mult)
    clear(nc, s)


LAGS = (0, 1, 1, 1, 1, 2)


def delta_rule(nc, k, m, A, TT, ps, s):
    Xd = m.delta_tm[:].rearrange("p t (h n) -> p (t h) n", n=2 * CHUNK)
    C, HALF = CHUNK, 2 * CHUNK
    B0, B1, B2, B3 = (slice(C * b, C * (b + 1)) for b in range(BLOCKS))
    TOP, LOW = slice(0, HALF), slice(HALF, P)
    KSU, O, ST, KQ, AT_T, L5, L6 = 0, 1, 2, (3, 4), 5, 6, 7
    with ExitStack() as tmp:
        def sb(name, shape):
            return tmp.enter_context(nc.sbuf_tensor(name, shape, F32))

        AT5 = sb("dr_at5", [P, 2, H, P])
        W = sb("dr_w", [P, 4, H, HALF])
        AT6, Y6 = W[TOP], W
        Z = sb("dr_z", [P, 2, H, P])
        S = sb("dr_s", [P, HALVES, P])
        r = sb("dr_r", [P, 2, D])
        u = sb("dr_u", [P, 2, D])
        attnT = sb("dr_attn", [P, 2, H * P])

        def tile(ap, t):
            return ap[:, t, :].rearrange("p (h n) -> p h n", h=H)

        def bank(b, n, first=0):
            return ps[:, b, first:first + H * n].rearrange("p (h n) -> p h n", h=H)

        y5, x10, t01 = bank(L5, C), bank(L5, C, H * C), bank(L5, HALF, 2 * H * C)
        squares = sb("dr_squares", [P, 2, 4, D])
        with_delta = A[:, 0:4, :].rearrange("p (b t) (n d) -> p b (t n) d", b=2, d=D)
        paths = [m.local_tm, m.mid_tm, m.v_tm]

        def feature_sums(first, src, t, n):
            return nc.vector.tensor_reduce(m.feats[:, t, first * H:(first + n) * H].rearrange("p (n h) -> p n h", h=H),
                                           src.rearrange("p n (h d) -> p n h d", h=H), AX.X, ALU.add)

        at, y6, t6 = bank(AT_T, P), bank(L6, HALF), bank(AT_T, HALF)
        steps = [[step - lag for lag in LAGS] for step in range(T + LAGS[-1])]
        with nc.Block() as block:
            @block.gpsimd
            def _(pool):
                nc.gpsimd.memset(AT5[:], 0.0).then_inc(s.zeroed, 1)
                nc.gpsimd.memset(Z[:], 0.0).then_inc(s.zeroed, 1)
                nc.gpsimd.memset(S[:], 0.0).then_inc(s.zeroed, 1)
                for t0, _, _, _, _, t in steps:
                    if t0 < T:
                        if t0 >= 2:
                            pool.wait_ge(s.summed, t0 - 1)
                        for n, (i, j) in enumerate(((0, 1), (0, 2), (1, 2))):
                            nc.gpsimd.tensor_tensor(squares[:, t0 % 2, 1 + n, :], paths[i][:, t0, :], paths[j][:, t0, :],
                                                    ALU.mult).then_inc(s.products, 1)
                    if t >= 0:
                        pool.wait_ge(s.o_out, t + 1)
                        if t >= 2:
                            pool.wait_ge(s.d_summed, t - 1)
                        for n in range(3):
                            nc.gpsimd.tensor_tensor(with_delta[:, t % 2, 1 + n, :], m.delta_tm[:, t, :], paths[n][:, t, :],
                                                    ALU.mult).then_inc(s.d_products, 1)

            @block.tensor
            def _(pe):
                for t0, t1, t2, t3, t4, t in steps:
                    if t >= 0:
                        b = t % 2
                        if t:
                            pe.wait_ge(s.attn, 2 * t)
                        for h in range(H):
                            rows = slice(DH * (h % 2), DH * (h % 2) + DH)
                            last = nc.tensor.matmul(ps[:, KQ[h % 2], h * P:(h + 1) * P], m.kT[rows, h // 2, t * P:(t + 1) * P],
                                                    m.qT[rows, h // 2, t * P:(t + 1) * P],
                                                    start=(h < 2), stop=True, skip_group_check=True)
                        last.then_inc(s.kq, 1)
                        if t:
                            pe.wait_ge(s.state, 2 * t)
                        for a in range(HALVES):
                            last = nc.tensor.matmul(ps[:, KSU, a * P:(a + 1) * P], m.kT[:, a, t * P:(t + 1) * P], S[:, a, :],
                                                    start=(a == 0), stop=True, skip_group_check=True)
                        last.then_inc(s.ks, 1)
                    if t0 < T:
                        if t4 > 0:
                            pe.wait_ge(s.t6, t4)
                        elif t0 > 0:
                            pe.wait_ge(s.at6, t0)
                        for h in range(H):
                            last = nc.tensor.transpose(at[:, h], tile(A, t0)[:, h], k.ident[:])
                        last.then_inc(s.at_ps, 1)
                    if t >= 0:
                        if t:
                            pe.wait_ge(s.o_out, t)
                        for a in range(HALVES):
                            nc.tensor.matmul(ps[:, O, a * P:(a + 1) * P], m.qT[:, a, t * P:(t + 1) * P], S[:, a, :],
                                             start=(a == 0), stop=False, skip_group_check=True)
                    if 0 <= t1 < T:
                        pe.wait_ge(s.at5, 2 * (t1 + 1))
                        if t1:
                            pe.wait_ge(s.z, 2 * t1)
                        if t2 > 0:
                            pe.wait_ge(s.x10, t2)
                            pe.wait_ge(s.t01, t2)
                            pe.wait_ge(s.t23, t2)
                        for h in range(H):
                            last = nc.tensor.matmul(y5[:, h], AT5[:, t1 % 2, h, :], Xd[:, t1 * H + h, 0:C],
                                                    start=(h == 0), stop=True, skip_group_check=True)
                        last.then_inc(s.y5_ps, 1)
                    if t >= 0:
                        pe.wait_ge(s.r, t + 1)
                        pe.wait_ge(s.t6, t + 1)
                        for h in range(H):
                            last = nc.tensor.matmul(ps[:, KSU, D + h * DH:D + (h + 1) * DH], TT[:, t, h * P:(h + 1) * P],
                                                    r[:, b, h * DH:(h + 1) * DH], start=False, stop=True,
                                                    skip_group_check=True)
                        last.then_inc(s.u_ps, 1)
                    if 0 <= t2 < T:
                        pe.wait_ge(s.z, 2 * min(t1 + 1, T))
                        for h in range(H):
                            nc.tensor.matmul(x10[:, h], tile(TT, t2)[:, h], Z[:, t2 % 2, h, 0:C],
                                             start=(h == 0), stop=True, skip_group_check=True)
                        for h in range(H):
                            last = nc.tensor.matmul(t01[:, h], Z[:, t2 % 2, h, :],
                                                    tile(TT, t2)[:, h].rearrange("p (b n) -> p b n", n=C)[:, 1::2],
                                                    start=False, stop=True, skip_group_check=True)
                        last.then_inc(s.x_ps, 1)
                    if t >= 0:
                        pe.wait_ge(s.u, t + 1)
                        if t < T - 1:
                            for a in range(HALVES):
                                last = nc.tensor.matmul(ps[:, ST, a * P:(a + 1) * P], m.k_tm[:, t, a * P:(a + 1) * P],
                                                        u[:, b, a * P:(a + 1) * P], start=(t == 0 and a == 0), stop=False,
                                                        skip_group_check=True)
                            last.then_inc(s.s_ps, 1)
                        pe.wait_ge(s.attn, 2 * (t + 1))
                        for h in range(H):
                            last = nc.tensor.matmul(ps[:, O, h * DH:(h + 1) * DH], attnT[:, b, h * P:(h + 1) * P],
                                                    u[:, b, h * DH:(h + 1) * DH], start=False, stop=True,
                                                    skip_group_check=True)
                        last.then_inc(s.o, 1)
                    if 0 <= t3 < T:
                        pe.wait_ge(s.x10, t3 + 1)
                        pe.wait_ge(s.at6, t3 + 1)
                        if t3:
                            pe.wait_ge(s.y6, t3)
                        for h in range(H):
                            last = nc.tensor.matmul(y6[LOW, h], AT6[:, t3 % 4, h, :], Xd[TOP, t3 * H + h, :],
                                                    start=(h == 0), stop=True, skip_group_check=True)
                        last.then_inc(s.y6_ps, 1)
                    if 0 <= t4 < T:
                        pe.wait_ge(s.y6, t4 + 1)
                        pe.wait_ge(s.t23, t4 + 1)
                        pe.wait_ge(s.at6, min(t0 + 1, T))
                        if t4:
                            pe.wait_ge(s.t6, t4)
                        for h in range(H):
                            last = nc.tensor.matmul(t6[TOP, h], Y6[LOW, t4 % 2, h, :], tile(TT, t4)[LOW, h, HALF:P],
                                                    start=(h == 0), stop=True, skip_group_check=True)
                        last.then_inc(s.t_ps, 1)

            @block.vector
            def _(dve):
                settle = chain_of(dve, s.dve)
                dve.wait_ge(s.zeroed, 3)
                def sum_with_delta(t):
                    dve.wait_ge(s.d_products, 3 * (t + 1))
                    dve.wait_ge(s.d_square, t + 1)
                    feature_sums(9, m.delta_tm[:, t:t + 1, :], t, 1)
                    feature_sums(10, with_delta[:, t % 2], t, 4).then_inc(s.d_summed, 1)

                for t0, t1, t2, t3, t4, t in steps:
                    b = t % 2
                    if t >= 0:
                        dve.wait_ge(s.ks, t + 1)
                        settle(nc.vector.tensor_tensor(r[:, b, :].rearrange("p (h d) -> p h d", h=H),
                                                       ps[:, KSU, 0:D].rearrange("p (h d) -> p h d", h=H),
                                                       bc(m.negd[:, t * H:(t + 1) * H], DH), ALU.mult))
                        nc.vector.tensor_tensor(r[:, b, :], r[:, b, :], m.ev[:, t, :], ALU.add).then_inc(s.r, 1)
                        for odd in range(2):
                            nc.vector.tensor_tensor(attnT[:, b, :].rearrange("p (h n) -> p h n", h=H)[:, odd::2],
                                                    ps[:, KQ[odd], :].rearrange("p (h n) -> p h n", h=H)[:, odd::2],
                                                    k.incl[:].unsqueeze(1).to_broadcast([P, H // 2, P]), ALU.mult)\
                                .then_inc(s.attn, 1)
                    if t0 < T:
                        dve.wait_ge(s.at_ps, t0 + 1)
                        if t0 >= 2:
                            dve.wait_ge(s.y5_ps, t0 - 1)
                        nc.vector.tensor_copy(AT5[B0, t0 % 2, :, B1], at[B0, :, B1]).then_inc(s.at5, 1)
                        nc.vector.tensor_copy(AT5[B2, t0 % 2, :, B3], at[B2, :, B3]).then_inc(s.at5, 1)
                        if t0 >= 4:
                            dve.wait_ge(s.y6_ps, t0 - 3)
                        nc.vector.tensor_copy(AT6[:, t0 % 4], at[TOP, :, HALF:P]).then_inc(s.at6, 1)
                        feature_sums(2, m.local_tm[:, t0:t0 + 1, :], t0, 1)
                    if t >= 2:
                        sum_with_delta(t - 2)
                    if 0 <= t2 < T:
                        dve.wait_ge(s.x_ps, t2 + 1)
                        nc.vector.tensor_copy(Xd[B1, t2 * H:(t2 + 1) * H, 0:C], x10[B1]).then_inc(s.x10, 1)
                        nc.vector.tensor_copy(tile(TT, t2)[B0, :, B1], t01[B0, :, 0:C]).then_inc(s.t01, 1)
                    if t >= 0:
                        if t < T - 1:
                            dve.wait_ge(s.s_ps, t + 1)
                            for part in (TOP, LOW):
                                nc.vector.tensor_copy(S[part, :, part],
                                                      ps[part, ST, 0:D].rearrange("p (a n) -> p a n", a=2)[:, :, part])\
                                    .then_inc(s.state, 1)
                        dve.wait_ge(s.o, t + 1)
                        nc.vector.tensor_tensor(m.delta_tm[:, t, :].rearrange("p (h d) -> p h d", h=H),
                                                ps[:, O, 0:D].rearrange("p (h d) -> p h d", h=H),
                                                bc(m.rn[:, 1, t * H:(t + 1) * H], DH), ALU.mult).then_inc(s.o_out, 1)
                    if t0 < T:
                        dve.wait_ge(s.products, 3 * (t0 + 1))
                        dve.wait_ge(s.square, t0 + 1)
                        feature_sums(5, squares[:, t0 % 2], t0, 4).then_inc(s.summed, 1)
                sum_with_delta(T - 2)
                sum_with_delta(T - 1)

            @block.scalar
            def _(act):
                act.wait_ge(s.zeroed, 2)
                def square_others(t):
                    if t >= 2:
                        act.wait_ge(s.summed, t - 1)
                    nc.scalar.activation(squares[:, t % 2, 0, :], m.local_tm[:, t, :], ACT.Square).then_inc(s.square, 1)

                def square_delta(t):
                    act.wait_ge(s.o_out, t + 1)
                    if t >= 2:
                        act.wait_ge(s.d_summed, t - 1)
                    nc.scalar.activation(with_delta[:, t % 2, 0, :], m.delta_tm[:, t, :], ACT.Square).then_inc(s.d_square, 1)

                square_others(0)
                for i in range(2):
                    nc.scalar.activation(m.feats[:, :, 3 * i * H:(3 * i + 2) * H].rearrange("p t (f h) -> p t f h", h=H),
                                         early_features(m)[:, :, 2 * i:2 * i + 2, :], ACT.Copy)
                for t0, t1, t2, t3, t4, t in steps:
                    if 0 <= t1 < T:
                        act.wait_ge(s.y5_ps, t1 + 1)
                        if t1 >= 2:
                            act.wait_ge(s.x_ps, t1 - 1)
                        nc.scalar.activation(Z[B1, t1 % 2, :, B0], y5[B1], ACT.Copy).then_inc(s.z, 1)
                        nc.scalar.activation(Z[B3, t1 % 2, :, B2], y5[B3], ACT.Copy).then_inc(s.z, 1)
                    if t >= 0:
                        act.wait_ge(s.u_ps, t + 1)
                        nc.scalar.activation(u[:, t % 2, :], ps[:, KSU, D:2 * D], ACT.Copy).then_inc(s.u, 1)
                    if 0 <= t2 < T:
                        act.wait_ge(s.x_ps, t2 + 1)
                        nc.scalar.activation(tile(TT, t2)[B2, :, B3], t01[B2, :, C:HALF], ACT.Copy).then_inc(s.t23, 1)
                    if 0 <= t3 < T:
                        act.wait_ge(s.y6_ps, t3 + 1)
                        if t3 >= 2:
                            act.wait_ge(s.t_ps, t3 - 1)
                        nc.scalar.activation(Y6[LOW, t3 % 2], y6[LOW], ACT.Copy).then_inc(s.y6, 1)
                    if 0 <= t4 < T:
                        act.wait_ge(s.t_ps, t4 + 1)
                        nc.scalar.activation(tile(TT, t4)[TOP, :, HALF:P], t6[TOP], ACT.Copy).then_inc(s.t6, 1)
                    if t0 + 1 < T:
                        square_others(t0 + 1)
                    if t > 0:
                        square_delta(t - 1)
                square_delta(T - 1)
    clear(nc, s)


def route(nc, k, m, ps, s):
    with ExitStack() as tmp:
        def sb(name, shape):
            return tmp.enter_context(nc.sbuf_tensor(name, shape, F32))

        F = m.feats
        var = sb("ro_var", [P, T, 4 * H])
        FT = sb("ro_ft", [FEATS, L])
        h1T = sb("ro_h1", [P, HC, L])
        lg = sb("ro_lg", [P, T * H, PATHS])
        red = sb("ro_red", [P, T * H])

        def feature(first, n):
            return F[:, :, first * H:(first + n) * H]

        with nc.Block() as block:
            @block.scalar
            def _(act):
                for n in range(NB):
                    act.wait_ge(s.ft_ps, n + 1)
                    nc.scalar.activation(FT[:, n * BANK:(n + 1) * BANK], ps[0:FEATS, n, :], ACT.Copy).then_inc(s.ft, 1)
                for n in range(NB):
                    for c in range(HC):
                        u = n * HC + c
                        rows = P if c < HC - 1 else HLAST
                        act.wait_ge(s.h1_ps, u + 1)
                        nc.scalar.activation(h1T[0:rows, c, n * BANK:(n + 1) * BANK], ps[0:rows, 2 + u % 4, :], ACT.Silu,
                                             bias=k.rb1[0:rows, c:c + 1]).then_inc(s.h1, 1)
                act.wait_ge(s.shifted, 1)
                nc.scalar.activation(lg[:].rearrange("p n c -> p (n c)"), lg[:].rearrange("p n c -> p (n c)"),
                                     ACT.Exp).then_inc(s.exp, 1)

            @block.vector
            def _(dve):
                settle = chain_of(dve, s.dve)
                for first, sums, squares, n in ((0, 0, 3, 3), (3, 9, 10, 1)):
                    last = nc.vector.tensor_tensor(var[:, :, first * H:(first + n) * H], feature(sums, n), feature(sums, n),
                                                   ALU.mult)
                settle(last)
                for first, sums, squares, n in ((0, 0, 3, 3), (3, 9, 10, 1)):
                    last = nc.vector.scalar_tensor_tensor(feature(squares, n), var[:, :, first * H:(first + n) * H], -1.0 / DH,
                                                          feature(squares, n), ALU.mult, ALU.add)
                settle(last)
                for squares, n in ((3, 3), (10, 1)):
                    nc.vector.tensor_scalar(feature(squares, n), feature(squares, n), 1.0 / (DH - 1), None, ALU.mult)
                for first, n in ((0, 3), (6, 4), (11, 3)):
                    last = nc.vector.tensor_scalar(feature(first, n), feature(first, n), 1.0 / DH, None, ALU.mult)
                last.then_inc(s.feats, 1)
                dve.wait_ge(s.logits, 1)
                settle(nc.vector.tensor_tensor(lg[:].rearrange("p (t h) c -> p t (h c)", h=H),
                                               ps[:, 6, 0:T * H * PATHS].rearrange("p (t n) -> p t n", t=T),
                                               k.rb2[:].unsqueeze(1).to_broadcast([P, T, H * PATHS]), ALU.add))
                settle(nc.vector.tensor_reduce(red[:], lg[:], AX.X, ALU.max))
                nc.vector.tensor_tensor(lg[:], lg[:], bc(red[:], PATHS), ALU.subtract).then_inc(s.shifted, 1)
                dve.wait_ge(s.exp, 1)
                settle(nc.vector.tensor_reduce(red[:], lg[:], AX.X, ALU.add))
                settle(nc.vector.reciprocal(red[:], red[:]))
                settle(nc.vector.tensor_tensor(lg[:], lg[:], bc(red[:], PATHS), ALU.mult))
                nc.vector.tensor_scalar(m.prob[:], lg[:], 1.0 - PATHS * FLOOR, FLOOR, ALU.mult, ALU.add)

            @block.tensor
            def _(pe):
                def unit(u):
                    n, c = u // HC, u % HC
                    rows = P if c < HC - 1 else HLAST
                    return n, slice(n * BANK, (n + 1) * BANK), ps[0:rows, 2 + u % 4, :], slice(c * P, c * P + rows)

                def from_hidden(u):
                    n, cols, out, hid = unit(u)
                    if u >= 4:
                        pe.wait_ge(s.h1, u - 3)
                    nc.tensor.matmul(out, k.rw1[:, 0, hid], k.xnT[:, 0, cols], start=True, stop=False)
                    nc.tensor.matmul(out, k.rw1[:, 1, hid], k.xnT[:, 1, cols], start=False, stop=False)

                def logits_of(n):
                    pe.wait_ge(s.h1, (n + 1) * HC)
                    for t in range(n * (BANK // P), (n + 1) * (BANK // P)):
                        for c in range(HC):
                            rows = P if c < HC - 1 else HLAST
                            last = nc.tensor.matmul(ps[:, 6, t * H * PATHS:(t + 1) * H * PATHS],
                                                    h1T[0:rows, c, t * P:(t + 1) * P], k.rw2[0:rows, c, :],
                                                    start=(t == 0 and c == 0), stop=(c == HC - 1), skip_group_check=True)
                    return last

                for u in range(3):
                    from_hidden(u)
                pe.wait_ge(s.feats, 1)
                for n in range(NB):
                    for i in range(BANK // P):
                        last = nc.tensor.transpose(ps[0:FEATS, n, i * P:(i + 1) * P], F[:, n * (BANK // P) + i, :], k.ident[:])
                    last.then_inc(s.ft_ps, 1)
                for u in range(NB * HC):
                    n, cols, out, hid = unit(u)
                    pe.wait_ge(s.ft, n + 1)
                    nc.tensor.matmul(out, k.rw1[0:FEATS, 2, hid], FT[:, cols], start=False, stop=True).then_inc(s.h1_ps, 1)
                    if u + 3 < NB * HC:
                        from_hidden(u + 3)
                    if u == HC + 1:
                        logits_of(0)
                logits_of(NB - 1).then_inc(s.logits, 1)
    clear(nc, s)


def mix_and_project(nc, k, m, ps, s):
    with ExitStack() as tmp:
        def sb(name, shape):
            return tmp.enter_context(nc.sbuf_tensor(name, shape, F32))

        part = [sb(f"mi_part{i}", [P, T, D]) for i in range(PATHS)]
        sq = sb("mi_sq", [P, T, D])
        oT = sb("mi_ot", [P, HALVES, L])
        ms = sb("mi_ms", [P, 4, T * H])
        paths = [m.local_tm, m.mid_tm, m.delta_tm, m.v_tm]
        TN, GN = T // NB, T * H // NB

        def of(ap, n):
            return ap[:, n * TN:(n + 1) * TN, :].rearrange("p t (h d) -> p (t h) d", h=H)

        def flat(ap, n):
            return ap[:, n * TN:(n + 1) * TN, :].rearrange("p t d -> p (t d)")

        def weight(i, n):
            return m.prob[:, n * GN:(n + 1) * GN, i:i + 1].to_broadcast([P, GN, DH])

        mixed, weighted = part[0], part[1]
        with nc.Block() as block:
            @block.gpsimd
            def _(pool):
                for n in range(NB):
                    for i in (2, 3):
                        nc.gpsimd.tensor_tensor(of(part[i], n), of(paths[i], n), weight(i, n), ALU.mult).then_inc(s.part, 1)
                for n in range(NB):
                    pool.wait_ge(s.mixed, n + 1)
                    nc.gpsimd.tensor_tensor(weighted[:, n * TN:(n + 1) * TN, :], mixed[:, n * TN:(n + 1) * TN, :],
                                            k.mixw[:].unsqueeze(1).to_broadcast([P, TN, D]), ALU.mult).then_inc(s.weighted, 1)
                for n in range(NB):
                    pool.wait_ge(s.scale_in, n + 1)
                    cols = slice(n * GN, (n + 1) * GN)
                    nc.gpsimd.tensor_tensor(ms[:, 3, cols], ms[:, 2, cols], k.mhalf[:, 0:GN], ALU.pow).then_inc(s.scale, 1)
                inverse_deviations(nc, k, s, pool)

            @block.vector
            def _(dve):
                settle = chain_of(dve, s.dve)

                def mix(n):
                    nc.vector.tensor_tensor(of(part[0], n), of(paths[0], n), weight(0, n), ALU.mult)
                    settle(nc.vector.tensor_tensor(of(part[1], n), of(paths[1], n), weight(1, n), ALU.mult))
                    settle(nc.vector.tensor_tensor(flat(part[0], n), flat(part[0], n), flat(part[1], n), ALU.add))
                    dve.wait_ge(s.part, 2 * n + 1)
                    settle(nc.vector.tensor_tensor(flat(part[0], n), flat(part[0], n), flat(part[2], n), ALU.add))
                    dve.wait_ge(s.part, 2 * n + 2)
                    nc.vector.tensor_tensor(flat(mixed, n), flat(part[0], n), flat(part[3], n), ALU.add).then_inc(s.mixed, 1)

                def first_mean(n):
                    cols = slice(n * GN, (n + 1) * GN)
                    dve.wait_ge(s.square, n + 1)
                    settle(nc.vector.tensor_reduce(ms[:, 0, cols], of(sq, n), AX.X, ALU.add))
                    settle(nc.vector.tensor_scalar(ms[:, 0, cols], ms[:, 0, cols], 1.0 / DH, EPS, ALU.mult, ALU.add))
                    nc.vector.reciprocal(ms[:, 2, cols], ms[:, 0, cols]).then_inc(s.sq_free, 1)

                def second_mean(n):
                    cols = slice(n * GN, (n + 1) * GN)
                    dve.wait_ge(s.square, NB + n + 1)
                    settle(nc.vector.tensor_reduce(ms[:, 1, cols], of(sq, n), AX.X, ALU.add))
                    dve.wait_ge(s.sq_free, n + 1)
                    settle(nc.vector.tensor_tensor(ms[:, 1, cols], ms[:, 1, cols], ms[:, 2, cols], ALU.mult))
                    settle(nc.vector.tensor_scalar(ms[:, 1, cols], ms[:, 1, cols], 1.0 / DH, EPS, ALU.mult, ALU.add))
                    nc.vector.tensor_tensor(ms[:, 2, cols], ms[:, 1, cols], ms[:, 0, cols], ALU.mult).then_inc(s.scale_in, 1)

                mix(0)
                mix(1)
                first_mean(0)
                first_mean(1)
                second_mean(0)
                second_mean(1)
                for u in range(T // 2):
                    rows = slice(2 * u * H, (2 * u + 2) * H)
                    dve.wait_ge(s.scale, 2 * u // TN + 1)
                    nc.vector.tensor_tensor(part[2][:].rearrange("p t (h d) -> p (t h) d", h=H)[:, rows],
                                            weighted[:].rearrange("p t (h d) -> p (t h) d", h=H)[:, rows],
                                            bc(ms[:, 3, rows], DH), ALU.mult).then_inc(s.normed, 1)
                for n in range(NB):
                    dve.wait_ge(s.turned, HALVES * n + 2)
                    nc.vector.tensor_copy(oT[:, 1, n * BANK:(n + 1) * BANK], ps[:, HALVES * n + 1, :]).then_inc(s.ot1, 1)
                add_with_statistics(nc, k, s, dve, settle, lambda u: ps[:, 4 + u, :])

            @block.scalar
            def _(act):
                for n in range(NB):
                    act.wait_ge(s.mixed, n + 1)
                    nc.scalar.activation(flat(sq, n), flat(mixed, n), ACT.Square).then_inc(s.square, 1)
                for n in range(NB):
                    act.wait_ge(s.weighted, n + 1)
                    act.wait_ge(s.sq_free, n + 1)
                    nc.scalar.activation(flat(sq, n), flat(weighted, n), ACT.Square).then_inc(s.square, 1)
                for n in range(NB):
                    act.wait_ge(s.turned, HALVES * n + 1)
                    nc.scalar.activation(oT[:, 0, n * BANK:(n + 1) * BANK], ps[:, HALVES * n, :], ACT.Copy).then_inc(s.ot0, 1)
                normalise(nc, k, s, act, k.x1)

            @block.tensor
            def _(pe):
                for n in range(NB):
                    for a in range(HALVES):
                        for i in range(BANK // P):
                            t = n * (BANK // P) + i
                            pe.wait_ge(s.normed, t // 2 + 1)
                            last = nc.tensor.transpose(ps[:, HALVES * n + a, i * P:(i + 1) * P],
                                                       part[2][:, t, a * P:(a + 1) * P], k.ident[:])
                        last.then_inc(s.turned, 1)
                for t in range(T):
                    n = t // (BANK // P)
                    pe.wait_ge(s.ot0, n + 1)
                    pe.wait_ge(s.ot1, n + 1)
                    for a in range(HALVES):
                        last = nc.tensor.matmul(ps[:, 4 + t // 2, (t % 2) * D:(t % 2 + 1) * D], oT[:, a, t * P:(t + 1) * P],
                                                k.wo[:, a, :], start=(t % 2 == 0 and a == 0), stop=(a == HALVES - 1),
                                                skip_group_check=True)
                    if t % 2:
                        last.then_inc(s.out, 1)
    clear(nc, s)



def slot_ffn(nc, k, ps, s, tag, io=None, store=None, load=None):
    with ExitStack() as tmp:
        def sb(name, shape):
            return tmp.enter_context(nc.sbuf_tensor(name, shape, F32))

        hT = sb(f"{tag}_ht", [FH, L])
        lg = sb(f"{tag}_lg", [P, T, SLOTS])
        left = sb(f"{tag}_left", [P, T, SLOTS])
        alpha = sb(f"{tag}_alpha", [P, T, SLOTS])
        top = sb(f"{tag}_top", [P, T, TOPK])
        total = sb(f"{tag}_total", [P, T])
        alphaT = sb(f"{tag}_alphat", [SLOTS, L])
        gi = sb(f"{tag}_gi", [SLOTS, D])
        wsum = sb(f"{tag}_wsum", [SLOTS, 1])
        giT = sb(f"{tag}_git", [P, HALVES, SLOTS])
        rz = sb(f"{tag}_rz", [SLOTS, 2 * D])
        new = sb(f"{tag}_new", [SLOTS, D])
        mem = sb(f"{tag}_mem", [SLOTS, D])
        memT = sb(f"{tag}_memt", [P, HALVES, SLOTS])
        values = sb(f"{tag}_values", [SLOTS, D])

        with nc.Block() as block:
            @block.tensor
            def _(pe):
                turn_normed_pe(nc, k, ps, s)
                for n in range(NB):
                    pe.wait_ge(s.xn0, n + 1)
                    pe.wait_ge(s.xn1, n + 1)
                    for c in range(HALVES):
                        last = nc.tensor.matmul(ps[:, n, :], k.w1x[:, c, :], k.xnT[:, c, n * BANK:(n + 1) * BANK],
                                                start=(c == 0), stop=(c == HALVES - 1))
                    last.then_inc(s.h_ps, 1)
                for t in range(T):
                    pe.wait_ge(s.h, t // (BANK // P) + 1)
                    last = nc.tensor.matmul(ps[:, 2, t * SLOTS:(t + 1) * SLOTS], hT[:, t * P:(t + 1) * P], k.w2T[:],
                                            start=(t == 0), stop=True, skip_group_check=True)
                last.then_inc(s.logits, 1)
                pe.wait_ge(s.alpha, 1)
                for t in range(T):
                    last = nc.tensor.matmul(ps[0:SLOTS, 3, 0:D + 1], alpha[:, t, :], k.xn[:, t, :],
                                            start=(t == 0), stop=(t == T - 1))
                last.then_inc(s.gathered, 1)
                for n in range(NB):
                    for i in range(BANK // P):
                        last = nc.tensor.transpose(ps[0:SLOTS, 4 + n, i * P:(i + 1) * P],
                                                   alpha[:, n * (BANK // P) + i, :], k.ident[:])
                    last.then_inc(s.at_ps, 1)
                pe.wait_ge(s.gi, 1)
                for a in range(HALVES):
                    last = nc.tensor.transpose(ps[:, 6, a * SLOTS:(a + 1) * SLOTS], gi[:, a * P:(a + 1) * P],
                                               k.ident[0:SLOTS, 0:SLOTS])
                last.then_inc(s.git_ps, 1)
                pe.wait_ge(s.git, 1)
                for a in range(HALVES):
                    last = nc.tensor.matmul(ps[0:SLOTS, 0, :], giT[:, a, :], k.wihT[:, a, 0:2 * D],
                                            start=(a == 0), stop=(a == HALVES - 1))
                last.then_inc(s.gates, 1)
                for a in range(HALVES):
                    last = nc.tensor.matmul(ps[0:SLOTS, 1, 0:D], giT[:, a, :], k.wihT[:, a, 2 * D:],
                                            start=(a == 0), stop=(a == HALVES - 1))
                last.then_inc(s.gates, 1)
                pe.wait_ge(s.mem, 1)
                for a in range(HALVES):
                    last = nc.tensor.transpose(ps[:, 6, a * SLOTS:(a + 1) * SLOTS], mem[:, a * P:(a + 1) * P],
                                               k.ident[0:SLOTS, 0:SLOTS])
                last.then_inc(s.memt_ps, 1)
                pe.wait_ge(s.memt, 1)
                for a in range(HALVES):
                    last = nc.tensor.matmul(ps[0:SLOTS, 7, 0:D], memT[:, a, :], k.wvo[:, a, :],
                                            start=(a == 0), stop=(a == HALVES - 1))
                last.then_inc(s.values_ps, 1)
                pe.wait_ge(s.values, 1)
                for t in range(T):
                    pe.wait_ge(s.alphat, t // (BANK // P) + 1)
                    last = nc.tensor.matmul(ps[:, t // 2, (t % 2) * D:(t % 2 + 1) * D], alphaT[:, t * P:(t + 1) * P],
                                            values[:], start=(t % 2 == 0), stop=True, skip_group_check=True)
                    if t % 2:
                        last.then_inc(s.out, 1)

            @block.scalar
            def _(act):
                turn_normed_act(nc, k, ps, s, act)
                for n in range(NB):
                    act.wait_ge(s.h_ps, n + 1)
                    nc.scalar.activation(hT[:, n * BANK:(n + 1) * BANK], ps[:, n, :], ACT.Gelu,
                                         bias=k.hbias[:, 0:1]).then_inc(s.h, 1)
                act.wait_ge(s.shifted, 1)
                nc.scalar.activation(alpha[:].rearrange("p t n -> p (t n)"), alpha[:].rearrange("p t n -> p (t n)"),
                                     ACT.Exp).then_inc(s.exp, 1)
                for n in range(NB):
                    act.wait_ge(s.at_ps, n + 1)
                    nc.scalar.activation(alphaT[:, n * BANK:(n + 1) * BANK], ps[0:SLOTS, 4 + n, :],
                                         ACT.Copy).then_inc(s.alphat, 1)
                act.wait_ge(s.rz_in, 1)
                nc.scalar.activation(rz[:], rz[:], ACT.Tanh, scale=0.5).then_inc(s.rz, 1)
                act.wait_ge(s.n_in, 1)
                nc.scalar.activation(new[:], new[:], ACT.Tanh).then_inc(s.n, 1)
                if store is None:
                    normalise(nc, k, s, act, k.x1)

            @block.vector
            def _(dve):
                settle = chain_of(dve, s.dve)
                turn_normed_dve(nc, k, ps, s, dve)
                dve.wait_ge(s.logits, 1)
                settle(nc.vector.tensor_tensor(lg[:], ps[:, 2, :].rearrange("p (t n) -> p t n", t=T),
                                               k.b2[:].unsqueeze(1).to_broadcast([P, T, SLOTS]), ALU.add))
                settle(nc.vector.tensor_scalar(lg[:], lg[:], k.invtau[:, 0:1], None, ALU.mult))
                for t in range(T):
                    last = nc.vector.max(top[:, t, :], lg[:, t, :])
                settle(last)
                nc.vector.tensor_tensor(alpha[:], lg[:], top[:, :, 0:1].to_broadcast([P, T, SLOTS]),
                                        ALU.subtract).then_inc(s.shifted, 1)
                for t in range(T):
                    last = nc.vector.match_replace(left[:, t, :], top[:, t, :], lg[:, t, :], NEG)
                settle(last)
                settle(nc.vector.tensor_tensor(left[:], left[:], lg[:], ALU.not_equal))
                dve.wait_ge(s.exp, 1)
                settle(nc.vector.tensor_tensor(alpha[:], alpha[:], left[:], ALU.mult))
                settle(nc.vector.tensor_reduce(total[:], alpha[:], AX.X, ALU.add))
                settle(nc.vector.reciprocal(total[:], total[:]))
                nc.vector.tensor_tensor(alpha[:], alpha[:], bc(total[:], SLOTS), ALU.mult).then_inc(s.alpha, 1)
                dve.wait_ge(s.gathered, 1)
                settle(nc.vector.tensor_scalar(wsum[:], ps[0:SLOTS, 3, D:D + 1], 1e-8, None, ALU.add))
                settle(nc.vector.reciprocal(wsum[:], wsum[:]))
                nc.vector.tensor_scalar(gi[:], ps[0:SLOTS, 3, 0:D], wsum[:, 0:1], None, ALU.mult).then_inc(s.gi, 1)
                dve.wait_ge(s.git_ps, 1)
                nc.vector.tensor_copy(giT[:].rearrange("p a n -> p (a n)"), ps[:, 6, 0:HALVES * SLOTS]).then_inc(s.git, 1)
                dve.wait_ge(s.gates, 1)
                nc.vector.tensor_tensor(rz[:], ps[0:SLOTS, 0, :], k.grz[:], ALU.add).then_inc(s.rz_in, 1)
                dve.wait_ge(s.rz, 1)
                settle(nc.vector.tensor_scalar(rz[:], rz[:], 0.5, 0.5, ALU.mult, ALU.add))
                settle(nc.vector.tensor_tensor(mem[:], rz[:, 0:D], k.hn[:], ALU.mult))
                settle(nc.vector.tensor_tensor(mem[:], mem[:], k.bihn[:], ALU.add))
                dve.wait_ge(s.gates, 2)
                nc.vector.tensor_tensor(new[:], ps[0:SLOTS, 1, 0:D], mem[:], ALU.add).then_inc(s.n_in, 1)
                dve.wait_ge(s.n, 1)
                settle(nc.vector.tensor_tensor(mem[:], k.hs[:], new[:], ALU.subtract))
                settle(nc.vector.tensor_tensor(mem[:], mem[:], rz[:, D:2 * D], ALU.mult))
                nc.vector.tensor_tensor(mem[:], mem[:], new[:], ALU.add).then_inc(s.mem, 1)
                dve.wait_ge(s.memt_ps, 1)
                nc.vector.tensor_copy(memT[:].rearrange("p a n -> p (a n)"), ps[:, 6, 0:HALVES * SLOTS]).then_inc(s.memt, 1)
                dve.wait_ge(s.values_ps, 1)
                nc.vector.tensor_tensor(values[:], ps[0:SLOTS, 7, 0:D], k.bvo[:], ALU.add).then_inc(s.values, 1)
                if store is None:
                    add_with_statistics(nc, k, s, dve, settle, lambda u: ps[:, u, :])
                else:
                    for u in range(T // 2):
                        dve.wait_ge(s.out, u + 1)
                        xs = k.x1[:, 2 * u:2 * u + 2, :].rearrange("p t d -> p (t d)")
                        nc.vector.tensor_tensor(xs, xs, ps[:, u, :], ALU.add).then_inc(s.x_out, 1)

            if store is None:
                @block.gpsimd
                def _(pool):
                    inverse_deviations(nc, k, s, pool)
            else:
                @block.sync
                def _(sp):
                    sp.dma_start(k.x0[:], load).then_inc(io.loaded, 16)
                    sp.wait_ge(s.x_out, T // 2)
                    sp.dma_start(store, k.x1[:]).then_inc(io.stored, 16)
    clear(nc, s)



GH = 4
AG = AH // GH
NBUF = 3
RING = 3
STEPS = [(n, kt) for n in range(NB) for kt in range((n + 1) * (BANK // P))]
PIECES = [(t, j, c) for t in range(T) for j in range(GH) for c in range(-(-(t + 1) * P // BANK))]
PER_STEP = 8
TURN_STEP = len(PIECES) // PER_STEP
Q_PARTS = (0, 0, 1, 0, 2, 1)
K_PARTS = (0, 1, 0, 2, 0, 1)
RATIO = float(AD) ** -0.5


def softmax_attention(nc, k, ps, s, stacked):
    with ExitStack() as tmp:
        def sb(name, shape, dt=F32):
            return tmp.enter_context(nc.sbuf_tensor(name, shape, dt))

        qs = sb("sa_qs", [P, NBUF, GH, L], BF16)
        ks = sb("sa_ks", [P, NBUF, GH, L], BF16)
        va = sb("sa_va", [P, T, AH, AD + 1])
        nm = sb("sa_nm", [P, 2, T, GH, 2])
        otm = sb("sa_otm", [P, T, D])
        rec = sb("sa_rec", [P, BANK // P, GH])
        osb = sb("sa_o", [P, BANK])
        mr = sb("sa_mr", [GH, BANK])
        mp = sb("sa_mp", [GH, 2, 3, L], BF16)

        with ExitStack() as early:
            parts = [early.enter_context(nc.sbuf_tensor(f"sa_parts{i}", [P, 3, HALVES, L], BF16)) for i in range(2)]
            pt = early.enter_context(nc.sbuf_tensor("sa_pt", [P, 2, GH, BANK], F32))
            rest = pt[:].rearrange("p b j l -> p (b j) l")

            pe_use, dve_use = [0], [0]

            def take(pe):
                if pe_use[0] >= RING:
                    pe.wait_ge(s.ring_free, pe_use[0] - RING + 1)
                pe_use[0] += 1
                return ps[:, (pe_use[0] - 1) % RING, :]

            def give(dve):
                dve_use[0] += 1
                dve.wait_ge(s.ring_ready, dve_use[0])
                return ps[:, (dve_use[0] - 1) % RING, :]

            def max_pe(pe, g, first, n):
                if first == 0:
                    pe.wait_ge(stacked[g], 16 * 2 * NCOMB * 2)
                    if g == 0:
                        pe.wait_ge(s.rest, 2 * HALVES * NB)
                for t, j, c in PIECES[first:first + n]:
                    bank = take(pe)
                    w = min(BANK, (t + 1) * P - c * BANK)
                    diagonal = c == t * P // BANK
                    last = nc.tensor.matmul(bank[:, 0:w], qs[0:NCOMB * AD, g % NBUF, j, t * P:(t + 1) * P],
                                            ks[0:NCOMB * AD, g % NBUF, j, c * BANK:c * BANK + w],
                                            start=True, stop=not diagonal, skip_group_check=True)
                    if diagonal:
                        last = nc.tensor.matmul(bank[:, w - P:w], k.identb[:, 0:P], k.causal[:], start=False,
                                                stop=True, skip_group_check=True)
                    last.then_inc(s.ring_ready, 1)

            def max_dve(dve, g, first, n):
                for t, j, c in PIECES[first:first + n]:
                    bank = give(dve)
                    w = min(BANK, (t + 1) * P - c * BANK)
                    nc.vector.tensor_reduce(nm[:, g % 2, t, j, c:c + 1], bank[:, 0:w], AX.X, ALU.max,
                                            negate=True).then_inc(s.ring_free, 1)

            def turn_max_pe(pe, g):
                pe.wait_ge(s.nm, g + 1)
                for n in range(NB):
                    bank = take(pe)
                    for i in range(BANK // P):
                        last = nc.tensor.transpose(bank[0:GH, i * P:(i + 1) * P],
                                                   nm[:, g % 2, n * (BANK // P) + i, :, 0], k.ident[:])
                    last.then_inc(s.ring_ready, 1)

            def turn_max_dve(dve, settle, g):
                late = nm[:, g % 2, BANK // P:T]
                dve.wait_ge(s.ring_free, dve_use[0])
                nc.vector.tensor_tensor(late[:, :, :, 0], late[:, :, :, 0], late[:, :, :, 1], ALU.min)\
                    .then_inc(s.nm, 1)
                if g >= 2:
                    dve.wait_ge(s.m_rows, 16 * 3 * (g - 1))
                for n in range(NB):
                    bank = give(dve)
                    cols = slice(n * BANK, (n + 1) * BANK)
                    settle(nc.vector.tensor_copy(mp[:, g % 2, 0, cols], bank[0:GH, :]))
                    nc.vector.tensor_tensor(mr[:], bank[0:GH, :], mp[:, g % 2, 0, cols], ALU.subtract)\
                        .then_inc(s.ring_free, 1)
                    dve.wait_ge(s.ring_free, dve_use[0])
                    settle(nc.vector.tensor_copy(mp[:, g % 2, 1, cols], mr[:]))
                    nc.vector.tensor_tensor(mp[:, g % 2, 2, cols], mr[:], mp[:, g % 2, 1, cols], ALU.subtract)\
                        .then_inc(s.m_parts, 1)

            def scores_pe(pe, g, st, heads):
                n, kt = STEPS[st]
                if st == 0 and heads[0] == 0:
                    pe.wait_ge(s.m_rows, 16 * 3 * (g + 1))
                    if g == 0:
                        pe.wait_ge(s.const, 2)
                        pe.wait_ge(s.v_out, T // 2)
                off = max(0, kt * P - n * BANK)
                unit = (g * len(STEPS) + st) * GH
                for j in heads:
                    if unit:
                        pe.wait_ge(s.exp, unit - GH + j + 1)
                    diagonal = kt * P >= n * BANK
                    last = nc.tensor.matmul(ps[:, RING + j, off:BANK], ks[0:QROWS, g % NBUF, j, kt * P:(kt + 1) * P],
                                            qs[0:QROWS, g % NBUF, j, n * BANK + off:(n + 1) * BANK],
                                            start=True, stop=not diagonal, skip_group_check=True)
                    if diagonal:
                        last = nc.tensor.matmul(ps[:, RING + j, off:off + P], k.identb[:, 0:P], k.causalT[:],
                                                start=False, stop=True, skip_group_check=True)
                    last.then_inc(s.scores, 1)

            def sums_pe(pe, g, st):
                n, kt = STEPS[st]
                off = max(0, kt * P - n * BANK)
                if kt == 0 and g * NB + n:
                    pe.wait_ge(s.o_out, g * NB + n)
                pe.wait_ge(s.exp, (g * len(STEPS) + st + 1) * GH)
                for j in range(GH):
                    head = (j % 2) * (AH // 2) + 2 * g + j // 2
                    last = nc.tensor.matmul(ps[2 * AD * j:2 * AD * j + AD + 1, 7, off:BANK], va[:, kt, head, :],
                                            pt[:, st % 2, j, off:BANK], start=(kt == 0),
                                            stop=(kt == (n + 1) * (BANK // P) - 1), skip_group_check=True)
                last.then_inc(s.sums, 1)

            def turn_sums_pe(pe, g, n):
                pe.wait_ge(s.o_out, g * NB + n + 1)
                bank = take(pe)
                for i in range(BANK // P):
                    last = nc.tensor.transpose(bank[:, i * P:(i + 1) * P], osb[:, i * P:(i + 1) * P], k.ident[:])
                last.then_inc(s.ring_ready, 1)

            def sums_dve(dve, g, n):
                dve.wait_ge(s.sums, g * len(STEPS) + (n + 1) * (BANK // P) + n * (BANK // P))
                nc.vector.tensor_copy(osb[:], ps[:, 7, :]).then_inc(s.o_out, 1)

            def turn_sums_dve(dve, settle, g, n):
                bank = give(dve).rearrange("p (i j c) -> p i j c", i=BANK // P, j=GH)
                settle(nc.vector.reciprocal(rec[:], bank[:, :, :, AD]))
                view = otm[:].rearrange("p t (a h d) -> p t a h d", a=HALVES, h=AH // 2)
                for hl in range(2):
                    last = nc.vector.tensor_tensor(view[:, n * (BANK // P):(n + 1) * (BANK // P), :, 2 * g + hl, :],
                                                   bank[:, :, 2 * hl:2 * hl + 2, 0:AD],
                                                   bc(rec[:, :, 2 * hl:2 * hl + 2], AD), ALU.mult)
                last.then_inc(s.ring_free, 1)

            with nc.Block() as block:
                @block.gpsimd
                def _(pool):
                    for u in range(2 * HALVES * NB):
                        i, a, n = u // (HALVES * NB), u // NB % HALVES, u % NB
                        cols = slice(n * BANK, (n + 1) * BANK)
                        pool.wait_ge(s.second, u + 1)
                        nc.gpsimd.tensor_tensor(parts[i][:, 2, a, cols], rest[:, u, :], parts[i][:, 1, a, cols],
                                                ALU.subtract).then_inc(s.third, 1)
                    pool.wait_ge(s.third, 2 * HALVES * NB)
                    nc.gpsimd.memset(va[:, :, :, AD:AD + 1], 1.0).then_inc(s.const, 1)
                    pool.wait_ge(s.const, 1)
                    nc.gpsimd.memset(ks[NCOMB * AD:QROWS], 1.0).then_inc(s.const, 1)

                @block.tensor
                def _(pe):
                    turn_normed_pe(nc, k, ps, s)
                    for u in range(2 * HALVES * NB):
                        i, a, n = u // (HALVES * NB), u // NB % HALVES, u % NB
                        if u < NB:
                            pe.wait_ge(s.xn0, n + 1)
                            pe.wait_ge(s.xn1, n + 1)
                        if u >= 4:
                            pe.wait_ge(s.rest, u - 3)
                        for c in range(HALVES):
                            last = nc.tensor.matmul(ps[:, u % 4, :], k.wqkvT[:, c, i * D + a * P:i * D + (a + 1) * P],
                                                    k.xnT[:, c, n * BANK:(n + 1) * BANK],
                                                    start=(c == 0), stop=(c == HALVES - 1))
                        last.then_inc(s.qk_ps, 1)
                    for t in range(T):
                        for c in range(HALVES):
                            last = nc.tensor.matmul(ps[:, 4 + t // 2, (t % 2) * D:(t % 2 + 1) * D],
                                                    k.xnT[:, c, t * P:(t + 1) * P], k.wqkvT[:, c, 2 * D:3 * D],
                                                    start=(t % 2 == 0 and c == 0), stop=(c == HALVES - 1),
                                                    skip_group_check=True)
                        if t % 2:
                            last.then_inc(s.v_ps, 1)
                    max_pe(pe, 0, 0, len(PIECES))
                    turn_max_pe(pe, 0)
                    for g in range(AG):
                        for st in range(len(STEPS)):
                            ahead = g + 1 < AG and st < TURN_STEP
                            scores_pe(pe, g, st, (0, 1))
                            if ahead:
                                max_pe(pe, g + 1, st * PER_STEP, 2)
                            scores_pe(pe, g, st, (2, 3))
                            if ahead:
                                max_pe(pe, g + 1, st * PER_STEP + 2, 2)
                            if st:
                                sums_pe(pe, g, st - 1)
                            if ahead:
                                max_pe(pe, g + 1, st * PER_STEP + 4, PER_STEP - 4)
                            if g and st == 1:
                                turn_sums_pe(pe, g - 1, 1)
                            if st == BANK // P + 1:
                                turn_sums_pe(pe, g, 0)
                            if g + 1 < AG and st == TURN_STEP:
                                turn_max_pe(pe, g + 1)
                        sums_pe(pe, g, len(STEPS) - 1)
                    turn_sums_pe(pe, AG - 1, 1)

                @block.scalar
                def _(act):
                    def part(u, which):
                        i, a, n = u // (HALVES * NB), u // NB % HALVES, u % NB
                        return parts[i][:, which, a, n * BANK:(n + 1) * BANK]

                    turn_normed_act(nc, k, ps, s, act)
                    for u in range(2 * HALVES * NB + 1):
                        if u < 2 * HALVES * NB:
                            act.wait_ge(s.qk_ps, u + 1)
                            nc.scalar.activation(part(u, 0), ps[:, u % 4, :], ACT.Copy).then_inc(s.first, 1)
                        if u:
                            act.wait_ge(s.rest, u)
                            nc.scalar.activation(part(u - 1, 1), rest[:, u - 1, :], ACT.Copy).then_inc(s.second, 1)
                    for u in range(T // 2):
                        act.wait_ge(s.v_ps, u + 1)
                        nc.scalar.activation(va[:, 2 * u:2 * u + 2, :, 0:AD],
                                             ps[:, 4 + u, :].rearrange("p (t h d) -> p t h d", t=2, h=AH),
                                             ACT.Copy).then_inc(s.v_out, 1)
                    act.wait_ge(s.third, 2 * HALVES * NB)
                    for g in range(AG):
                        for st, (n, kt) in enumerate(STEPS):
                            off = max(0, kt * P - n * BANK)
                            gs = g * len(STEPS) + st
                            if gs >= 2:
                                act.wait_ge(s.sums, gs - 1)
                            for j in range(GH):
                                act.wait_ge(s.scores, gs * GH + j + 1)
                                nc.scalar.activation(pt[:, st % 2, j, off:BANK], ps[:, RING + j, off:BANK], ACT.Exp,
                                                     scale=RATIO).then_inc(s.exp, 1)

                @block.vector
                def _(dve):
                    settle = chain_of(dve, s.dve)
                    turn_normed_dve(nc, k, ps, s, dve)
                    for u in range(2 * HALVES * NB):
                        i, a, n = u // (HALVES * NB), u // NB % HALVES, u % NB
                        dve.wait_ge(s.first, u + 1)
                        nc.vector.tensor_tensor(rest[:, u, :], ps[:, u % 4, :],
                                                parts[i][:, 0, a, n * BANK:(n + 1) * BANK], ALU.subtract).then_inc(s.rest, 1)
                    max_dve(dve, 0, 0, len(PIECES))
                    turn_max_dve(dve, settle, 0)
                    for g in range(AG):
                        for st in range(len(STEPS)):
                            if g and st == 0:
                                sums_dve(dve, g - 1, 1)
                            if g + 1 < AG and st < TURN_STEP:
                                max_dve(dve, g + 1, st * PER_STEP, PER_STEP)
                            if st == BANK // P:
                                sums_dve(dve, g, 0)
                            if g and st == 1:
                                turn_sums_dve(dve, settle, g - 1, 1)
                            if st == BANK // P + 1:
                                turn_sums_dve(dve, settle, g, 0)
                            if g + 1 < AG and st == TURN_STEP:
                                turn_max_dve(dve, settle, g + 1)
                    sums_dve(dve, AG - 1, 1)
                    turn_sums_dve(dve, settle, AG - 1, 1)

                @block.sync
                def _(sp):
                    def stack(g):
                        if g >= NBUF:
                            sp.wait_ge(s.scores, (g - NBUF + 1) * len(STEPS) * GH)
                        for i, (dst, src, order) in enumerate(((qs, parts[0], Q_PARTS), (ks, parts[1], K_PARTS))):
                            for c in sorted(range(NCOMB), key=lambda c: order[c]):
                                if g == 0:
                                    sp.wait_ge((s.first, s.second, s.third)[order[c]], (i + 1) * HALVES * NB)
                                for hl in range(2):
                                    sp.dma_start(dst[AD * c:AD * (c + 1), g % NBUF, 2 * hl:2 * hl + 2, :],
                                                 src[AD * (2 * g + hl):AD * (2 * g + hl + 1), order[c], :, :])\
                                        .then_inc(stacked[g], 16)

                    def rows(g):
                        sp.wait_ge(s.m_parts, NB * (g + 1))
                        for c in range(3):
                            sp.dma_start(qs[NCOMB * AD + c:NCOMB * AD + c + 1, g % NBUF, :, :],
                                         mp[:, g % 2, c, :]).then_inc(s.m_rows, 16)

                    for g in range(NBUF):
                        stack(g)
                    rows(0)
                    rows(1)
                    for g in range(NBUF, AG):
                        stack(g)
                    for g in range(2, AG):
                        rows(g)

        oT = sb("sa_ot", [P, HALVES, L])
        with nc.Block() as block:
            @block.tensor
            def _(pe):
                for n in range(NB):
                    for a in range(HALVES):
                        for i in range(BANK // P):
                            last = nc.tensor.transpose(ps[:, HALVES * n + a, i * P:(i + 1) * P],
                                                       otm[:, n * (BANK // P) + i, a * P:(a + 1) * P], k.ident[:])
                        last.then_inc(s.turned, 1)
                for t in range(T):
                    n = t // (BANK // P)
                    pe.wait_ge(s.ot0, n + 1)
                    pe.wait_ge(s.ot1, n + 1)
                    for a in range(HALVES):
                        last = nc.tensor.matmul(ps[:, 4 + t // 2, (t % 2) * D:(t % 2 + 1) * D], oT[:, a, t * P:(t + 1) * P],
                                                k.woutT[:, a, :], start=(t % 2 == 0 and a == 0), stop=(a == HALVES - 1),
                                                skip_group_check=True)
                    if t % 2:
                        last.then_inc(s.out, 1)

            @block.scalar
            def _(act):
                for n in range(NB):
                    act.wait_ge(s.turned, HALVES * n + 1)
                    nc.scalar.activation(oT[:, 0, n * BANK:(n + 1) * BANK], ps[:, HALVES * n, :], ACT.Copy).then_inc(s.ot0, 1)
                normalise(nc, k, s, act, k.x1)

            @block.vector
            def _(dve):
                settle = chain_of(dve, s.out_dve)
                for n in range(NB):
                    dve.wait_ge(s.turned, HALVES * n + 2)
                    nc.vector.tensor_copy(oT[:, 1, n * BANK:(n + 1) * BANK], ps[:, HALVES * n + 1, :]).then_inc(s.ot1, 1)
                add_with_statistics(nc, k, s, dve, settle, lambda u: ps[:, 4 + u, :])

            @block.gpsimd
            def _(pool):
                inverse_deviations(nc, k, s, pool)
        nc.sync.sem_clear(range(stacked[0].num, stacked[-1].num + 1))
        clear(nc, s)



COMMON = "dve var rstd xn_turned xn0 xn1"
SET_OF = {"su": 0, "ln": 2, "pc": 0, "lc": 1, "dr": 0, "ro": 1, "mi": 0, "ff": 1, "sa": 0}
SEMS = {
    "io": "loaded stored",
    "ln": "",
    "su": "loaded all_in const prepared hs pe back",
    "pc": "padded proj pre tap conv silu beta tanh turned tm squared sums ss gram a blocks_out blocks unit rep",
    "lc": "square summed conv evac turned tm zeroed rnorm inverse inverse_out inverse_in",
    "dr": "zeroed products square summed d_products d_square d_summed at_ps at5 at6 y5_ps z "
          "x_ps x10 t01 t23 y6_ps y6 t_ps t6 kq attn ks r u_ps u s_ps state o o_out",
    "ro": "feats ft_ps ft h1_ps h1 logits shifted exp",
    "mi": "part mixed weighted scale_in scale square sq_free normed turned ot0 ot1 out",
    "ff": "h_ps h logits shifted exp alpha gathered at_ps alphat gi git_ps git gates rz_in rz n_in n mem memt_ps memt "
          "values_ps values out x_out",
    "sa": "const first second third rest qk_ps v_ps v_out ring_ready ring_free nm m_parts m_rows scores exp sums o_out "
          "turned ot0 ot1 out out_dve",
}


def sequence(nc, k, ps, s, stacked, bounce, store, load):
    with ExitStack() as first:
        def sf(name, shape):
            return first.enter_context(nc.sbuf_tensor(name, shape, F32))

        paths = sf("paths", [P, PATHS, T, D])
        m = named(
            "DeltaTensors",
            kT=sf("kT", [P, HALVES, L]), qT=sf("qT", [P, HALVES, L]),
            paths=paths, local_tm=paths[:, 0], mid_tm=paths[:, 1], v_tm=paths[:, 2], delta_tm=paths[:, 3],
            feats=k.xn[:, :, 0:FEATS],
            k_tm=sf("k_tm", [P, T, D]), ev=k.x0,
            beta=sf("beta", [P, T * H]), ss=sf("ss", [P, 2, T * H]),
            rn=sf("rn", [P, 2, T * H]), negd=sf("negd", [P, T * H]), e=sf("e", [P, T * H]),
            prob=sf("prob", [P, T * H, PATHS]))
        first_norm(nc, k, s["ln"], s["io"])
        with ExitStack() as inner:
            pre = inner.enter_context(nc.sbuf_tensor("pre", [P, 2, HALVES, 3 + L], F32))
            TT = pre[:].rearrange("p i a l -> p (i a l)")[:, 0:T * H * P].rearrange("p (t n) -> p t n", t=T)
            A = inner.enter_context(nc.sbuf_tensor("A", [P, T, H * P], F32))
            with nc.sbuf_tensor("rep", [P, GROUPS, PAD + L], F32) as rep:
                project_and_convolve(nc, k, m, rep, pre, A, bounce, ps, s["pc"])
                long_convolutions(nc, k, m, rep, TT, bounce, ps, s["lc"])
            delta_rule(nc, k, m, A, TT, ps, s["dr"])
        route(nc, k, m, ps, s["ro"])
        mix_and_project(nc, k, m, ps, s["mi"])
    slot_ffn(nc, k, ps, s["ff"], "ffa")
    softmax_attention(nc, k, ps, s["sa"], stacked)
    slot_ffn(nc, k, ps, s["ff"], "ffb", s["io"], store=store, load=load)


def build(nc, w, y):
    with ExitStack() as ctx:
        def sb(name, shape, dt=F32):
            return ctx.enter_context(nc.sbuf_tensor(name, shape, dt))

        ps = ctx.enter_context(nc.psum_tensor("ps", [P, 8, BANK], F32))
        k = named(
            "Constants",
            wq=sb("wq", [P, HALVES, D]), wk=sb("wk", [P, HALVES, D]), wv=sb("wv", [P, HALVES, D]),
            wb=sb("wb", [P, HALVES, H]), cw=sb("cw", [P, 3, HALVES, 4]),
            stack=sb("stack", [P, (MID_STEPS + LOCAL_STEPS) * GROUPS, CG]),
            wo=sb("wo", [P, HALVES, D]), mixw=sb("mixw", [P, D]),
            rw1=sb("rw1", [P, 3, HID]), rb1=sb("rb1", [P, HC]), rw2=sb("rw2", [P, HC, H * PATHS]),
            rb2=sb("rb2", [P, H * PATHS]),
            ident=sb("ident", [P, P]), identb=sb("identb", [P, 4 * P], BF16),
            incl=sb("incl", [P, P]),
            causal=sb("causal", [P, P], BF16), causalT=sb("causalT", [P, P], BF16), ones2=sb("ones2", [P, 2]),
            invtau=sb("invtau", [P, 1]), w1x=sb("w1x", [P, HALVES, FH]), w2T=sb("w2T", [FH, SLOTS]),
            b2=sb("b2", [P, SLOTS]), wihT=sb("wihT", [P, HALVES, 3 * D]), hs=sb("hs", [SLOTS, D]),
            hbias=sb("hbias", [FH, 1]), grz=sb("grz", [SLOTS, 2 * D]), hn=sb("hn", [SLOTS, D]),
            bihn=sb("bihn", [SLOTS, D]), wvo=sb("wvo", [P, HALVES, D]), bvo=sb("bvo", [SLOTS, D]),
            wqkvT=sb("wqkvT", [P, HALVES, 3 * D]), woutT=sb("woutT", [P, HALVES, D]),
            mhalf=sb("mhalf", [P, 2 * T * H]),
            x0=sb("x0", [P, T, D]), x1=sb("x1", [P, T, D]), xn=sb("xn", [P, T, D + 1]), xnT=sb("xnT", [P, HALVES, L]),
            stats=sb("stats", [P, T, 6]), mv=sb("mv", [P, T, 2]), vare=sb("vare", [P, T]), negm=sb("negm", [P, T]),
            shift=sb("shift", [P, T]), rstd=sb("rstd", [P, T]),
        )
        common = [sems(nc, ctx, f"common{i}", COMMON) for i in range(3)]
        s = {n: sems(nc, ctx, n, names, () if n == "io" else common[SET_OF[n]]) for n, names in SEMS.items()}
        stacked = [ctx.enter_context(nc.semaphore(f"sa_stacked{g}")) for g in range(AG)]
        next_x_view = w["x"].rearrange("b (t p) d -> b p t d", p=P)
        y_view = y.rearrange("b (t p) d -> b p t d", p=P)
        bounce = nc.dram_tensor("bounce", [3, BLOCKS, T * H, CHUNK, CHUNK], F32, kind="Internal").ap()
        setup(nc, w, k, ps, s["su"])
        with nc.Block() as block:
            @block.sync
            def _(sp):
                sp.dma_start(k.x0[:], next_x_view[SEQS - 1]).then_inc(s["io"].loaded, 16)
                sp.sem_inc(s["io"].stored, 16)
        with nc.Fori(0, SEQS) as b:
            sequence(nc, k, ps, s, stacked, bounce, y_view[b], next_x_view[b])
        with nc.Block() as block:
            @block.sync
            def _(sp):
                sp.wait_ge(s["io"].loaded, 16)
                sp.wait_ge(s["io"].stored, 16)


def laid_out(inputs):
    def a(name):
        return np.asarray(inputs[name])

    def lags(w, taps, steps):
        padded = np.zeros((D, SHIFTS * steps), w.dtype)
        padded[:, :taps] = w[:, ::-1]
        return padded.reshape(GROUPS, CG, steps, SHIFTS).transpose(3, 1, 2, 0).reshape(P, steps * GROUPS)

    def rows(v, n):
        return np.broadcast_to(v.reshape(1, -1), (n, v.size))

    i, j = np.arange(P)[:, None], np.arange(P)[None, :]
    order = (2, 6, 0, 3, 7, 1, 8, 10, 12, 4, 5, 9, 11, 13)
    feature_rows = np.concatenate([np.arange(D)] + [D + n * H + np.arange(H) for n in order])
    own, ffn = "L0_attn_a_", "L0_ffn_"
    out = {
        "x": np.roll(a(own + "hidden_states"), -1, axis=0),
        "Wq": a(own + "Wq"), "Wk": a(own + "Wk"), "Wv": a(own + "Wv"), "Wb": a(own + "Wb"),
        "cw": np.stack([a(own + f"conv_{n}_w") for n in "qkv"]),
        "taps": np.concatenate([lags(a(own + "mid_w"), MID, MID_STEPS), lags(a(own + "local_w"), LOCAL, LOCAL_STEPS)], 1),
        "eye32": np.tile(np.eye(CG, dtype=np.float32), (SHIFTS, 1)),
        "Wo": a(own + "Wo"), "onorm": np.tile(a(own + "onorm_w"), P // DH)[:, None],
        "mixw": rows(a(own + "mix_w"), P),
        "rw1": a(own + "r_w1")[feature_rows], "rb1": a(own + "r_b1"), "rw2": a(own + "r_w2"), "rb2": rows(a(own + "r_b2"), P),
        "ident": np.eye(P, dtype=np.float32),
        "identb": np.tile(np.eye(P, dtype=np.float32), (1, 4)),
        "incl": (j >= i).astype(np.float32),
        "causal": np.where(j > i, NEG, 0.0).astype(np.float32),
        "causalT": np.where(i > j, NEG, 0.0).astype(np.float32),
        "ones2": ((i // DH) == j[:, 0:2]).astype(np.float32),
        "tau": rows(a(ffn + "tau"), P), "slot_init": a(ffn + "slot_init"), "slot_scale": a(ffn + "slot_scale"),
        "w1T": a(ffn + "w1").T, "b1": a(ffn + "b1")[:, None], "w2T": a(ffn + "w2").T, "b2": rows(a(ffn + "b2"), P),
        "wihT": a(ffn + "gru_wih").T, "whhT": a(ffn + "gru_whh").T,
        "bih": rows(a(ffn + "gru_bih"), SLOTS), "bhh": rows(a(ffn + "gru_bhh"), SLOTS),
        "wv": a(ffn + "wv"), "woT": a(ffn + "wo").T,
        "bvb": np.broadcast_to(a(ffn + "bv")[:, None], (D, SLOTS)), "bo": rows(a(ffn + "bo"), SLOTS),
        "wqkvT": a("L0_attn_b_w_qkv").T, "woutT": a("L0_attn_b_w_out").T,
    }
    return {n: np.ascontiguousarray(v) for n, v in out.items()}


def kernel(**inputs):
    import concourse.bacc as bacc
    from concourse.bass_utils import run_bass_kernel_spmd

    nc = bacc.Bacc("TRN2", target_bir_lowering=False, num_devices=1)
    arrays = {f"in_{n}": v for n, v in laid_out(inputs).items()}
    w = {n[3:]: nc.dram_tensor(n, v.shape, mybir.dt.from_np(v.dtype), kind="ExternalInput").ap() for n, v in arrays.items()}
    y = nc.dram_tensor("out_y", (SEQS, L, D), F32, kind="ExternalOutput").ap()
    build(nc, w, y)
    r = run_bass_kernel_spmd(nc, [arrays], core_ids=[0])
    return r.results[0]["out_y"]
```
